# Optimizing a Trainium2 kernel written in Bass

```python
import numpy as np
import jax
import jax.numpy as jnp

def _softmax(x, axis=-1):
    return jax.nn.softmax(x, axis=axis)

def _gelu(x):
    return jax.nn.gelu(x, approximate=True)

def _silu(x):
    return jax.nn.silu(x)

def _sigmoid(x):
    return jax.nn.sigmoid(x)

def _layernorm(x, axis=-1, eps=1e-05):
    m = jnp.mean(x, axis=axis, keepdims=True)
    v = jnp.var(x, axis=axis, keepdims=True)
    return (x - m) / jnp.sqrt(v + eps)

def _scatter_add(tgt, idx, src, axis=0):
    return tgt.at[idx].add(src)

def _segment_sum(src, seg, n):
    return jax.ops.segment_sum(src, seg, n)
kernel_name = 'mk_gnn_preln_d4_gnn_r32_9c6296'

def setup_inputs(seed: int=0):
    np.random.seed(seed)
    _w = jnp.asarray

    def _rec_inputs():
        import jax
        import jax.numpy as jnp
        _gk = jax.random.key(seed)
        x = -0.000202 + 1 * jax.random.normal(jax.random.fold_in(_gk, 1), (3125, 128), jnp.float32)
        src = jax.random.randint(jax.random.fold_in(_gk, 2), (50000,), 0, 3125, jnp.int32)
        dst = jax.random.randint(jax.random.fold_in(_gk, 3), (50000,), 0, 3125, jnp.int32)
        _o = jnp.argsort(dst, stable=True)
        src = src[_o]
        dst = dst[_o]
        edge_attr_16 = 0.000189758 + 1.00013 * jax.random.normal(jax.random.fold_in(_gk, 12), (50000, 16), jnp.float32)
        edge_attr_4 = 0.000227908 + 0.99994 * jax.random.normal(jax.random.fold_in(_gk, 13), (50000, 4), jnp.float32)
        edge_attr_8 = jax.random.uniform(jax.random.fold_in(_gk, 14), (50000, 8), jnp.float32, 0.0, 0.999999)
        node_type_4 = jax.random.randint(jax.random.fold_in(_gk, 16), (3125,), 0, 4, jnp.int32)
        return (x, src, dst, edge_attr_16, edge_attr_4, edge_attr_8, node_type_4)
    x, src, dst, edge_attr_16, edge_attr_4, edge_attr_8, node_type_4 = _rec_inputs()

    def _L0_gnn_setup():
        import jax, jax.numpy as jnp
        import numpy as np
        N_NODES = 50000
        N_EDGES = 25000
        DIM = 128
        N_LAYERS = 3

        def _sage_mean_layer(h, edge_src, edge_dst, deg):
            msg = h[edge_src]
            agg = jax.ops.segment_sum(msg, edge_dst, num_segments=h.shape[0])
            neigh = agg / deg[:, None]
            return h + neigh
        key = jax.random.key(seed)
        k1, k2, k3 = jax.random.split(key, 3)
        h = jax.random.normal(k1, (N_NODES, DIM), dtype=jnp.float32)
        edge_src = jax.random.randint(k2, (N_EDGES,), 0, N_NODES, dtype=jnp.int32)
        edge_dst = jax.random.randint(k3, (N_EDGES,), 0, N_NODES, dtype=jnp.int32)
        return {'h': h, 'edge_src': edge_src, 'edge_dst': edge_dst}
    _L0_gnn_all = _L0_gnn_setup()
    _L0_gnn_in = {k: v for k, v in _L0_gnn_all.items() if k in ()}
    del _L0_gnn_all

    def _L1_gnn_setup():
        import jax, jax.numpy as jnp
        import numpy as np
        NEG_SLOPE = 0.01

        def _scatter_mean(vals, idx, num_segments):
            s = jax.ops.segment_sum(vals, idx, num_segments=num_segments)
            cnt = jax.ops.segment_sum(jnp.ones((vals.shape[0],), vals.dtype), idx, num_segments=num_segments)
            return s / jnp.maximum(cnt, 1.0)[:, None]
        key = jax.random.key(seed)
        ks = jax.random.split(key, 8)
        N, E = (3125, 100000)
        node_emb, edge_emb = (128, 16)
        d_in = node_emb + 2 * edge_emb
        x = jax.random.normal(ks[0], (N, node_emb), dtype=jnp.float32)
        edge_index = jax.random.randint(ks[1], (2, E), 0, N, dtype=jnp.int32)
        edge_attr = jax.random.normal(ks[2], (E, edge_emb), dtype=jnp.float32)
        W1 = jax.random.normal(ks[3], (d_in, node_emb), dtype=jnp.float32) * (1.0 / np.sqrt(d_in))
        b1 = jax.random.normal(ks[4], (node_emb,), dtype=jnp.float32) * 0.01
        W2 = jax.random.normal(ks[5], (node_emb, node_emb), dtype=jnp.float32) * (1.0 / np.sqrt(node_emb))
        b2 = jax.random.normal(ks[6], (node_emb,), dtype=jnp.float32) * 0.01
        return {'x': x, 'edge_index': edge_index, 'edge_attr': edge_attr, 'W1': W1, 'b1': b1, 'W2': W2, 'b2': b2}
    _L1_gnn_all = _L1_gnn_setup()
    _L1_gnn_in = {k: v for k, v in _L1_gnn_all.items() if k in ('W1', 'b1', 'W2', 'b2')}
    del _L1_gnn_all

    def _L2_gnn_setup():
        import jax, jax.numpy as jnp
        import numpy as np
        N = 50000
        E = 18750
        H = 4
        C = 32
        IN = 128
        NEG_SLOPE = 0.2
        key = jax.random.key(seed)
        ks = jax.random.split(key, 6)
        s = 1.0 / np.sqrt(IN)
        return {'x': jax.random.normal(ks[0], (N, IN), dtype=jnp.float32), 'edge_index': jax.random.randint(ks[1], (2, E), 0, N, dtype=jnp.int64), 'W_l': jax.random.normal(ks[2], (H * C, IN), dtype=jnp.float32) * s, 'b_l': jnp.zeros((H * C,), jnp.float32), 'W_r': jax.random.normal(ks[3], (H * C, IN), dtype=jnp.float32) * s, 'b_r': jnp.zeros((H * C,), jnp.float32), 'att': jax.random.normal(ks[4], (H, C), dtype=jnp.float32) * s, 'bias': jnp.zeros((H * C,), jnp.float32)}
    _L2_gnn_all = _L2_gnn_setup()
    _L2_gnn_in = {k: v for k, v in _L2_gnn_all.items() if k in ('W_l', 'b_l', 'W_r', 'b_r', 'att', 'bias')}
    del _L2_gnn_all

    def _L3_gnn_setup():
        import jax, jax.numpy as jnp
        import numpy as np
        MUL = 32
        N_NODES = 512
        N_EDGES = 8192
        AVG_NEIGH = 16.0
        N_SPECIES = 4
        RADIAL_DIM = 8
        INV_SQRT3 = 0.5773502691896258
        key = jax.random.key(seed)
        ks = jax.random.split(key, 14)
        f32 = jnp.float32
        return {'node_features': jax.random.normal(ks[0], (N_NODES, 4 * MUL), dtype=f32), 'edge_sh': jax.random.normal(ks[1], (N_EDGES, 4), dtype=f32), 'radial_embedding': jax.random.uniform(ks[2], (N_EDGES, RADIAL_DIM), dtype=f32), 'W_up_s': jax.random.normal(ks[3], (MUL, MUL), dtype=f32), 'W_up_v': jax.random.normal(ks[4], (MUL, MUL), dtype=f32), 'W_r1': jax.random.normal(ks[5], (RADIAL_DIM, RADIAL_DIM), dtype=f32), 'W_r2': jax.random.normal(ks[6], (RADIAL_DIM, 4 * MUL), dtype=f32), 'W_dn_s': jax.random.normal(ks[7], (2 * MUL, 2 * MUL), dtype=f32), 'W_dn_v': jax.random.normal(ks[8], (2 * MUL, MUL), dtype=f32), 'W_sk_s': jax.random.normal(ks[9], (N_SPECIES, MUL, 2 * MUL), dtype=f32), 'W_sk_v': jax.random.normal(ks[10], (N_SPECIES, MUL, MUL), dtype=f32), 'senders': jax.random.randint(ks[11], (N_EDGES,), 0, N_NODES), 'receivers': jax.random.randint(ks[12], (N_EDGES,), 0, N_NODES), 'node_species': jax.random.randint(ks[13], (N_NODES,), 0, N_SPECIES)}
    _L3_gnn_all = _L3_gnn_setup()
    _L3_gnn_in = {k: v for k, v in _L3_gnn_all.items() if k in ('W_up_s', 'W_up_v', 'W_r1', 'W_r2', 'W_dn_s', 'W_dn_v', 'W_sk_s', 'W_sk_v')}
    del _L3_gnn_all
    return {'x': x, 'src': src, 'dst': dst, 'edge_attr_16': edge_attr_16, 'edge_attr_4': edge_attr_4, 'edge_attr_8': edge_attr_8, 'node_type_4': node_type_4, 'L1_gnn_W1': _L1_gnn_in['W1'], 'L1_gnn_b1': _L1_gnn_in['b1'], 'L1_gnn_W2': _L1_gnn_in['W2'], 'L1_gnn_b2': _L1_gnn_in['b2'], 'L2_gnn_W_l': _L2_gnn_in['W_l'], 'L2_gnn_b_l': _L2_gnn_in['b_l'], 'L2_gnn_W_r': _L2_gnn_in['W_r'], 'L2_gnn_b_r': _L2_gnn_in['b_r'], 'L2_gnn_att': _L2_gnn_in['att'], 'L2_gnn_bias': _L2_gnn_in['bias'], 'L3_gnn_W_up_s': _L3_gnn_in['W_up_s'], 'L3_gnn_W_up_v': _L3_gnn_in['W_up_v'], 'L3_gnn_W_r1': _L3_gnn_in['W_r1'], 'L3_gnn_W_r2': _L3_gnn_in['W_r2'], 'L3_gnn_W_dn_s': _L3_gnn_in['W_dn_s'], 'L3_gnn_W_dn_v': _L3_gnn_in['W_dn_v'], 'L3_gnn_W_sk_s': _L3_gnn_in['W_sk_s'], 'L3_gnn_W_sk_v': _L3_gnn_in['W_sk_v']}

def reference(x, src, dst, edge_attr_16, edge_attr_4, edge_attr_8, node_type_4, L1_gnn_W1, L1_gnn_b1, L1_gnn_W2, L1_gnn_b2, L2_gnn_W_l, L2_gnn_b_l, L2_gnn_W_r, L2_gnn_b_r, L2_gnn_att, L2_gnn_bias, L3_gnn_W_up_s, L3_gnn_W_up_v, L3_gnn_W_r1, L3_gnn_W_r2, L3_gnn_W_dn_s, L3_gnn_W_dn_v, L3_gnn_W_sk_s, L3_gnn_W_sk_v):
    import jax
    import jax.numpy as jnp

    def _L0_gnn_ref(h, edge_src, edge_dst):
        import jax, jax.numpy as jnp
        import numpy as np
        N_NODES = 50000
        N_EDGES = 25000
        DIM = 128
        N_LAYERS = 3

        def _sage_mean_layer(h, edge_src, edge_dst, deg):
            msg = h[edge_src]
            agg = jax.ops.segment_sum(msg, edge_dst, num_segments=h.shape[0])
            neigh = agg / deg[:, None]
            return h + neigh
        n = h.shape[0]
        deg = jax.ops.segment_sum(jnp.ones((edge_dst.shape[0],), dtype=h.dtype), edge_dst, num_segments=n)
        deg = jnp.maximum(deg, 1.0)
        res = h
        tmp = h
        for i in range(N_LAYERS):
            tmp = _sage_mean_layer(tmp, edge_src, edge_dst, deg)
            res = res + tmp / (1.0 + i)
        return res

    def _L1_gnn_ref(x, edge_index, edge_attr, W1, b1, W2, b2):
        import jax, jax.numpy as jnp
        import numpy as np
        NEG_SLOPE = 0.01

        def _scatter_mean(vals, idx, num_segments):
            s = jax.ops.segment_sum(vals, idx, num_segments=num_segments)
            cnt = jax.ops.segment_sum(jnp.ones((vals.shape[0],), vals.dtype), idx, num_segments=num_segments)
            return s / jnp.maximum(cnt, 1.0)[:, None]
        N = x.shape[0]
        row, col = (edge_index[0], edge_index[1])
        rec_attr = _scatter_mean(edge_attr, row, N)
        sent_attr = _scatter_mean(edge_attr, col, N)
        out = jnp.concatenate([x, rec_attr, sent_attr], axis=1)
        h = out @ W1 + b1
        h = jnp.where(h >= 0, h, NEG_SLOPE * h)
        return h @ W2 + b2

    def _L2_gnn_ref(x, edge_index, W_l, b_l, W_r, b_r, att, bias):
        import jax, jax.numpy as jnp
        import numpy as np
        N = 50000
        E = 18750
        H = 4
        C = 32
        IN = 128
        NEG_SLOPE = 0.2
        n = x.shape[0]
        loops = jnp.arange(n, dtype=edge_index.dtype)
        src = jnp.concatenate([edge_index[0], loops])
        dst = jnp.concatenate([edge_index[1], loops])
        x_l = (x @ W_l.T + b_l).reshape(n, H, C)
        x_r = (x @ W_r.T + b_r).reshape(n, H, C)
        z = jax.nn.leaky_relu(x_l[src] + x_r[dst], NEG_SLOPE)
        e = jnp.einsum('ehc,hc->eh', z, att)
        m = jax.ops.segment_max(e, dst, num_segments=n)
        e = jnp.exp(e - m[dst])
        denom = jax.ops.segment_sum(e, dst, num_segments=n)
        alpha = e / (denom[dst] + 1e-16)
        out = jax.ops.segment_sum(alpha[:, :, None] * x_l[src], dst, num_segments=n)
        out = out.reshape(n, H * C) + bias
        return jax.nn.elu(out)

    def _L3_gnn_ref(node_features, edge_sh, radial_embedding, W_up_s, W_up_v, W_r1, W_r2, W_dn_s, W_dn_v, W_sk_s, W_sk_v, senders, receivers, node_species):
        import jax, jax.numpy as jnp
        import numpy as np
        MUL = 32
        N_NODES = 512
        N_EDGES = 8192
        AVG_NEIGH = 16.0
        N_SPECIES = 4
        RADIAL_DIM = 8
        INV_SQRT3 = 0.5773502691896258
        n = node_features.shape[0]
        s = node_features[:, :MUL]
        v = node_features[:, MUL:].reshape(n, MUL, 3)
        s1 = s @ W_up_s * MUL ** (-0.5)
        v1 = jnp.einsum('nmi,mk->nki', v, W_up_v) * MUL ** (-0.5)
        ss = s1[senders]
        vs = v1[senders]
        yv = edge_sh[:, 1:4]
        m_v_tp = ss[:, :, None] * yv[:, None, :]
        m_s_tp = jnp.einsum('emi,ei->em', vs, yv) * INV_SQRT3
        h = jax.nn.silu(radial_embedding @ W_r1 * RADIAL_DIM ** (-0.5))
        w = h @ W_r2 * RADIAL_DIM ** (-0.5)
        w_ss, w_vs, w_vt, w_st = jnp.split(w, 4, axis=1)
        m_s = jnp.concatenate([ss * w_ss, m_s_tp * w_st], axis=1)
        m_v = jnp.concatenate([vs * w_vs[:, :, None], m_v_tp * w_vt[:, :, None]], axis=1)
        inv = AVG_NEIGH ** (-0.5)
        S = jax.ops.segment_sum(m_s, receivers, num_segments=n) * inv
        V = jax.ops.segment_sum(m_v.reshape(m_v.shape[0], -1), receivers, num_segments=n).reshape(n, 2 * MUL, 3) * inv
        g_s = S @ W_dn_s * (2 * MUL) ** (-0.5)
        g_v = jnp.einsum('nmi,mk->nki', V, W_dn_v) * (2 * MUL) ** (-0.5)
        sk_s = jnp.einsum('nm,nmk->nk', s, W_sk_s[node_species]) * MUL ** (-0.5)
        sk_v = jnp.einsum('nmi,nmk->nki', v, W_sk_v[node_species]) * MUL ** (-0.5)
        g_s = 0.5 * (g_s + sk_s)
        g_v = 0.5 * (g_v + sk_v)
        feat_s = jax.nn.silu(g_s[:, :MUL])
        gates = jax.nn.silu(g_s[:, MUL:])
        out_v = g_v * gates[:, :, None]
        return jnp.concatenate([feat_s, out_v.reshape(n, 3 * MUL)], axis=1)
    edge_index = jnp.stack([src, dst])
    h = jnp.maximum(_layernorm(x, axis=-1), 0.0)
    x = x + _L0_gnn_ref(h, src, dst)
    h = jnp.maximum(_layernorm(x, axis=-1), 0.0)
    x = x + _L1_gnn_ref(h, edge_index, edge_attr_16, L1_gnn_W1, L1_gnn_b1, L1_gnn_W2, L1_gnn_b2)
    h = jnp.maximum(_layernorm(x, axis=-1), 0.0)
    x = x + _L2_gnn_ref(h, edge_index, L2_gnn_W_l, L2_gnn_b_l, L2_gnn_W_r, L2_gnn_b_r, L2_gnn_att, L2_gnn_bias)
    h = jnp.maximum(_layernorm(x, axis=-1), 0.0)
    x = x + _L3_gnn_ref(h, edge_attr_4, edge_attr_8, L3_gnn_W_up_s, L3_gnn_W_up_v, L3_gnn_W_r1, L3_gnn_W_r2, L3_gnn_W_dn_s, L3_gnn_W_dn_v, L3_gnn_W_sk_s, L3_gnn_W_sk_v, src, dst, node_type_4)
    return x

_drawn_inputs = setup_inputs


def setup_inputs(seed=0):
    import zlib

    import numpy as np

    out = dict(_drawn_inputs(seed))
    spreads = {'L2_gnn_b_l': (0.0, 0.352), 'L2_gnn_b_r': (0.0, 2.0), 'L2_gnn_bias': (0.0, 0.359)}
    factors = {'edge_attr_16': 2.961,
     'edge_attr_4': 4.325,
     'edge_attr_8': 5.953,
     'L1_gnn_b1': 22.865,
     'L1_gnn_b2': 8.0,
     'L2_gnn_W_r': 8.0,
     'L2_gnn_att': 5.063,
     'L3_gnn_W_up_v': 3.261,
     'L3_gnn_W_r1': 2.757,
     'L3_gnn_W_dn_v': 3.539,
     'L3_gnn_W_sk_v': 14.107,
     'L3_gnn_W_sk_s': 5.434}
    for name, (base, spread) in spreads.items():
        noise = np.random.default_rng([zlib.crc32(name.encode()), seed]).standard_normal(out[name].shape)
        drawn = base * np.exp(spread * noise) if base else spread * noise
        out[name] = jnp.asarray(drawn.astype(out[name].dtype))
    for name, factor in factors.items():
        out[name] = (out[name] * factor).astype(out[name].dtype)
    return out
```

```python
from contextlib import ExitStack

import concourse.bass as bass
from concourse import mybir

F32 = mybir.dt.float32
I32 = mybir.dt.int32
ALU = mybir.AluOpType
ACT = mybir.ActivationFunctionType
AX = mybir.AxisListType.X

P = 128
NODES, D = 3125, 128
EDGES = 50000
NBLK = -(-NODES // P)
NPAD = NBLK * P
NT = -(-EDGES // P)
NV = NT + NBLK - 1
VB = 5
NB = NV // VB
VG = -(-NV // P)
VW = VG * P
WG = [min(P, NV - g * P) for g in range(VG)]
HEADS, C = 4, 32
N_ATTR = 16 + 4 + 8
LAYERS = 3
CH = 6
ROWS = 18 + 4 + 8
SH, RAD = 18, 22
BIG = 1.0e30
LN_EPS = 1e-5
INV_SQRT3 = 0.5773502691896258
MSG = 256
SUM_SCALE = 16.0 ** -0.5 * 8.0 ** -0.5 * 64.0 ** -0.5 * 32.0 ** 0.5
OUTW = 160
SRC_SUM = NPAD
DST_SUM = 7 * 512
assert NB * VB == NV and NB % 2 == 1 and SRC_SUM + CH * NBLK <= DST_SUM


def gnn_program(nc, x, edge_ids, last_dst, edge_attrs, species, w1a, w1b, b1, w2, row_params, wlr, wup,
                wr1, wr2, wdn_a, wdn_b, wsk, out):
    ctx = ExitStack()
    with ctx:
        def sb(name, shape, dt=F32):
            return ctx.enter_context(nc.sbuf_tensor(name, shape, dt))

        def sem(name):
            return ctx.enter_context(nc.semaphore(name))

        def dram(name, shape, dt=F32):
            return nc.dram_tensor(name, shape, dt).ap()

        tables = [dram(f"table{i}", [NPAD, D]) for i in range(LAYERS + 2)]
        gathered_rows = dram("gathered_rows", [NB, P, VB * D])
        radial_hidden = dram("radial_hidden", [NB, 8 * VB, P])
        block_of_visit = dram("block_of_visit", [VG, P], I32)

        X = sb("X", [P, NBLK, D])
        H = sb("H", [P, NBLK, D])
        HT = sb("HT", [P, 2 * NV * HEADS + 80])
        RX = sb("RX", [P, 32 * MSG])
        SCR = sb("SCR", [P, 7680])
        AT = sb("AT", [P, ROWS, NV + 1])
        EI = sb("EI", [P, 5, VW])
        G = sb("G", [P, 2, VB, D])
        OH = sb("OH", [P, 2, VB, P])
        dst_rows = sb("dst_rows", [P, VG, 3, P])
        invalid_neg = sb("invalid_neg", [P, VG, P])
        src_idx = sb("src_idx", [P, NV + 1], I32)
        gather_idx = sb("gather_idx", [P, 2, VB], I32)
        block_words = sb("block_words", [1, NB], I32)
        ident = sb("ident", [P, P])
        iota_i = sb("iota_i", [P, P], I32)
        iota = sb("iota", [P, P])
        small = sb("small", [P, 8, NBLK])
        inv_deg = sb("inv_deg", [P, 2, NBLK])
        no_edges = sb("no_edges", [P, NBLK])
        self_score = sb("self_score", [P, NBLK, HEADS])
        node_max = sb("node_max", [P, NBLK, HEADS])
        self_prob = sb("self_prob", [P, NBLK, HEADS])
        means = sb("means", [P, NBLK, 32])
        tv = sb("tv", [P, 6, VG])
        tvi = sb("tvi", [P, VG], I32)
        vrow = sb("vrow", [4, P], I32)
        rowi = sb("rowi", [1, 2 * NT + 600], I32)
        rowf = sb("rowf", [1, 2 * NT])
        ones_row = sb("ones_row", [1, P])
        w1a_s, w2_s, wup_s = (sb(n, [P, D]) for n in ("w1a_s", "w2_s", "wup_s"))
        w1b_s = sb("w1b_s", [32, D])
        b1_s = sb("b1_s", [P, 1])
        rows_s = sb("rows_s", [P, 5 * D])
        wlr_s = sb("wlr_s", [P, 2 * D])
        wr1_s = sb("wr1_s", [8 * VB, 8 * VB])
        wr2_s = sb("wr2_s", [8 * VB, VB, P])
        wdna_s, wdnb_s = sb("wdna_s", [P, 96]), sb("wdnb_s", [P, 64])
        wsk_s = sb("wsk_s", [P, 96])
        spec_s = sb("spec_s", [P, NBLK], I32)
        spec_f = sb("spec_f", [P, NBLK])
        smask = sb("smask", [P, NBLK, 4])
        PS = ctx.enter_context(nc.psum_tensor("PS", [P, 8, 512], F32))
        PSF = PS[:, :, :].rearrange("p a b -> p (a b)")

        def view(t, offset, dims, parts=P, dt=None):
            width = 1
            for n in t.shape[1:]:
                width *= n
            return bass.AP(t, offset, [[width, parts]] + [list(d) for d in dims])

        RES = view(RX, 0, [[D, NBLK], [1, D]])
        XR_W = D + HEADS
        XR = view(RX, 0, [[XR_W, NBLK], [1, XR_W]])
        PM = view(RX, 0, [[8, NV], [1, 8]])
        XL_AT = NV * 8 + 8
        XL = view(RX, XL_AT, [[D, NBLK], [1, D]])
        ACC = view(RX, 0, [[MSG, NBLK], [1, MSG]])
        HTF = view(HT, 0, [[1, NPAD]])
        ES = view(HT, 0, [[HEADS, NV], [1, HEADS]])
        MS_AT = NV * HEADS
        MS = view(HT, MS_AT, [[HEADS, NV], [1, HEADS]])
        hid = view(RX, 0, [[1, NPAD]])
        bias2 = rows_s[:, 0:D]
        att = rows_s[:, D:2 * D]
        gat_bias = rows_s[:, 2 * D:3 * D]
        attr_rows = view(SCR, 0, [[N_ATTR * P, 2], [1, N_ATTR * P]])

        def id_rows(g):
            return view(HT, g * 3 * P, [[1, 3 * P]]).bitcast(I32)

        N_FILL = 9 * VG

        def fill_copy(f):
            g, j = divmod(f, 9)
            n = 1 if j == 1 else 4
            if j < 2:
                w = P
                dst = view(EI, 4 * j * VW + g * P, [[VW, n], [1, w]])
            else:
                w = min(P, NV + 1 - g * P)
                row = (0, 4, 8, 12, SH, RAD, RAD + 4)[j - 2]
                dst = view(AT, row * (NV + 1) + g * P, [[NV + 1, n], [1, w]])
            return dst, view(PS, (2 + f % 6) * 512, [[P, n], [1, w]])
        def OHS(p):
            return view(SCR, p * VB * P, [[P, VB], [1, P]])

        PR_AT = 2 * VB * P
        OT_AT = 0
        Z_AT = 2 * VB * P
        L_AT = Z_AT + 2 * VB * D
        RS_AT = L_AT + VB * D
        RT_AT = RS_AT + 8 * VB
        RH_AT = RT_AT + P
        END_AT = 2 * NV * HEADS
        M_AT = 0
        C_AT = 2 * VB * MSG
        T_AT = C_AT + VB * C
        U_AT = T_AT + 3 * VB * C
        CH_AT = U_AT + VB * C
        AC_AT = NBLK * OUTW
        ST_AT = AC_AT + 512
        SP_AT = ST_AT + 1024

        def bc(ap_tensor, offset, dims, parts=P):
            return view(ap_tensor, offset, dims, parts)

        S = {}

        def s(name):
            if name not in S:
                S[name] = sem(name)
            return S[name]

        block = ctx.enter_context(nc.Block())

        def pairs(eng, body):
            for k in range(3):
                body(k, k % 2, k // 2)
            with eng.Fori(1, (NB - 1) // 2) as j:
                body(2 * j + 1, 1, j)
                body(2 * j + 2, 0, j + 1)

        def late(k, n):
            return not (isinstance(k, int) and k < n)

        def gate(eng):
            eng.sem_inc(s("gates_passed"))

        def load_all(eng):
            for t, a in ((w1a_s, w1a), (w1b_s, w1b), (b1_s, b1), (w2_s, w2), (wlr_s, wlr), (wup_s, wup),
                         (wr1_s, wr1), (wr2_s, wr2), (wdna_s, wdn_a), (wdnb_s, wdn_b), (wsk_s, wsk), (spec_s, species)):
                eng.dma_start(t[:], a).then_inc(s("weights_loaded"), 16)
            eng.dma_start(rows_s[:], row_params.partition_broadcast(P)).then_inc(s("weights_loaded"), 16)

        W_ALL = 13 * 16
        passes = ["sage0", "sage1", "sage2", "score", "conv"]

        @block.sync
        def _(sp):
            sp.dma_start(rowi[:, 0:NT], last_dst).then_inc(s("last_loaded"), 16)
            sp.wait_ge(s("x_tail_zeroed"), 1)
            sp.dma_start(X[:, 0:NBLK - 1, :], x[0:(NBLK - 1) * P, :].rearrange("(b p) d -> p b d", p=P)).then_inc(s("x_loaded"), 16)
            sp.dma_start(X[0:NODES - (NBLK - 1) * P, NBLK - 1, :], x[(NBLK - 1) * P:NODES, :]).then_inc(s("x_loaded"), 16)
            sp.wait_ge(s("blocks_turned"), 1)
            sp.dma_start(block_of_visit, vrow[:, 0:P]).then_inc(s("blocks_out"), 16)
            sp.wait_ge(s("blocks_out"), 16)
            sp.dma_start(rowi[:, 2 * NT:2 * NT + VW], block_of_visit.rearrange("g v -> (g v)").rearrange("(o n) -> o n", o=1)).then_inc(s("blocks_in"), 16)
            for i in range(LAYERS + 2):
                src = [H[:], H[:], H[:], XL, XL][i]
                sp.wait_ge(s("table_ready"), i + 1)
                sp.dma_start(tables[i].rearrange("(b p) d -> p b d", p=P), src).then_inc(s("table_written"), 16)
                if i == LAYERS:
                    def store(k, p, m):
                        sp.wait_ge(s(f"score_gathered{p}"), 16 * VB * (m + 1))
                        sp.dma_start(gathered_rows[bass.ds(k, 1)].rearrange("o p n -> p (o n)"),
                                     G[:, p].rearrange("p a b -> p (a b)")).then_inc(s(f"rows_stored{p}"), 16)
                        sp.wait_ge(s("radial_hidden_ready"), k + 1)
                        sp.dma_start(radial_hidden[bass.ds(k, 1)].rearrange("o p n -> p (o n)"),
                                     bc(SCR, RH_AT + p * P, [[1, P]], 8 * VB)).then_inc(s(f"hidden_stored{p}"), 16)
                    pairs(sp, store)
                    for p in range(2):
                        n = NB // 2 + (1 - p)
                        sp.wait_ge(s(f"rows_stored{p}"), 16 * n)
                        sp.wait_ge(s(f"hidden_stored{p}"), 16 * n)

                    def load(k, p, m):
                        if late(k, 2):
                            sp.wait_ge(s("sum_done"), k - 1)
                        else:
                            sp.wait_ge(s("z_made"), NB)
                        sp.dma_start(G[:, p].rearrange("p a b -> p (a b)"),
                                     gathered_rows[bass.ds(k, 1)].rearrange("o p n -> p (o n)")).then_inc(s(f"rows_back{p}"), 16)
                    pairs(sp, load)
                if i == LAYERS + 1:
                    def load_hidden(k, p, m):
                        if late(k, 2):
                            sp.wait_ge(s("conv_weights_made"), k - 1)
                        sp.dma_start(bc(SCR, CH_AT + p * P, [[1, P]], 8 * VB),
                                     radial_hidden[bass.ds(k, 1)].rearrange("o p n -> p (o n)")).then_inc(s(f"hidden_back{p}"), 16)
                    pairs(sp, load_hidden)
            sp.wait_ge(s("result_ready"), 1)
            sp.dma_start(out[0:(NBLK - 1) * P, :].rearrange("(b p) d -> p b d", p=P), X[:, 0:NBLK - 1, :]).then_inc(s("out_written"), 16)
            sp.dma_start(out[(NBLK - 1) * P:NODES, :], X[0:NODES - (NBLK - 1) * P, NBLK - 1, :]).then_inc(s("out_written"), 16)
            sp.wait_ge(s("out_written"), 32)
            sp.wait_ge(s("table_written"), 16 * (LAYERS + 2))

        @block.gpsimd
        def _(pool):
            pool.memset(X[:, NBLK - 1, :], 0.0).then_inc(s("x_tail_zeroed"), 1)
            pool.iota(iota_i[:], pattern=[[1, P]], base=0, channel_multiplier=0).then_inc(s("iota_made"), 1)
            pool.iota(tvi[:], pattern=[[P, VG]], base=0, channel_multiplier=1).then_inc(s("iota_made"), 1)
            pool.iota(rowi[:, NT:2 * NT], pattern=[[1, NT]], base=0, channel_multiplier=0).then_inc(s("iota_made"), 1)
            pool.memset(ident[:], 0.0).then_inc(s("ident_zeroed"), 1)
            pool.memset(ones_row[:], 1.0).then_inc(s("ones_made"), 1)
            pool.memset(AT[:, 16:18, :], 1.0).then_inc(s("ones_made"), 1)
            pool.wait_ge(s("ident_zeroed"), 1)
            pool.affine_select(out=ident[:], in_=ident[:], compare_op=ALU.not_equal, fill=1.0, base=0,
                               pattern=[[-1, P]], channel_multiplier=1).then_inc(s("ident_made"), 1)
            pool.wait_ge(s("tiles_found"), 1)
            for g in range(VG):
                at = bass.IndirectOffsetOnAxis(ap=tvi[:, g:g + 1], axis=0)
                pool.indirect_dma_start(id_rows(g), None, edge_ids, at).then_inc(s(f"ids_in{g}"), 16)
            for g in range(VG):
                at = bass.IndirectOffsetOnAxis(ap=tvi[:, g:g + 1], axis=0)
                if g >= 2:
                    pool.wait_ge(s("fill_turned"), 9 * (g - 1))
                pool.indirect_dma_start(view(SCR, (g % 2) * N_ATTR * P, [[1, N_ATTR * P]]), None, edge_attrs, at).then_inc(s(f"attrs_in{g}"), 16)

            for i, name in enumerate(passes):
                pool.wait_ge(s("table_written"), 16 * (i + 1))

                def gather(k, p, m):
                    pool.wait_ge(s(f"{name}_idx_ready"), k + 1)
                    gate(pool)
                    if late(k, 2):
                        pool.wait_ge(s({"score": "z_made", "conv": "messages_ready"}.get(name, f"{name}_rows_used")), k - 1)
                        gate(pool)
                        if name == "score":
                            pool.wait_ge(s(f"rows_stored{p}"), 16 * m)
                            gate(pool)
                    for q in range(VB):
                        pool.indirect_dma_start(G[:, p, q, :], None, tables[i],
                                                bass.IndirectOffsetOnAxis(ap=gather_idx[:, p, q:q + 1], axis=0)
                                                ).then_inc(s(f"{name}_gathered{p}"), 16)
                pairs(pool, gather)

            pool.wait_ge(s("messages_summed"), 1)
            for b in range(NBLK):
                if b >= 2:
                    pool.wait_ge(s("spread_turned"), b - 1)
                h0 = b * D
                pool.tensor_tensor(view(SCR, SP_AT + (b % 2) * 512, [[32, 4], [1, 32]]),
                                   view(H, h0, [[0, 4], [1, 32]]), view(smask, 4 * b, [[1, 4], [0, 32]]), ALU.mult)
                for i3 in range(3):
                    ins = pool.tensor_tensor(view(SCR, SP_AT + (b % 2) * 512 + 128 * (i3 + 1), [[32, 4], [1, 32]]),
                                             view(H, h0 + 32 + i3, [[0, 4], [3, 32]]), view(smask, 4 * b, [[1, 4], [0, 32]]), ALU.mult)
                ins.then_inc(s("spread"), 1)

        @block.scalar
        def _(act):
            load_all(act)

            def norm_part(n):
                act.wait_ge(s("centred"), n + 1)
                act.activation(XL, H[:], ACT.Square).then_inc(s("squared"), 1)
                act.wait_ge(s("var_ready"), n + 1)
                act.activation(small[:, 4, :], small[:, 3, :], ACT.Sqrt).then_inc(s("std_ready"), 1)

            def copy_idx(name, k, p, m):
                if late(k, 2):
                    act.wait_ge(s(f"{name}_gathered{p}"), 16 * VB * m)
                    gate(act)
                act.copy(gather_idx[:, p, :], src_idx[:, bass.ds(VB * k, VB)]).then_inc(s(f"{name}_idx_ready"), 1)

            def turned_h(n):
                for g in range(7):
                    w = min(4, NBLK - 4 * g) * P
                    act.wait_ge(s("h_turned"), 7 * n + g + 1)
                    act.copy(HTF[:, g * 512:g * 512 + w], PSF[:, g * 512:g * 512 + w]).then_inc(s("ht_ready"), 1)

            norm_part(0)
            for f in range(1, N_FILL, 2):
                act.wait_ge(s("fill_turned"), f + 1)
                dst, src = fill_copy(f)
                act.copy(dst, src).then_inc(s("fill_copied_act"), 1)

            act.wait_ge(s("idx_made"), 1)
            for i, name in enumerate(passes[:LAYERS]):
                if i:
                    act.wait_ge(s(f"{passes[i - 1]}_rows_used"), NB)

                def idx(k, p, m):
                    copy_idx(name, k, p, m)
                pairs(act, idx)
            norm_part(1)
            turned_h(0)
            for g in range(7):
                w = min(4, NBLK - 4 * g) * P
                act.wait_ge(s("means_turned"), g + 1)
                act.copy(view(SCR, g * 512, [[1, w]], 32), PS[0:32, g % 2, 0:w]).then_inc(s("mt_ready"), 1)
            act.wait_ge(s("weights_loaded"), W_ALL)
            for g in range(7):
                w = min(4, NBLK - 4 * g) * P
                act.wait_ge(s("hidden_made"), g + 1)
                act.activation(hid[:, g * 512:g * 512 + w], PS[:, 2 + g % 2, 0:w], ACT.Identity, bias=b1_s[:, 0:1]).then_inc(s("hidden_biased"), 1)
            norm_part(2)
            turned_h(1)

            def score(k, p, m):
                copy_idx("score", k, p, m)
                if late(k, 1):
                    act.wait_ge(s("radial_turned"), k)
                    gate(act)
                act.copy(bc(SCR, RS_AT, [[VB, 8], [1, VB]]), AT[:, RAD:RAD + 8, bass.ds(VB * k, VB)]).then_inc(s("radial_ready"), 1)
                act.wait_ge(s("oh_turned"), k + 1)
                if late(k, 2):
                    act.wait_ge(s("z_made"), k - 1)
                act.copy(bc(SCR, OT_AT + p * VB * P, [[1, VB * P]]), bc(PS, p * 1024, [[1, VB * P]])).then_inc(s("ot_ready"), 1)
                act.wait_ge(s("radial_turned"), k + 1)
                act.copy(bc(SCR, RT_AT, [[1, P]], 8 * VB), PS[0:8 * VB, 7, 0:P]).then_inc(s("radial_t_ready"), 1)
                if late(k, 1):
                    z_out(k - 1, 1 - p)
                act.wait_ge(s("hidden_pre_made"), k + 1)
                if late(k, 2):
                    act.wait_ge(s(f"hidden_stored{p}"), 16 * m)
                act.activation(bc(SCR, RH_AT + p * P, [[1, P]], 8 * VB), PS[0:8 * VB, 7, 256:256 + P], ACT.Silu,
                               scale=8.0 ** -0.5).then_inc(s("radial_hidden_ready"), 1)

            def z_out(k, p):
                act.wait_ge(s("z_made"), k + 1)
                if late(k, 2):
                    act.wait_ge(s("scored"), k - 1)
                act.copy(bc(SCR, Z_AT + p * VB * D, [[D, VB], [1, D]]), bc(PS, 4 * 512, [[256, VB], [1, D]])).then_inc(s("z_copied"), 1)
                act.copy(view(HT, MS_AT + VB * HEADS * k, [[HEADS, VB], [1, HEADS]]),
                         bc(PS, 4 * 512 + D, [[256, VB], [1, HEADS]])).then_inc(s("z_copied"), 1)
            pairs(act, score)
            z_out(NB - 1, 0)

            act.wait_ge(s("below_max"), 1)
            act.activation(PM[:, :, 0:HEADS], ES, ACT.Exp).then_inc(s("probs_ready"), 1)
            act.wait_ge(s("self_below_max"), 1)
            act.activation(self_prob[:], self_prob[:], ACT.Exp).then_inc(s("self_prob_ready"), 1)
            act.wait_ge(s("elu_arg"), 1)
            act.activation(H[:], H[:], ACT.Exp).then_inc(s("elu_exp"), 1)
            norm_part(3)
            turned_h(2)

            def conv(k, p, m):
                copy_idx("conv", k, p, m)
            pairs(act, conv)
            for b in range(NBLK):
                act.wait_ge(s("acc_turned"), b + 1)
                if b >= 2:
                    act.wait_ge(s("update_made"), b - 1)
                act.activation(view(SCR, AC_AT + (b % 2) * 256, [[1, 256]]), PS[:, b % 2, 0:256], ACT.Copy, scale=SUM_SCALE)
                act.wait_ge(s("spread_turned"), b + 1)
                act.copy(view(SCR, ST_AT + (b % 2) * 512, [[1, 512]]), PS[:, 2 + b % 2, :]).then_inc(s("final_copied"), 1)
            act.wait_ge(s("update_ready"), 1)
            act.activation(view(SCR, 0, [[OUTW, NBLK], [1, 64]]), view(SCR, 0, [[OUTW, NBLK], [1, 64]]), ACT.Silu).then_inc(s("gates_ready"), 1)

        @block.vector
        def _(dve):
            steps = [0]

            def done(ins):
                steps[0] += 1
                ins.then_inc(s("dve_step"), 1)
                dve.wait_ge(s("dve_step"), steps[0])

            def norm(n):
                done(dve.tensor_reduce(small[:, 0, :], X[:], AX, ALU.add))
                done(dve.tensor_scalar(small[:, 1, :], small[:, 0, :], 1.0 / D, None, ALU.mult))
                dve.tensor_tensor(H[:], X[:], view(small, NBLK, [[1, NBLK], [0, D]]), ALU.subtract).then_inc(s("centred"), 1)
                dve.wait_ge(s("squared"), n + 1)
                done(dve.tensor_reduce(small[:, 2, :], XL, AX, ALU.add))
                dve.tensor_scalar(small[:, 3, :], small[:, 2, :], 1.0 / D, LN_EPS, ALU.mult, ALU.add).then_inc(s("var_ready"), 1)
                dve.wait_ge(s("std_ready"), n + 1)
                done(dve.reciprocal(small[:, 5, :], small[:, 4, :]))
                return dve.scalar_tensor_tensor(H[:], H[:], 0.0, view(small, 5 * NBLK, [[1, NBLK], [0, D]]), ALU.max, ALU.mult)

            dve.wait_ge(s("iota_made"), 3)
            dve.tensor_copy(iota[:], iota_i[:])
            dve.tensor_copy(tv[:, 0, :], tvi[:])
            done(dve.tensor_copy(rowf[:, NT:2 * NT], rowi[:, NT:2 * NT]))
            dve.wait_ge(s("last_loaded"), 16)
            done(dve.tensor_scalar(rowi[:, 0:NT], rowi[:, 0:NT], 7, None, ALU.arith_shift_right))
            done(dve.tensor_copy(rowf[:, 0:NT], rowi[:, 0:NT]))
            dve.tensor_tensor(rowf[:, 0:NT], rowf[:, 0:NT], rowf[:, NT:2 * NT], ALU.add).then_inc(s("ends_ready"), 1)
            dve.wait_ge(s("ends_spread"), 1)
            for g in range(VG):
                done(dve.tensor_scalar(H[:, g * 4:g * 4 + 4, :].rearrange("p a b -> p (a b)")[:, 0:NT], PS[:, 0, 0:NT], tv[:, 0, g:g + 1], None, ALU.is_lt))
                done(dve.tensor_reduce(tv[:, 1, g:g + 1], H[:, g * 4:g * 4 + 4, :].rearrange("p a b -> p (a b)")[:, 0:NT], AX, ALU.add))
            done(dve.tensor_scalar(tv[:, 2, :], tv[:, 1, :], float(NT - 1), None, ALU.min))
            dve.tensor_copy(tvi[:], tv[:, 2, :]).then_inc(s("tiles_found"), 1)
            done(dve.tensor_tensor(tv[:, 3, :], tv[:, 0, :], tv[:, 2, :], ALU.subtract))
            done(dve.tensor_scalar(tv[:, 4, :], tv[:, 3, :], float(NBLK - 1), None, ALU.min))
            dve.tensor_scalar(tv[:, 5, :], tv[:, 4, :], -float(P), None, ALU.mult).then_inc(s("blocks_ready"), 1)
            dve.wait_ge(s("blocks_in_psum"), 1)
            dve.tensor_copy(vrow[:, 0:P], PS[0:4, 1, 0:P]).then_inc(s("blocks_turned"), 1)
            dve.wait_ge(s("blocks_in"), 16)
            B0 = 2 * NT
            done(dve.tensor_copy(block_words[:], view(rowi, B0, [[VB, NB]], 1)))
            for q in range(1, VB):
                done(dve.tensor_scalar(view(rowi, 0, [[1, NB]], 1), view(rowi, B0 + q, [[VB, NB]], 1), 5 * q, None, ALU.logical_shift_left))
                done(dve.tensor_tensor(block_words[:], block_words[:], view(rowi, 0, [[1, NB]], 1), ALU.bitwise_or))
            dve.wait_ge(s("x_loaded"), 32)
            norm(0).then_inc(s("table_ready"), 1)
            dve.wait_ge(s("table_ready"), 1)
            for g in range(VG):
                dve.wait_ge(s(f"ids_in{g}"), 16)
                dr = dst_rows[:, g]
                idr = id_rows(g)
                done(dve.tensor_copy(dr.rearrange("p a b -> p (a b)"), idr))
                st = [view(RX, (5 * g + i) * P, [[1, P]]) for i in range(5)]
                dve.tensor_copy(st[0], dr[:, 0])
                dve.tensor_scalar(view(HT, 1536, [[1, P]]).bitcast(I32), idr[:, 0:P], 7, None, ALU.arith_shift_right)
                dve.tensor_scalar(view(HT, 1664, [[1, P]]).bitcast(I32), idr[:, 0:P], 127, None, ALU.bitwise_and)
                done(dve.tensor_scalar(st[3], dr[:, 1], tv[:, 5, g:g + 1], None, ALU.add))
                va, vb, vc = (view(HT, 1792 + 128 * i, [[1, P]]) for i in range(3))
                dve.tensor_copy(st[2], view(HT, 1664, [[1, P]]).bitcast(I32))
                dve.tensor_copy(vc, view(HT, 1536, [[1, P]]).bitcast(I32))
                done(dve.tensor_scalar(va, st[3], 0.0, None, ALU.is_ge))
                done(dve.scalar_tensor_tensor(vb, st[3], float(P - 1), va, ALU.is_le, ALU.mult))
                done(dve.scalar_tensor_tensor(vc, vb, -64.0, vc, ALU.mult, ALU.add))
                dve.tensor_scalar(st[1], vc, 64.0, None, ALU.add)
                dve.tensor_scalar(invalid_neg[:, g, :], vb, 1.0, BIG, ALU.subtract, ALU.mult)
                done(dve.tensor_tensor(va, dr[:, 1], dr[:, 2], ALU.not_equal))
                dve.tensor_tensor(st[4], va, vb, ALU.mult).then_inc(s("kinds_ready"), 1)
            for f in range(0, N_FILL, 2):
                dve.wait_ge(s("fill_turned"), f + 1)
                dst, src = fill_copy(f)
                dve.tensor_copy(dst, src).then_inc(s("fill_copied_dve"), 1)
            dve.wait_ge(s("fill_copied_act"), N_FILL // 2)
            dve.wait_ge(s("fill_copied_dve"), N_FILL - N_FILL // 2)
            dve.tensor_copy(src_idx[:], EI[:, 0, 0:NV + 1]).then_inc(s("idx_made"), 1)
            done(dve.tensor_copy(RES, H[:]))
            dve.wait_ge(s("ones_made"), 2)

            def one_hot(dst, kind, k):
                return dve.tensor_tensor(dst, view(iota, 0, [[0, VB], [1, P]]), view(EI, kind * VW + VB * k, [[1, VB], [0, P]]), ALU.is_equal)

            for i in range(LAYERS):
                name = passes[i]
                r0 = 12 - CH * i
                dve.memset(PSF, 0.0).then_inc(s("sums_zeroed"), 1)

                def hot(k, p, m):
                    if late(k, 2):
                        dve.wait_ge(s(f"{name}_rows_used"), k - 1)
                    sbh = view(SCR, PR_AT + p * VB * NBLK * 7, [[NBLK, VB], [1, NBLK]])
                    prod = view(SCR, PR_AT + p * VB * NBLK * 7 + VB * NBLK, [[NBLK * CH, VB], [CH, NBLK], [1, CH]])
                    dve.tensor_tensor(sbh, view(iota, 0, [[0, VB], [1, NBLK]]), view(EI, VW + VB * k, [[1, VB], [0, NBLK]]), ALU.is_equal).then_inc(s(f"{name}_src_block"), 1)
                    one_hot(OH[:, p], 3, k)
                    one_hot(OHS(p), 2, k)
                    dve.wait_ge(s(f"{name}_src_block"), k + 1)
                    dve.tensor_tensor(prod, view(SCR, PR_AT + p * VB * NBLK * 7, [[NBLK, VB], [1, NBLK], [0, CH]]),
                                      view(AT, r0 * (NV + 1) + VB * k, [[1, VB], [0, NBLK], [NV + 1, CH]]), ALU.mult).then_inc(s(f"{name}_hot"), 1)
                pairs(dve, hot)
                dve.wait_ge(s(f"{name}_rows_used"), NB)
                by_src = view(PS, SRC_SUM, [[CH, NBLK], [1, CH]])
                by_dst = view(PS, DST_SUM, [[CH, NBLK], [1, CH]])
                n = min(CH, 16 - r0)
                if i == 0:
                    for side, sums in enumerate((by_src, by_dst)):
                        done(dve.tensor_scalar(small[:, side, :], sums[:, :, 4], 1.0, None, ALU.max))
                        done(dve.reciprocal(inv_deg[:, side, :], small[:, side, :]))
                    dve.tensor_scalar(no_edges[:], by_dst[:, :, 4], 0.5, None, ALU.is_lt)
                dve.tensor_copy(means[:, :, r0:r0 + n], by_src[:, :, 0:n])
                dve.tensor_copy(means[:, :, 16 + r0:16 + r0 + n], by_dst[:, :, 0:n])
                done(dve.tensor_tensor(XL, view(PS, 0, [[D, NBLK], [1, D]]), view(inv_deg, NBLK, [[1, NBLK], [0, D]]), ALU.mult))
                dve.wait_ge(s("table_written"), 16 * (i + 1))
                add = dve.tensor_tensor(H[:], H[:], XL, ALU.add)
                if i < LAYERS - 1:
                    add.then_inc(s("table_ready"), 1)
                    dve.wait_ge(s("table_ready"), i + 2)
                else:
                    done(add)
                done(dve.scalar_tensor_tensor(RES, H[:], 1.0 / (1.0 + i), RES, ALU.mult, ALU.add))
            done(dve.tensor_tensor(X[:], X[:], RES, ALU.add))

            done(dve.tensor_tensor(means[:, :, 0:16], means[:, :, 0:16], view(inv_deg, 0, [[1, NBLK], [0, 16]]), ALU.mult))
            dve.tensor_tensor(means[:, :, 16:32], means[:, :, 16:32], view(inv_deg, NBLK, [[1, NBLK], [0, 16]]), ALU.mult).then_inc(s("means_ready"), 1)
            norm(1).then_inc(s("h_ready"), 1)
            dve.wait_ge(s("weights_loaded"), W_ALL)
            done(dve.tensor_tensor(X[:], X[:], view(rows_s, 0, [[0, NBLK], [1, D]]), ALU.add))
            for g in range(7):
                w = min(4, NBLK - 4 * g) * P
                dve.wait_ge(s("hidden_biased"), g + 1)
                hg = hid[:, g * 512:g * 512 + w]
                dve.scalar_tensor_tensor(hg, hg, 0.01, hg, ALU.mult, ALU.max).then_inc(s("hidden_ready"), 1)
            for g in range(7):
                w = min(4, NBLK - 4 * g)
                dve.wait_ge(s("mlp_made"), g + 1)
                xg = view(X, g * 512, [[1, w * P]])
                ins = dve.tensor_tensor(xg, xg, PS[:, 4 + g % 2, 0:w * P], ALU.add)
                ins.then_inc(s("mlp_added"), 1)
            dve.wait_ge(s("mlp_added"), 7)

            norm(2).then_inc(s("h_ready"), 1)
            for g in range(13):
                w = min(2, NBLK - 2 * g)
                dve.wait_ge(s("lr_made"), g + 1)
                bank = g % 4
                dve.tensor_tensor(XL[:, 2 * g:2 * g + w, :], view(PS, bank * 512, [[256, w], [1, D]]),
                                  view(rows_s, 3 * D, [[0, w], [1, D]]), ALU.add)
                ins = dve.tensor_tensor(XR[:, 2 * g:2 * g + w, 0:D], view(PS, bank * 512 + D, [[256, w], [1, D]]),
                                        view(rows_s, 4 * D, [[0, w], [1, D]]), ALU.add)
                ins.then_inc(s("lr_copied"), 1)
            dve.wait_ge(s("lr_copied"), 13)
            ins = dve.tensor_tensor(H[:], XL, XR[:, :, 0:D], ALU.add)
            ins.then_inc(s("table_ready"), 1)
            dve.wait_ge(s("table_ready"), 4)
            done(dve.scalar_tensor_tensor(H[:], H[:], 0.2, H[:], ALU.mult, ALU.max))
            done(dve.tensor_tensor(H[:], H[:], view(rows_s, D, [[0, NBLK], [1, D]]), ALU.mult))
            done(dve.tensor_reduce(self_score[:], H[:].rearrange("p b (h c) -> p b h c", h=HEADS), AX, ALU.add))
            dve.tensor_copy(XR[:, :, D:XR_W], self_score[:]).then_inc(s("xr_ready"), 1)

            def score(k, p, m):
                if late(k, 2):
                    dve.wait_ge(s("oh_turned"), k - 1)
                one_hot(OH[:, p], 3, k).then_inc(s("score_hot"), 1)
                if late(k, 1):
                    rate(k - 1, 1 - p)

            def rate(k, p):
                dve.wait_ge(s("z_copied"), 2 * k + 2)
                zz = bc(SCR, Z_AT + p * VB * D, [[1, VB * D]])
                ll = bc(SCR, L_AT, [[1, VB * D]])
                dve.scalar_tensor_tensor(ll, zz, 0.2, zz, ALU.mult, ALU.max).then_inc(s("leaky"), 1)
                dve.wait_ge(s("leaky"), k + 1)
                dve.tensor_tensor(bc(SCR, L_AT, [[D, VB], [1, D]]), bc(SCR, L_AT, [[D, VB], [1, D]]),
                                  view(rows_s, D, [[0, VB], [1, D]]), ALU.mult).then_inc(s("weighed"), 1)
                dve.wait_ge(s("weighed"), k + 1)
                gate(dve)
                dve.tensor_reduce(view(HT, VB * HEADS * k, [[1, VB * HEADS]]), bc(SCR, L_AT, [[C, VB * HEADS], [1, C]]),
                                  AX, ALU.add).then_inc(s("scored"), 1)
            pairs(dve, score)
            dve.wait_ge(s("scored"), NB - 1)
            rate(NB - 1, 0)
            dve.wait_ge(s("scored"), NB)

            N16 = VG * HEADS * P
            CF_AT, PRE_AT, SUF_AT = 0, N16 + 1, 2 * N16 + 1
            E2 = view(H, 0, [[HEADS * P, VG], [P, HEADS], [1, P]])
            cont = view(SCR, CF_AT, [[HEADS * P, VG], [P, HEADS], [1, P]])
            dve.memset(view(H, 0, [[1, N16]]), -BIG)
            done(dve.memset(view(SCR, CF_AT, [[1, N16 + 1]]), -BIG))
            for g in range(VG):
                first = g * 3 * P + P
                done(dve.tensor_tensor(view(RX, g * P, [[1, P - 1]]), view(dst_rows, first + 1, [[1, P - 1]]), view(dst_rows, first, [[1, P - 1]]), ALU.not_equal))
                done(dve.tensor_scalar(view(SCR, CF_AT + g * HEADS * P + 1, [[P, HEADS], [1, P - 1]]), view(RX, g * P, [[0, HEADS], [1, P - 1]]), -BIG, None, ALU.mult))
            dve.wait_ge(s("scores_turned"), 1)
            for g in range(VG):
                w = WG[g]
                ins = dve.tensor_tensor(view(H, g * HEADS * P, [[P, HEADS], [1, P]], w), view(PS, g * 512, [[P, HEADS], [1, P]], w),
                                        view(invalid_neg, g * P, [[0, HEADS], [1, P]], w), ALU.add)
            done(ins)
            for p in range(2):
                dve.wait_ge(s(f"hidden_stored{p}"), 16 * (NB // 2 + 1 - p))
            flat = lambda t, at, step=1: view(t, at + (N16 - 1 if step < 0 else 0), [[step, N16]])
            dve.tensor_tensor_scan(flat(SCR, PRE_AT), flat(SCR, CF_AT), flat(H, 0), -BIG, ALU.add, ALU.max)
            done(dve.tensor_tensor_scan(flat(SCR, SUF_AT, -1), flat(SCR, CF_AT + 1, -1), flat(H, 0, -1), -BIG, ALU.add, ALU.max))
            for g in range(VG):
                dve.tensor_copy(view(HT, END_AT + (0 * VG + g) * 4, [[1, 4]]), view(SCR, PRE_AT + g * 512 + P - 1, [[P, 4]]))
                dve.tensor_copy(view(HT, END_AT + (1 * VG + g) * 4, [[1, 4]]), view(SCR, SUF_AT + g * 512, [[P, 4]]))
                dve.tensor_copy(view(HT, END_AT + (2 * VG + g) * 4, [[1, 4]]), view(dst_rows, g * 3 * P + P, [[0, 4]]))
                ins = dve.tensor_copy(view(HT, END_AT + (3 * VG + g) * 4, [[1, 4]]), view(dst_rows, g * 3 * P + 2 * P - 1, [[0, 4]]))
            ins.then_inc(s("ends_made"), 1)
            dve.wait_ge(s("ends_turned"), 1)
            R = lambda i, at=0, n=NV, step=1: view(H, i * VW + at, [[step, n]], 4)
            for i in range(4):
                ins = dve.tensor_copy(R(i), PS[0:4, i, 0:NV])
            done(ins)
            A = lambda i, at=0, n=NV, step=1: view(RX, i * VW + at, [[step, n]], 4)
            done(dve.memset(view(RX, 0, [[1, 6 * VW]], 4), 1.0))
            dve.tensor_tensor(A(0, 1, NV - 1), R(2, 1, NV - 1), R(3, 0, NV - 1), ALU.not_equal)
            done(dve.tensor_tensor(A(1), R(2), R(3), ALU.not_equal))
            dve.tensor_tensor(A(2), A(0), A(1), ALU.max)
            done(dve.tensor_tensor(A(3), A(0, 1), A(1), ALU.max))
            done(dve.tensor_scalar(view(RX, 0, [[VW, 4], [1, NV + 1]], 4), view(RX, 0, [[VW, 4], [1, NV + 1]], 4), -BIG, None, ALU.mult))
            dve.tensor_tensor_scan(A(4), A(2), R(0), -BIG, ALU.add, ALU.max)
            done(dve.tensor_tensor_scan(A(5, NV - 1, NV, -1), A(3, NV - 1, NV, -1), R(1, NV - 1, NV, -1), -BIG, ALU.add, ALU.max))
            done(dve.memset(view(H, 0, [[1, 2 * VW]], 4), -BIG))
            dve.tensor_tensor(R(0, 1, NV - 1), A(4, 0, NV - 1), A(0, 1, NV - 1), ALU.add)
            dve.tensor_tensor(R(1, 0, NV - 1), A(5, 1, NV - 1), A(0, 1, NV - 1), ALU.add).then_inc(s("carries_ready"), 1)
            dve.wait_ge(s("carries_turned"), 1)
            done(dve.tensor_tensor(flat(SCR, PRE_AT), flat(SCR, PRE_AT), flat(SCR, SUF_AT), ALU.max))
            done(dve.tensor_copy(view(HT, END_AT, [[1, 32]]), PS[:, 4, 0:32]))
            for side in range(2):
                edge_of = P if side == 0 else 2 * P - 1
                for g in range(VG):
                    done(dve.tensor_scalar(view(SCR, CF_AT, [[1, P]]), view(dst_rows, g * 3 * P + P, [[1, P]]),
                                           view(dst_rows, g * 3 * P + edge_of, [[1, 1]]), -BIG, ALU.not_equal, ALU.mult))
                    for h in range(HEADS):
                        m_gh = view(SCR, PRE_AT + (g * HEADS + h) * P, [[1, P]])
                        ins = dve.scalar_tensor_tensor(m_gh, view(SCR, CF_AT, [[1, P]]), view(HT, END_AT + side * 16 + g * 4 + h, [[1, 1]]),
                                                       m_gh, ALU.add, ALU.max)
                    done(ins)
            dve.memset(small[:, 6, :], 0.0).then_inc(s("maxima_ready"), 1)
            dve.wait_ge(s("maxima_turned"), 1)
            for g in range(VG):
                w = WG[g]
                ms = view(HT, MS_AT + g * P * HEADS, [[1, HEADS], [HEADS, w]])
                ins = dve.tensor_tensor(ms, ms, view(PS, g * 512, [[P, HEADS], [1, w]]), ALU.max)
            done(ins)
            done(dve.tensor_tensor(ES, ES, MS, ALU.subtract))
            dve.tensor_scalar(ES, ES, 0.0, None, ALU.min).then_inc(s("below_max"), 1)
            dve.tensor_tensor(PM[:, :, HEADS:8], MS, view(EI, 4 * VW, [[1, NV], [0, HEADS]]), ALU.mult)
            dve.memset(PSF, 0.0).then_inc(s("sums_zeroed"), 1)
            dve.wait_ge(s("probs_ready"), 1)

            def weigh(k, p, m):
                if late(k, 2):
                    dve.wait_ge(s("sum_done"), k - 1)
                one_hot(OH[:, p], 3, k)
                dve.wait_ge(s(f"rows_back{p}"), 16 * (m + 1))
                gg = view(G, p * VB * D, [[D, VB], [C, HEADS], [1, C]])
                dve.tensor_tensor(gg, gg, view(RX, 8 * VB * k, [[8, VB], [1, HEADS], [0, C]]), ALU.mult).then_inc(s("sum_hot"), 1)
            pairs(dve, weigh)
            dve.wait_ge(s("sum_done"), NB)
            sums8 = view(PS, DST_SUM, [[8, NBLK], [1, 8]])
            done(dve.tensor_tensor(node_max[:], self_score[:], view(no_edges, 0, [[1, NBLK], [0, HEADS]]), ALU.mult))
            done(dve.tensor_tensor(node_max[:], node_max[:], sums8[:, :, 4:8], ALU.add))
            dve.tensor_tensor(self_prob[:], self_score[:], node_max[:], ALU.subtract).then_inc(s("self_below_max"), 1)
            dve.wait_ge(s("self_prob_ready"), 1)
            h4 = H[:].rearrange("p b (h c) -> p b h c", h=HEADS)
            for h in range(HEADS):
                dve.tensor_tensor(H[:, :, h * C:(h + 1) * C], XL[:, :, h * C:(h + 1) * C], view(self_prob, h, [[HEADS, NBLK], [0, C]]), ALU.mult)
            done(dve.tensor_tensor(node_max[:], self_prob[:], sums8[:, :, 0:4], ALU.add))
            done(dve.tensor_tensor(H[:], H[:], view(PS, 0, [[D, NBLK], [1, D]]), ALU.add))
            done(dve.tensor_scalar(node_max[:], node_max[:], 1e-16, None, ALU.add))
            done(dve.reciprocal(node_max[:], node_max[:]))
            for h in range(HEADS):
                ins = dve.tensor_tensor(H[:, :, h * C:(h + 1) * C], H[:, :, h * C:(h + 1) * C], view(node_max, h, [[HEADS, NBLK], [0, C]]), ALU.mult)
            done(ins)
            done(dve.tensor_tensor(H[:], H[:], view(rows_s, 2 * D, [[0, NBLK], [1, D]]), ALU.add))
            done(dve.scalar_tensor_tensor(X[:], H[:], 0.0, X[:], ALU.max, ALU.add))
            dve.tensor_scalar(H[:], H[:], 0.0, None, ALU.min).then_inc(s("elu_arg"), 1)
            dve.wait_ge(s("elu_exp"), 1)
            done(dve.scalar_tensor_tensor(X[:], H[:], -1.0, X[:], ALU.add, ALU.add))

            norm(3).then_inc(s("h_ready"), 1)
            for g in range(7):
                w = min(4, NBLK - 4 * g) * P
                dve.wait_ge(s("up_made"), g + 1)
                dve.tensor_scalar(view(RX, XL_AT + g * 512, [[1, w]]), PS[:, g, 0:w], 32.0 ** -0.5, None, ALU.mult).then_inc(s("up_copied"), 1)
            dve.wait_ge(s("up_copied"), 7)
            dve.tensor_copy(spec_f[:], spec_s[:]).then_inc(s("table_ready"), 1)
            dve.wait_ge(s("table_ready"), 5)
            for sp_ in range(4):
                dve.tensor_scalar(smask[:, :, sp_], spec_f[:], float(sp_), None, ALU.is_equal)
            dve.wait_ge(s("table_written"), 16 * 5)
            done(dve.memset(view(RX, 0, [[1, NBLK * MSG]]), 0.0))

            def message(k, p, m):
                if late(k, 2):
                    dve.wait_ge(s("message_sums"), VB * (k - 1))
                one_hot(OH[:, p], 3, k)
                dve.wait_ge(s(f"conv_gathered{p}"), 16 * VB * (m + 1))
                dve.wait_ge(s("conv_weights_made"), k + 1)
                g0 = p * VB * D
                m0 = M_AT + p * VB * MSG
                w0 = 5 * 512
                y = lambda dims: view(AT, (SH + 1) * (NV + 1) + VB * k, dims)
                dve.tensor_tensor(view(SCR, C_AT, [[C, VB], [1, C]]), view(G, g0, [[D, VB], [1, C]]), view(PS, w0 + 64, [[P, VB], [1, C]]), ALU.mult)
                dve.tensor_tensor(view(SCR, T_AT, [[96, VB], [C, 3], [1, C]]), view(G, g0 + C, [[D, VB], [C, 3], [1, C]]),
                                  y([[1, VB], [NV + 1, 3], [0, C]]), ALU.mult).then_inc(s("conv_parts"), 1)
                dve.tensor_tensor(view(SCR, m0, [[MSG, VB], [1, C]]), view(G, g0, [[D, VB], [1, C]]), view(PS, w0, [[P, VB], [1, C]]), ALU.mult)
                dve.tensor_tensor(view(SCR, m0 + 64, [[MSG, VB], [64, 3], [1, C]]), view(G, g0 + C, [[D, VB], [C, 3], [1, C]]),
                                  view(PS, w0 + C, [[P, VB], [0, 3], [1, C]]), ALU.mult)
                dve.wait_ge(s("conv_parts"), k + 1)
                dve.tensor_tensor(view(SCR, m0 + 96, [[MSG, VB], [64, 3], [1, C]]), view(SCR, C_AT, [[C, VB], [0, 3], [1, C]]),
                                  y([[1, VB], [NV + 1, 3], [0, C]]), ALU.mult)
                dve.tensor_reduce(view(SCR, U_AT, [[C, VB], [1, C]]), view(SCR, T_AT, [[96, VB], [1, C], [C, 3]]), AX, ALU.add).then_inc(s("conv_dot"), 1)
                dve.wait_ge(s("conv_dot"), k + 1)
                dve.scalar_tensor_tensor(view(SCR, m0 + C, [[MSG, VB], [1, C]]), view(SCR, U_AT, [[C, VB], [1, C]]), INV_SQRT3,
                                         view(PS, w0 + 96, [[P, VB], [1, C]]), ALU.mult, ALU.mult).then_inc(s("messages_ready"), 1)
                if late(k, 1):
                    add_up(k - 1)

            def add_up(k):
                word = dve.value_load(block_words[0:1, bass.ds(k, 1)])
                dve.wait_ge(s("message_sums"), VB * (k + 1))
                for q in range(VB):
                    acc = view(RX, ((word >> (5 * q)) & 31) * MSG, [[1, MSG]])
                    if late(k, 1) or q:
                        dve.wait_ge(s("added"), VB * k + q)
                    dve.tensor_tensor(acc, acc, PS[:, q, 0:MSG], ALU.add).then_inc(s("added"), 1)
            pairs(dve, message)
            add_up(NB - 1)
            dve.wait_ge(s("added"), NV)
            dve.memset(small[:, 7, :], 0.0).then_inc(s("messages_summed"), 1)

            for b in range(NBLK):
                dve.wait_ge(s("update_made"), b + 1)
                dve.tensor_scalar(view(SCR, b * OUTW, [[1, OUTW]]), PS[:, 4 + b % 2, 0:OUTW], 0.5 * 32.0 ** -0.5, None, ALU.mult).then_inc(s("update_copied"), 1)
            dve.wait_ge(s("update_copied"), NBLK)
            dve.memset(small[:, 7, :], 0.0).then_inc(s("update_ready"), 1)
            dve.wait_ge(s("gates_ready"), 1)
            for i3 in range(3):
                ins = dve.tensor_tensor(view(SCR, 64 + 32 * i3, [[OUTW, NBLK], [1, 32]]), view(SCR, 64 + 32 * i3, [[OUTW, NBLK], [1, 32]]),
                                        view(SCR, 32, [[OUTW, NBLK], [1, 32]]), ALU.mult)
            done(ins)
            dve.tensor_tensor(X[:, :, 0:32], X[:, :, 0:32], view(SCR, 0, [[OUTW, NBLK], [1, 32]]), ALU.add)
            xv = view(X, 32, [[D, NBLK], [3, 32], [1, 3]])
            dve.tensor_tensor(xv, xv, view(SCR, 64, [[OUTW, NBLK], [1, 32], [32, 3]]), ALU.add).then_inc(s("result_ready"), 1)

        @block.tensor
        def _(pe):
            def turn_h(n):
                pe.wait_ge(s("h_ready"), n + 1)
                for b in range(NBLK):
                    ins = pe.transpose(PS[:, b // 4, (b % 4) * P:(b % 4 + 1) * P], H[:, b, :], ident[:])
                    if b % 4 == 3 or b == NBLK - 1:
                        ins.then_inc(s("h_turned"), 1)

            pe.wait_ge(s("ends_ready"), 1)
            pe.wait_ge(s("ones_made"), 2)
            pe.matmul(PS[:, 0, 0:NT], ones_row[:], rowf[:, 0:NT], start=True, stop=True).then_inc(s("ends_spread"), 1)
            pe.wait_ge(s("blocks_ready"), 1)
            pe.wait_ge(s("ident_made"), 1)
            pe.transpose(PS[0:4, 1, 0:P], tv[:, 4, :], ident[:]).then_inc(s("blocks_in_psum"), 1)
            pe.wait_ge(s("blocks_turned"), 1)
            for f in range(N_FILL):
                g, j = divmod(f, 9)
                if j == 0:
                    pe.wait_ge(s("kinds_ready"), g + 1)
                if j == 2:
                    pe.wait_ge(s(f"attrs_in{g}"), 16)
                if f >= 6:
                    o = f - 6
                    pe.wait_ge(s("fill_copied_act" if o % 2 else "fill_copied_dve"), o // 2 + 1)
                n = 4 if j != 1 else 1
                for i in range(n):
                    if j < 2:
                        src = view(RX, (5 * g + 4 * j + i) * P, [[1, P]])
                    else:
                        src = view(SCR, (g % 2) * N_ATTR * P + (4 * (j - 2) + i) * P, [[1, P]])
                    ins = pe.transpose(PS[:, 2 + f % 6, i * P:(i + 1) * P], src, ident[:])
                ins.then_inc(s("fill_turned"), 1)

            for i in range(LAYERS):
                name = passes[i]
                r0 = 12 - CH * i
                pe.wait_ge(s("sums_zeroed"), i + 1)

                def scatter(k, p, m):
                    word = pe.value_load(block_words[0:1, bass.ds(k, 1)])
                    pe.wait_ge(s(f"{name}_hot"), k + 1)
                    pe.wait_ge(s(f"{name}_gathered{p}"), 16 * VB * (m + 1))
                    for q in range(VB):
                        b = (word >> (5 * q)) & 31
                        pe.matmul(PSF[:, bass.ds(b * P, P)], OH[:, p, q, :], G[:, p, q, :], start=False, stop=False, skip_group_check=True)
                        pe.matmul(PSF[:, bass.ds(b * CH + DST_SUM, CH)], OH[:, p, q, :],
                                  view(AT, r0 * (NV + 1) + VB * k + q, [[NV + 1, CH]]), start=False, stop=False, skip_group_check=True)
                        ins = pe.matmul(PSF[:, SRC_SUM:SRC_SUM + CH * NBLK], view(SCR, p * VB * P + q * P, [[1, P]]),
                                        view(SCR, PR_AT + p * VB * NBLK * 7 + VB * NBLK + q * NBLK * CH, [[1, NBLK * CH]]),
                                        start=False, stop=False, skip_group_check=True)
                    ins.then_inc(s(f"{name}_rows_used"), 1)
                pairs(pe, scatter)

            turn_h(0)
            pe.wait_ge(s("means_ready"), 1)
            pe.wait_ge(s("ht_ready"), 7)
            for g in range(7):
                w = min(4, NBLK - 4 * g)
                if g >= 2:
                    pe.wait_ge(s("mt_ready"), g - 1)
                for b in range(w):
                    ins = pe.transpose(PS[0:32, g % 2, b * P:(b + 1) * P], means[:, 4 * g + b, :], ident[:])
                ins.then_inc(s("means_turned"), 1)
            pe.wait_ge(s("weights_loaded"), W_ALL)
            for g in range(7):
                w = min(4, NBLK - 4 * g) * P
                pe.wait_ge(s("mt_ready"), g + 1)
                if g >= 2:
                    pe.wait_ge(s("hidden_biased"), g - 1)
                pe.matmul(PS[:, 2 + g % 2, 0:w], w1a_s[:], HTF[:, g * 512:g * 512 + w], start=True, stop=False)
                pe.matmul(PS[:, 2 + g % 2, 0:w], w1b_s[:], view(SCR, g * 512, [[1, w]], 32), start=False, stop=True).then_inc(s("hidden_made"), 1)
            for g in range(7):
                w = min(4, NBLK - 4 * g)
                pe.wait_ge(s("hidden_ready"), g + 1)
                if g >= 2:
                    pe.wait_ge(s("mlp_added"), g - 1)
                for b in range(w):
                    ins = pe.matmul(PS[:, 4 + g % 2, b * P:(b + 1) * P], hid[:, (4 * g + b) * P:(4 * g + b + 1) * P], w2_s[:], start=True, stop=True)
                ins.then_inc(s("mlp_made"), 1)

            turn_h(1)
            pe.wait_ge(s("ht_ready"), 14)
            for g in range(13):
                if g >= 4:
                    pe.wait_ge(s("lr_copied"), g - 3)
                for b in range(min(2, NBLK - 2 * g)):
                    ins = pe.matmul(PS[:, g % 4, b * 256:(b + 1) * 256], HTF[:, (2 * g + b) * P:(2 * g + b + 1) * P], wlr_s[:], start=True, stop=True)
                ins.then_inc(s("lr_made"), 1)
            pe.wait_ge(s("xr_ready"), 1)

            def score(k, p, m):
                pe.wait_ge(s("score_hot"), k + 1)
                if late(k, 2):
                    pe.wait_ge(s("ot_ready"), k - 1)
                for q in range(VB):
                    ins = pe.transpose(view(PS, p * 1024 + q * P, [[1, P]]), OH[:, p, q, :], ident[:])
                ins.then_inc(s("oh_turned"), 1)
                pe.wait_ge(s("radial_ready"), k + 1)
                if late(k, 1):
                    pe.wait_ge(s("radial_hidden_ready"), k)
                gate(pe)
                pe.transpose(PS[0:8 * VB, 7, 0:P], view(SCR, RS_AT, [[1, 8 * VB]]), ident[:]).then_inc(s("radial_turned"), 1)
                if late(k, 1):
                    add_lr(k - 1, 1 - p, m if p == 1 else m - 1)
                pe.wait_ge(s("radial_t_ready"), k + 1)
                gate(pe)
                pe.matmul(PS[0:8 * VB, 7, 256:256 + P], wr1_s[:], view(SCR, RT_AT, [[1, P]], 8 * VB), start=True, stop=True).then_inc(s("hidden_pre_made"), 1)

            def add_lr(k, p, m):
                word = pe.value_load(block_words[0:1, bass.ds(k, 1)])
                pe.wait_ge(s("ot_ready"), k + 1)
                pe.wait_ge(s(f"score_gathered{p}"), 16 * VB * (m + 1))
                if late(k, 1):
                    pe.wait_ge(s("z_copied"), 2 * k)
                for q in range(VB):
                    b = (word >> (5 * q)) & 31
                    zq = 4 * 512 + 256 * q
                    pe.matmul(view(PS, zq, [[1, XR_W]]), view(SCR, OT_AT + (p * VB + q) * P, [[1, P]]),
                              view(RX, b * XR_W, [[1, XR_W]]), start=True, stop=False)
                    ins = pe.matmul(view(PS, zq, [[1, D]]), ident[:], G[:, p, q, :], start=False, stop=True)
                ins.then_inc(s("z_made"), 1)
            pairs(pe, score)
            add_lr(NB - 1, 0, (NB - 1) // 2)

            pe.wait_ge(s("scored"), NB)
            pe.wait_ge(s("z_copied"), 2 * NB)
            for g in range(VG):
                for h in range(HEADS):
                    ins = pe.transpose(view(PS, g * 512 + h * P, [[1, P]], WG[g]), view(HT, g * P * HEADS + h, [[HEADS, WG[g]]]), ident[:])
            ins.then_inc(s("scores_turned"), 1)
            pe.wait_ge(s("ends_made"), 1)
            for i in range(4):
                for g in range(VG):
                    ins = pe.transpose(PS[0:4, i, g * P:(g + 1) * P], view(HT, END_AT + (i * VG + g) * 4, [[1, 4]]), ident[:])
            ins.then_inc(s("ends_turned"), 1)
            pe.wait_ge(s("carries_ready"), 1)
            for i in range(2):
                for g in range(VG):
                    ins = pe.transpose(PS[:, 4, i * 16 + g * 4:i * 16 + g * 4 + 4], view(H, i * VW + g * P, [[1, P]], 4), ident[0:4, 0:4])
            ins.then_inc(s("carries_turned"), 1)
            pe.wait_ge(s("maxima_ready"), 1)
            for g in range(VG):
                for h in range(HEADS):
                    ins = pe.transpose(view(PS, g * 512 + h * P, [[1, WG[g]]]), view(SCR, VG * HEADS * P + 1 + (g * HEADS + h) * P, [[1, P]], WG[g]), ident[0:WG[g], 0:WG[g]])
            ins.then_inc(s("maxima_turned"), 1)

            pe.wait_ge(s("sums_zeroed"), LAYERS + 1)
            pe.wait_ge(s("probs_ready"), 1)

            def weighted(k, p, m):
                word = pe.value_load(block_words[0:1, bass.ds(k, 1)])
                pe.wait_ge(s("sum_hot"), k + 1)
                for q in range(VB):
                    b = (word >> (5 * q)) & 31
                    pe.matmul(PSF[:, bass.ds(b * P, P)], OH[:, p, q, :], G[:, p, q, :], start=False, stop=False, skip_group_check=True)
                    ins = pe.matmul(PSF[:, bass.ds(b * 8 + DST_SUM, 8)], OH[:, p, q, :],
                                    view(RX, 8 * (VB * k + q), [[1, 8]]), start=False, stop=False, skip_group_check=True)
                ins.then_inc(s("sum_done"), 1)
            pairs(pe, weighted)

            turn_h(2)
            for b in range(NBLK):
                if b % 4 == 0:
                    pe.wait_ge(s("ht_ready"), 14 + b // 4 + 1)
                ins = pe.matmul(PS[:, b // 4, (b % 4) * P:(b % 4 + 1) * P], HTF[:, b * P:(b + 1) * P], wup_s[:], start=True, stop=True)
                if b % 4 == 3 or b == NBLK - 1:
                    ins.then_inc(s("up_made"), 1)
            pe.wait_ge(s("up_copied"), 7)

            def conv(k, p, m):
                pe.wait_ge(s(f"hidden_back{p}"), 16 * (m + 1))
                if late(k, 1):
                    pe.wait_ge(s("messages_ready"), k)
                for q in range(VB):
                    ins = pe.matmul(view(PS, 5 * 512 + q * P, [[1, P]]), view(SCR, CH_AT + p * P, [[1, P]], 8 * VB), wr2_s[:, q, :], start=True, stop=True)
                ins.then_inc(s("conv_weights_made"), 1)
                if late(k, 1):
                    sums(k - 1, 1 - p)

            def sums(k, p):
                pe.wait_ge(s("messages_ready"), k + 1)
                if late(k, 1):
                    pe.wait_ge(s("added"), VB * k)
                for q in range(VB):
                    ins = pe.matmul(PS[:, q, 0:MSG], OH[:, p, q, :], view(SCR, M_AT + (p * VB + q) * MSG, [[1, MSG]]), start=True, stop=True)
                    ins.then_inc(s("message_sums"), 1)
            pairs(pe, conv)
            sums(NB - 1, 0)

            def update(b):
                pe.wait_ge(s("final_copied"), b + 1)
                if b >= 2:
                    pe.wait_ge(s("update_copied"), b - 1)
                ps = PS[:, 4 + b % 2, :]
                sums_t = lambda j: view(SCR, AC_AT + (b % 2) * 256 + j * P, [[1, P]])
                spread_t = lambda j: view(SCR, ST_AT + (b % 2) * 512 + j * P, [[1, P]])
                pe.matmul(ps[:, 0:96], sums_t(0), wdna_s[:], start=True, stop=False, skip_group_check=True)
                pe.matmul(ps[:, 96:160], sums_t(1), wdnb_s[:], start=False, stop=False, skip_group_check=True)
                pe.matmul(ps[:, 0:64], spread_t(0), wsk_s[:, 0:64], start=False, stop=False, skip_group_check=True)
                for i3 in range(3):
                    ins = pe.matmul(ps[:, 64 + 32 * i3:96 + 32 * i3], spread_t(i3 + 1), wsk_s[:, 64:96], start=False,
                                    stop=i3 == 2, skip_group_check=True)
                ins.then_inc(s("update_made"), 1)

            pe.wait_ge(s("messages_summed"), 1)
            for b in range(NBLK):
                if b >= 2:
                    pe.wait_ge(s("final_copied"), b - 1)
                for j in range(2):
                    ins = pe.transpose(PS[:, b % 2, j * P:(j + 1) * P], view(RX, b * MSG + j * P, [[1, P]]), ident[:])
                ins.then_inc(s("acc_turned"), 1)
                pe.wait_ge(s("spread"), b + 1)
                for j in range(4):
                    ins = pe.transpose(PS[:, 2 + b % 2, j * P:(j + 1) * P], view(SCR, SP_AT + (b % 2) * 512 + j * P, [[1, P]]), ident[:])
                ins.then_inc(s("spread_turned"), 1)
                if b >= 1:
                    update(b - 1)
            update(NBLK - 1)


def kernel(x, src, dst, edge_attr_16, edge_attr_4, edge_attr_8, node_type_4, L1_gnn_W1, L1_gnn_b1, L1_gnn_W2, L1_gnn_b2,
           L2_gnn_W_l, L2_gnn_b_l, L2_gnn_W_r, L2_gnn_b_r, L2_gnn_att, L2_gnn_bias, L3_gnn_W_up_s, L3_gnn_W_up_v,
           L3_gnn_W_r1, L3_gnn_W_r2, L3_gnn_W_dn_s, L3_gnn_W_dn_v, L3_gnn_W_sk_s, L3_gnn_W_sk_v):
    import numpy as np
    import concourse.bacc as bacc
    from concourse.bass_utils import run_bass_kernel_spmd

    a = lambda t: np.ascontiguousarray(np.asarray(t))
    f32, i32 = np.float32, np.int32
    ids = np.full((3, NT * P), NPAD - 1, i32)
    ids[0, :EDGES], ids[1, :EDGES] = a(src), a(dst)
    ids[2, 1:], ids[2, 0] = ids[1, :-1], -1
    attrs = np.zeros((NT * P, N_ATTR), f32)
    attrs[:EDGES] = np.concatenate([a(edge_attr_16), a(edge_attr_4), a(edge_attr_8)], 1)
    types = np.zeros((NPAD,), i32)
    types[:NODES] = a(node_type_4)

    up = np.zeros((D, D), f32)
    up[0:32, 0:32] = a(L3_gnn_W_up_s)
    for i in range(3):
        up[32 + i::3, 32 + 32 * i:64 + 32 * i] = a(L3_gnn_W_up_v)
    wr1 = np.zeros((8, VB, VB, 8), f32)
    wr2 = np.zeros((VB, 8, VB, P), f32)
    for q in range(VB):
        wr1[:, q, q, :] = a(L3_gnn_W_r1)
        wr2[q, :, q, :] = a(L3_gnn_W_r2)
    dn_a, dn_b = np.zeros((P, 96), f32), np.zeros((P, 64), f32)
    dn_a[0:64, 0:64] = a(L3_gnn_W_dn_s)
    dn_a[64:128, 64:96] = dn_b[0:64, 0:32] = dn_b[64:128, 32:64] = a(L3_gnn_W_dn_v)
    arrays = {
        "x": a(x),
        "edge_ids": a(ids.reshape(3, NT, P).transpose(1, 0, 2).reshape(NT, 3 * P)),
        "last_dst": a(ids[1, P - 1::P].reshape(1, NT)),
        "edge_attrs": a(attrs.reshape(NT, P, N_ATTR).transpose(0, 2, 1).reshape(NT, N_ATTR * P)),
        "species": a(types.reshape(NBLK, P).T),
        "w1a": a(L1_gnn_W1)[0:D], "w1b": a(a(L1_gnn_W1)[D:D + 32]), "b1": a(L1_gnn_b1).reshape(D, 1), "w2": a(L1_gnn_W2),
        "row_params": np.concatenate([a(L1_gnn_b2), a(L2_gnn_att).reshape(-1), a(L2_gnn_bias), a(L2_gnn_b_l), a(L2_gnn_b_r)]),
        "wlr": a(np.concatenate([a(L2_gnn_W_l).T, a(L2_gnn_W_r).T], 1)),
        "wup": up, "wr1": wr1.reshape(8 * VB, 8 * VB), "wr2": wr2.reshape(8 * VB, VB, P), "wdn_a": dn_a, "wdn_b": dn_b,
        "wsk": a(np.concatenate([a(L3_gnn_W_sk_s).reshape(P, 64), a(L3_gnn_W_sk_v).reshape(P, 32)], 1)),
    }
    nc = bacc.Bacc("TRN2", target_bir_lowering=False, num_devices=1)
    handles = [nc.dram_tensor(f"in_{n}", v.shape, mybir.dt.from_np(v.dtype), kind="ExternalInput").ap() for n, v in arrays.items()]
    handles.append(nc.dram_tensor("out", (NODES, D), F32, kind="ExternalOutput").ap())
    gnn_program(nc, *handles)
    r = run_bass_kernel_spmd(nc, [{f"in_{n}": v for n, v in arrays.items()}], core_ids=[0])
    return r.results[0]["out"]
```

```python
from contextlib import ExitStack

import concourse.bass as bass
from concourse import mybir

F32 = mybir.dt.float32
BF16 = mybir.dt.bfloat16
I32 = mybir.dt.int32
ALU = mybir.AluOpType
ACT = mybir.ActivationFunctionType
AX = mybir.AxisListType.X

P = 128
NODES, D = 3125, 128
EDGES = 50000
NBLK = -(-NODES // P)
NPAD = NBLK * P
NT = -(-EDGES // P)
NV = NT + NBLK - 1
VB = 5
NB = NV // VB
DEPTH = 3
PEEL = 5
LAST = ((NB - 1) % DEPTH, (NB - 1) // DEPTH)
VG = -(-NV // P)
VW = VG * P
WG = [min(P, NV - g * P) for g in range(VG)]
HEADS, C = 4, 32
N_ATTR = 16 + 4 + 8
LAYERS = 3
CH = 6
ROWS = 18 + 4 + 8
SH, RAD = 18, 22
BIG = 1.0e30
LN_EPS = 1e-5
INV_SQRT3 = 0.5773502691896258
MSG = 256
SUM_SCALE = 16.0 ** -0.5 * 8.0 ** -0.5 * 64.0 ** -0.5 * 32.0 ** 0.5
OUTW = 160
SRC_SUM = NPAD
DST_SUM = 7 * 512
assert NB * VB == NV and (NB - PEEL) % DEPTH == 0 and SRC_SUM + CH * NBLK <= DST_SUM


def gnn_program(nc, x, edge_ids, last_dst, edge_attrs, species, w1a, w1b, b1, w2, row_params, wlr, wup,
                wr1, wr2, wdn_a, wdn_b, wsk, out):
    ctx = ExitStack()
    with ctx:
        def sb(name, shape, dt=F32):
            return ctx.enter_context(nc.sbuf_tensor(name, shape, dt))

        def sem(name):
            return ctx.enter_context(nc.semaphore(name))

        def dram(name, shape, dt=F32):
            return nc.dram_tensor(name, shape, dt).ap()

        tables = [dram(f"table{i}", [NPAD, D]) for i in range(LAYERS + 2)]
        gathered_rows = dram("gathered_rows", [NB, P, VB * D])
        radial_hidden = dram("radial_hidden", [NB, 8 * VB, P])
        block_of_visit = dram("block_of_visit", [VG, P], I32)

        X = sb("X", [P, NBLK, D])
        H = sb("H", [P, NBLK, D])
        HT_AT = NV * 8 + NPAD + 136
        RX = sb("RX", [P, HT_AT + 2 * NV * HEADS + 80])
        HT = (RX, HT_AT)
        SCR = sb("SCR", [P, 7680])
        AT = sb("AT", [P, ROWS, NV + 1])
        EI = sb("EI", [P, 5, VW])
        G = sb("G", [P, DEPTH, VB, D])
        OH = sb("OH", [P, DEPTH, VB, P])
        dst_rows = sb("dst_rows", [P, VG, 3, P])
        invalid_neg = sb("invalid_neg", [P, VG, P])
        src_idx = sb("src_idx", [P, NV + 1], I32)
        gather_idx = sb("gather_idx", [P, DEPTH, VB], I32)
        block_words = sb("block_words", [1, NB], I32)
        ident = sb("ident", [P, P])
        ident_b = sb("ident_b", [P, P], BF16)
        iota_i = sb("iota_i", [P, P], I32)
        iota = sb("iota", [P, P])
        small = sb("small", [P, 8, NBLK])
        inv_deg = sb("inv_deg", [P, 2, NBLK])
        no_edges = sb("no_edges", [P, NBLK])
        self_score = sb("self_score", [P, NBLK, HEADS])
        node_max = sb("node_max", [P, NBLK, HEADS])
        self_prob = sb("self_prob", [P, NBLK, HEADS])
        means = sb("means", [P, NBLK, 32])
        tv = sb("tv", [P, 6, VG])
        tvi = sb("tvi", [P, VG], I32)
        vrow = sb("vrow", [4, P], I32)
        rowi = sb("rowi", [1, 2 * NT + 600], I32)
        rowf = sb("rowf", [1, 2 * NT])
        ones_row = sb("ones_row", [1, P])
        w1a_s, w2_s, wup_s = (sb(n, [P, D]) for n in ("w1a_s", "w2_s", "wup_s"))
        w1b_s = sb("w1b_s", [32, D])
        b1_s = sb("b1_s", [P, 1])
        rows_s = sb("rows_s", [P, 5 * D])
        wlr_s = sb("wlr_s", [P, 2 * D])
        wr1_s = sb("wr1_s", [8 * VB, 8 * VB])
        wr2_s = sb("wr2_s", [8 * VB, VB, P])
        wdna_s, wdnb_s = sb("wdna_s", [P, 96]), sb("wdnb_s", [P, 64])
        wsk_s = sb("wsk_s", [P, 96])
        spec_s = sb("spec_s", [P, NBLK], I32)
        spec_f = sb("spec_f", [P, NBLK])
        smask = sb("smask", [P, NBLK, 4])
        PS = ctx.enter_context(nc.psum_tensor("PS", [P, 8, 512], F32))
        PSF = PS[:, :, :].rearrange("p a b -> p (a b)")

        def view(t, offset, dims, parts=P, dt=None):
            t, at = t if isinstance(t, tuple) else (t, 0)
            width = 1
            for n in t.shape[1:]:
                width *= n
            return bass.AP(t, offset + at, [[width, parts]] + [list(d) for d in dims])

        RES = view(RX, 0, [[D, NBLK], [1, D]])
        XR_W = D + HEADS
        XR = view(RX, 0, [[XR_W, NBLK], [1, XR_W]])
        PM = view(RX, 0, [[8, NV], [1, 8]])
        XL_AT = NV * 8 + 8
        XL = view(RX, XL_AT, [[D, NBLK], [1, D]])
        ACC = view(RX, 0, [[MSG, NBLK], [1, MSG]])
        HTF = view(HT, 0, [[1, NPAD]])
        ES = view(HT, 0, [[HEADS, NV], [1, HEADS]])
        MS_AT = NV * HEADS
        MS = view(HT, MS_AT, [[HEADS, NV], [1, HEADS]])
        hid = view(RX, 0, [[1, NPAD]])
        bias2 = rows_s[:, 0:D]
        att = rows_s[:, D:2 * D]
        gat_bias = rows_s[:, 2 * D:3 * D]
        attr_rows = view(SCR, 0, [[N_ATTR * P, 2], [1, N_ATTR * P]])

        def id_rows(g):
            return view(HT, g * 3 * P, [[1, 3 * P]]).bitcast(I32)

        N_FILL = 9 * VG

        def fill_copy(f):
            g, j = divmod(f, 9)
            n = 1 if j == 1 else 4
            if j < 2:
                w = P
                dst = view(EI, 4 * j * VW + g * P, [[VW, n], [1, w]])
            else:
                w = min(P, NV + 1 - g * P)
                row = (0, 4, 8, 12, SH, RAD, RAD + 4)[j - 2]
                dst = view(AT, row * (NV + 1) + g * P, [[NV + 1, n], [1, w]])
            return dst, view(PS, (2 + f % 6) * 512, [[P, n], [1, w]])
        def OHS(p):
            return view(SCR, p * VB * P, [[P, VB], [1, P]])

        PR_AT = DEPTH * VB * P

        def OHB(p):
            return OH[:, p].rearrange("p a b -> p (a b)").bitcast(BF16)[:, 0:VB * P].rearrange("p (a b) -> p a b", a=VB)

        def ot_ps(p):
            return PS[:, p, :].bitcast(BF16)[:, 0:VB * P]

        OT_AT = 0
        Z_AT = DEPTH * VB * P
        L_AT = Z_AT + DEPTH * VB * D
        RS_AT = L_AT + VB * D
        RT_AT = RS_AT + 8 * VB
        RH_AT = RT_AT + P
        END_AT = 2 * NV * HEADS
        M_AT = 0
        C_AT = DEPTH * VB * MSG
        T_AT = C_AT + VB * C
        U_AT = T_AT + 3 * VB * C
        CH_AT = U_AT + VB * C
        W_AT = CH_AT + DEPTH * P
        AC_AT = NBLK * OUTW
        ST_AT = AC_AT + 512
        SP_AT = ST_AT + 1024

        def bc(ap_tensor, offset, dims, parts=P):
            return view(ap_tensor, offset, dims, parts)

        S = {}

        def s(name):
            if name not in S:
                S[name] = sem(name)
            return S[name]

        block = ctx.enter_context(nc.Block())

        def batches(eng, body):
            for k in range(PEEL):
                body(k, k % DEPTH, k // DEPTH)
            with eng.Fori(1, (NB - PEEL) // DEPTH + 1) as j:
                for i in range(DEPTH):
                    k0 = PEEL - DEPTH + i
                    body(DEPTH * j + k0, k0 % DEPTH, j + k0 // DEPTH)

        uses = lambda p: (NB - 1 - p) // DEPTH + 1

        def before(p, m):
            return (p - 1, m) if p else (DEPTH - 1, m - 1)

        def late(k, n):
            return not (isinstance(k, int) and k < n)

        def gate(eng):
            eng.sem_inc(s("gates_passed"))

        def load_all(eng):
            for t, a in ((w1a_s, w1a), (w1b_s, w1b), (b1_s, b1), (w2_s, w2), (wlr_s, wlr), (wup_s, wup),
                         (wr1_s, wr1), (wr2_s, wr2), (wdna_s, wdn_a), (wdnb_s, wdn_b), (wsk_s, wsk), (spec_s, species)):
                eng.dma_start(t[:], a).then_inc(s("weights_loaded"), 16)
            eng.dma_start(rows_s[:], row_params.partition_broadcast(P)).then_inc(s("weights_loaded"), 16)

        W_ALL = 13 * 16
        passes = ["sage0", "sage1", "sage2", "score", "conv"]

        @block.sync
        def _(sp):
            sp.dma_start(rowi[:, 0:NT], last_dst).then_inc(s("last_loaded"), 16)
            sp.wait_ge(s("x_tail_zeroed"), 1)
            sp.dma_start(X[:, 0:NBLK - 1, :], x[0:(NBLK - 1) * P, :].rearrange("(b p) d -> p b d", p=P)).then_inc(s("x_loaded"), 16)
            sp.dma_start(X[0:NODES - (NBLK - 1) * P, NBLK - 1, :], x[(NBLK - 1) * P:NODES, :]).then_inc(s("x_loaded"), 16)
            sp.wait_ge(s("blocks_turned"), 1)
            sp.dma_start(block_of_visit, vrow[:, 0:P]).then_inc(s("blocks_out"), 16)
            sp.wait_ge(s("blocks_out"), 16)
            sp.dma_start(rowi[:, 2 * NT:2 * NT + VW], block_of_visit.rearrange("g v -> (g v)").rearrange("(o n) -> o n", o=1)).then_inc(s("blocks_in"), 16)
            for i in range(LAYERS + 2):
                src = [H[:], H[:], H[:], XL, XL][i]
                sp.wait_ge(s("table_ready"), i + 1)
                sp.dma_start(tables[i].rearrange("(b p) d -> p b d", p=P), src).then_inc(s("table_written"), 16)
                if i == LAYERS:
                    def store(k, p, m):
                        sp.wait_ge(s(f"score_gathered{p}"), 16 * VB * (m + 1))
                        sp.dma_start(gathered_rows[bass.ds(k, 1)].rearrange("o p n -> p (o n)"),
                                     G[:, p].rearrange("p a b -> p (a b)")).then_inc(s(f"rows_stored{p}"), 16)
                        sp.wait_ge(s("radial_hidden_ready"), k + 1)
                        sp.dma_start(radial_hidden[bass.ds(k, 1)].rearrange("o p n -> p (o n)"),
                                     bc(SCR, RH_AT + p * P, [[1, P]], 8 * VB)).then_inc(s(f"hidden_stored{p}"), 16)
                    batches(sp, store)
                    for p in range(DEPTH):
                        n = uses(p)
                        sp.wait_ge(s(f"rows_stored{p}"), 16 * n)
                        sp.wait_ge(s(f"hidden_stored{p}"), 16 * n)

                    def load(k, p, m):
                        if late(k, DEPTH):
                            sp.wait_ge(s("sum_done"), k - DEPTH + 1)
                        else:
                            sp.wait_ge(s("z_read"), NB)
                        sp.dma_start(G[:, p].rearrange("p a b -> p (a b)"),
                                     gathered_rows[bass.ds(k, 1)].rearrange("o p n -> p (o n)")).then_inc(s(f"rows_back{p}"), 16)
                    batches(sp, load)
                if i == LAYERS + 1:
                    def load_hidden(k, p, m):
                        if late(k, DEPTH):
                            sp.wait_ge(s("conv_weights_made"), k - DEPTH + 1)
                        sp.dma_start(bc(SCR, CH_AT + p * P, [[1, P]], 8 * VB),
                                     radial_hidden[bass.ds(k, 1)].rearrange("o p n -> p (o n)")).then_inc(s(f"hidden_back{p}"), 16)
                    batches(sp, load_hidden)
            sp.wait_ge(s("result_ready"), 1)
            sp.dma_start(out[0:(NBLK - 1) * P, :].rearrange("(b p) d -> p b d", p=P), X[:, 0:NBLK - 1, :]).then_inc(s("out_written"), 16)
            sp.dma_start(out[(NBLK - 1) * P:NODES, :], X[0:NODES - (NBLK - 1) * P, NBLK - 1, :]).then_inc(s("out_written"), 16)
            sp.wait_ge(s("out_written"), 32)
            sp.wait_ge(s("table_written"), 16 * (LAYERS + 2))

        @block.gpsimd
        def _(pool):
            pool.memset(X[:, NBLK - 1, :], 0.0).then_inc(s("x_tail_zeroed"), 1)
            pool.iota(iota_i[:], pattern=[[1, P]], base=0, channel_multiplier=0).then_inc(s("iota_made"), 1)
            pool.iota(tvi[:], pattern=[[P, VG]], base=0, channel_multiplier=1).then_inc(s("iota_made"), 1)
            pool.iota(rowi[:, NT:2 * NT], pattern=[[1, NT]], base=0, channel_multiplier=0).then_inc(s("iota_made"), 1)
            pool.memset(ident[:], 0.0).then_inc(s("ident_zeroed"), 1)
            pool.memset(ones_row[:], 1.0).then_inc(s("ones_made"), 1)
            pool.memset(AT[:, 16:18, :], 1.0).then_inc(s("ones_made"), 1)
            pool.wait_ge(s("ident_zeroed"), 1)
            pool.affine_select(out=ident[:], in_=ident[:], compare_op=ALU.not_equal, fill=1.0, base=0,
                               pattern=[[-1, P]], channel_multiplier=1).then_inc(s("ident_made"), 1)
            pool.wait_ge(s("tiles_found"), 1)
            for g in range(VG):
                at = bass.IndirectOffsetOnAxis(ap=tvi[:, g:g + 1], axis=0)
                pool.indirect_dma_start(id_rows(g), None, edge_ids, at).then_inc(s(f"ids_in{g}"), 16)
            for g in range(VG):
                at = bass.IndirectOffsetOnAxis(ap=tvi[:, g:g + 1], axis=0)
                if g >= 2:
                    pool.wait_ge(s("fill_turned"), 9 * (g - 1))
                pool.indirect_dma_start(view(SCR, (g % 2) * N_ATTR * P, [[1, N_ATTR * P]]), None, edge_attrs, at).then_inc(s(f"attrs_in{g}"), 16)

            for i, name in enumerate(passes):
                pool.wait_ge(s("table_written"), 16 * (i + 1))

                def gather(k, p, m):
                    pool.wait_ge(s(f"{name}_idx_ready"), k + 1)
                    gate(pool)
                    if late(k, DEPTH):
                        pool.wait_ge(s({"score": "z_read", "conv": "messages_ready"}.get(name, f"{name}_rows_used")), k - DEPTH + 1)
                        gate(pool)
                        if name == "score":
                            pool.wait_ge(s(f"rows_stored{p}"), 16 * m)
                            gate(pool)
                    for q in range(VB):
                        pool.indirect_dma_start(G[:, p, q, :], None, tables[i],
                                                bass.IndirectOffsetOnAxis(ap=gather_idx[:, p, q:q + 1], axis=0)
                                                ).then_inc(s(f"{name}_gathered{p}"), 16)
                batches(pool, gather)

            pool.wait_ge(s("messages_summed"), 1)
            for b in range(NBLK):
                if b >= 2:
                    pool.wait_ge(s("spread_turned"), b - 1)
                h0 = b * D
                pool.tensor_tensor(view(SCR, SP_AT + (b % 2) * 512, [[32, 4], [1, 32]]),
                                   view(H, h0, [[0, 4], [1, 32]]), view(smask, 4 * b, [[1, 4], [0, 32]]), ALU.mult)
                for i3 in range(3):
                    ins = pool.tensor_tensor(view(SCR, SP_AT + (b % 2) * 512 + 128 * (i3 + 1), [[32, 4], [1, 32]]),
                                             view(H, h0 + 32 + i3, [[0, 4], [3, 32]]), view(smask, 4 * b, [[1, 4], [0, 32]]), ALU.mult)
                ins.then_inc(s("spread"), 1)

        @block.scalar
        def _(act):
            load_all(act)

            def norm_part(n):
                act.wait_ge(s("centred"), n + 1)
                act.activation(XL, H[:], ACT.Square).then_inc(s("squared"), 1)
                act.wait_ge(s("var_ready"), n + 1)
                act.activation(small[:, 4, :], small[:, 3, :], ACT.Sqrt).then_inc(s("std_ready"), 1)

            def copy_idx(name, k, p, m):
                if late(k, DEPTH):
                    act.wait_ge(s(f"{name}_gathered{p}"), 16 * VB * m)
                    gate(act)
                act.copy(gather_idx[:, p, :], src_idx[:, bass.ds(VB * k, VB)]).then_inc(s(f"{name}_idx_ready"), 1)

            def turned_h(n):
                for g in range(7):
                    w = min(4, NBLK - 4 * g) * P
                    act.wait_ge(s("h_turned"), 7 * n + g + 1)
                    act.copy(HTF[:, g * 512:g * 512 + w], PSF[:, g * 512:g * 512 + w]).then_inc(s("ht_ready"), 1)

            norm_part(0)
            for f in range(1, N_FILL, 2):
                act.wait_ge(s("fill_turned"), f + 1)
                dst, src = fill_copy(f)
                act.copy(dst, src).then_inc(s("fill_copied_act"), 1)

            act.wait_ge(s("idx_made"), 1)
            for i, name in enumerate(passes[:LAYERS]):
                if i:
                    act.wait_ge(s(f"{passes[i - 1]}_rows_used"), NB)

                def idx(k, p, m):
                    copy_idx(name, k, p, m)
                batches(act, idx)
            norm_part(1)
            turned_h(0)
            for g in range(7):
                w = min(4, NBLK - 4 * g) * P
                act.wait_ge(s("means_turned"), g + 1)
                act.copy(view(SCR, g * 512, [[1, w]], 32), PS[0:32, g % 2, 0:w]).then_inc(s("mt_ready"), 1)
            act.wait_ge(s("weights_loaded"), W_ALL)
            for g in range(7):
                w = min(4, NBLK - 4 * g) * P
                act.wait_ge(s("hidden_made"), g + 1)
                act.activation(hid[:, g * 512:g * 512 + w], PS[:, 2 + g % 2, 0:w], ACT.Identity, bias=b1_s[:, 0:1]).then_inc(s("hidden_biased"), 1)
            norm_part(2)
            turned_h(1)

            def score(k, p, m):
                copy_idx("score", k, p, m)
                if late(k, 1):
                    act.wait_ge(s("radial_turned"), k)
                    gate(act)
                act.copy(bc(SCR, RS_AT, [[VB, 8], [1, VB]]), AT[:, RAD:RAD + 8, bass.ds(VB * k, VB)]).then_inc(s("radial_ready"), 1)
                act.wait_ge(s("oh_turned"), k + 1)
                if late(k, DEPTH):
                    act.wait_ge(s("z_made"), k - DEPTH + 1)
                act.copy(bc(SCR, OT_AT + p * VB * P, [[1, VB * P]]), ot_ps(p)).then_inc(s("ot_ready"), 1)
                act.wait_ge(s("radial_turned"), k + 1)
                act.copy(bc(SCR, RT_AT, [[1, P]], 8 * VB), PS[0:8 * VB, 7, 0:P]).then_inc(s("radial_t_ready"), 1)
                act.wait_ge(s("hidden_pre_made"), k + 1)
                if late(k, DEPTH):
                    act.wait_ge(s(f"hidden_stored{p}"), 16 * m)
                act.activation(bc(SCR, RH_AT + p * P, [[1, P]], 8 * VB), PS[0:8 * VB, 7, 256:256 + P], ACT.Silu,
                               scale=8.0 ** -0.5).then_inc(s("radial_hidden_ready"), 1)

            batches(act, score)

            act.wait_ge(s("below_max"), 1)
            act.activation(PM[:, :, 0:HEADS], ES, ACT.Exp).then_inc(s("probs_ready"), 1)
            act.wait_ge(s("self_below_max"), 1)
            act.activation(self_prob[:], self_prob[:], ACT.Exp).then_inc(s("self_prob_ready"), 1)
            act.wait_ge(s("elu_arg"), 1)
            act.activation(H[:], H[:], ACT.Exp).then_inc(s("elu_exp"), 1)
            norm_part(3)
            turned_h(2)

            def conv(k, p, m):
                copy_idx("conv", k, p, m)
                if late(k, DEPTH):
                    act.wait_ge(s("message_sums"), VB * (k - DEPTH + 1))
                    gate(act)
                for q in range(VB):
                    ins = act.activation(OH[:, p, q, :], iota[:], ACT.Abs, bias=view(EI, 3 * VW + VB * k + q, [[1, 1]]), scale=-1.0)
                ins.then_inc(s("conv_distance"), 1)
                act.wait_ge(s("conv_distance"), k + 1)
                oh = OH[:, p].rearrange("p a b -> p (a b)")
                act.activation(oh, oh, ACT.Relu, bias=1.0, scale=-1.0).then_inc(s("conv_hot"), 1)
                act.wait_ge(s("conv_weights_made"), k + 1)
                act.copy(bc(SCR, W_AT + p * VB * P, [[1, VB * P]]), bc(PS, 5 * 512, [[1, VB * P]])).then_inc(s("conv_weights"), 1)
            batches(act, conv)
            for b in range(NBLK):
                act.wait_ge(s("acc_turned"), b + 1)
                if b >= 2:
                    act.wait_ge(s("update_made"), b - 1)
                act.activation(view(SCR, AC_AT + (b % 2) * 256, [[1, 256]]), PS[:, b % 2, 0:256], ACT.Copy, scale=SUM_SCALE)
                act.wait_ge(s("spread_turned"), b + 1)
                act.copy(view(SCR, ST_AT + (b % 2) * 512, [[1, 512]]), PS[:, 2 + b % 2, :]).then_inc(s("final_copied"), 1)
            act.wait_ge(s("update_ready"), 1)
            act.activation(view(SCR, 0, [[OUTW, NBLK], [1, 64]]), view(SCR, 0, [[OUTW, NBLK], [1, 64]]), ACT.Silu).then_inc(s("gates_ready"), 1)

        @block.vector
        def _(dve):
            steps = [0]

            def done(ins):
                steps[0] += 1
                ins.then_inc(s("dve_step"), 1)
                dve.wait_ge(s("dve_step"), steps[0])

            def norm(n):
                done(dve.tensor_reduce(small[:, 0, :], X[:], AX, ALU.add))
                done(dve.tensor_scalar(small[:, 1, :], small[:, 0, :], 1.0 / D, None, ALU.mult))
                dve.tensor_tensor(H[:], X[:], view(small, NBLK, [[1, NBLK], [0, D]]), ALU.subtract).then_inc(s("centred"), 1)
                dve.wait_ge(s("squared"), n + 1)
                done(dve.tensor_reduce(small[:, 2, :], XL, AX, ALU.add))
                dve.tensor_scalar(small[:, 3, :], small[:, 2, :], 1.0 / D, LN_EPS, ALU.mult, ALU.add).then_inc(s("var_ready"), 1)
                dve.wait_ge(s("std_ready"), n + 1)
                done(dve.reciprocal(small[:, 5, :], small[:, 4, :]))
                return dve.scalar_tensor_tensor(H[:], H[:], 0.0, view(small, 5 * NBLK, [[1, NBLK], [0, D]]), ALU.max, ALU.mult)

            dve.wait_ge(s("iota_made"), 3)
            dve.tensor_copy(iota[:], iota_i[:])
            dve.wait_ge(s("ident_made"), 1)
            dve.tensor_copy(ident_b[:], ident[:])
            dve.tensor_copy(tv[:, 0, :], tvi[:])
            done(dve.tensor_copy(rowf[:, NT:2 * NT], rowi[:, NT:2 * NT]))
            dve.wait_ge(s("last_loaded"), 16)
            done(dve.tensor_scalar(rowi[:, 0:NT], rowi[:, 0:NT], 7, None, ALU.arith_shift_right))
            done(dve.tensor_copy(rowf[:, 0:NT], rowi[:, 0:NT]))
            dve.tensor_tensor(rowf[:, 0:NT], rowf[:, 0:NT], rowf[:, NT:2 * NT], ALU.add).then_inc(s("ends_ready"), 1)
            dve.wait_ge(s("ends_spread"), 1)
            for g in range(VG):
                done(dve.tensor_scalar(H[:, g * 4:g * 4 + 4, :].rearrange("p a b -> p (a b)")[:, 0:NT], PS[:, 0, 0:NT], tv[:, 0, g:g + 1], None, ALU.is_lt))
                done(dve.tensor_reduce(tv[:, 1, g:g + 1], H[:, g * 4:g * 4 + 4, :].rearrange("p a b -> p (a b)")[:, 0:NT], AX, ALU.add))
            done(dve.tensor_scalar(tv[:, 2, :], tv[:, 1, :], float(NT - 1), None, ALU.min))
            dve.tensor_copy(tvi[:], tv[:, 2, :]).then_inc(s("tiles_found"), 1)
            done(dve.tensor_tensor(tv[:, 3, :], tv[:, 0, :], tv[:, 2, :], ALU.subtract))
            done(dve.tensor_scalar(tv[:, 4, :], tv[:, 3, :], float(NBLK - 1), None, ALU.min))
            dve.tensor_scalar(tv[:, 5, :], tv[:, 4, :], -float(P), None, ALU.mult).then_inc(s("blocks_ready"), 1)
            dve.wait_ge(s("blocks_in_psum"), 1)
            dve.tensor_copy(vrow[:, 0:P], PS[0:4, 1, 0:P]).then_inc(s("blocks_turned"), 1)
            dve.wait_ge(s("blocks_in"), 16)
            B0 = 2 * NT
            done(dve.tensor_copy(block_words[:], view(rowi, B0, [[VB, NB]], 1)))
            for q in range(1, VB):
                done(dve.tensor_scalar(view(rowi, 0, [[1, NB]], 1), view(rowi, B0 + q, [[VB, NB]], 1), 5 * q, None, ALU.logical_shift_left))
                done(dve.tensor_tensor(block_words[:], block_words[:], view(rowi, 0, [[1, NB]], 1), ALU.bitwise_or))
            dve.wait_ge(s("x_loaded"), 32)
            norm(0).then_inc(s("table_ready"), 1)
            dve.wait_ge(s("table_ready"), 1)
            for g in range(VG):
                dve.wait_ge(s(f"ids_in{g}"), 16)
                dr = dst_rows[:, g]
                idr = id_rows(g)
                done(dve.tensor_copy(dr.rearrange("p a b -> p (a b)"), idr))
                st = [view(RX, (5 * g + i) * P, [[1, P]]) for i in range(5)]
                dve.tensor_copy(st[0], dr[:, 0])
                dve.tensor_scalar(view(HT, 1536, [[1, P]]).bitcast(I32), idr[:, 0:P], 7, None, ALU.arith_shift_right)
                dve.tensor_scalar(view(HT, 1664, [[1, P]]).bitcast(I32), idr[:, 0:P], 127, None, ALU.bitwise_and)
                done(dve.tensor_scalar(st[3], dr[:, 1], tv[:, 5, g:g + 1], None, ALU.add))
                va, vb, vc = (view(HT, 1792 + 128 * i, [[1, P]]) for i in range(3))
                dve.tensor_copy(st[2], view(HT, 1664, [[1, P]]).bitcast(I32))
                dve.tensor_copy(vc, view(HT, 1536, [[1, P]]).bitcast(I32))
                done(dve.tensor_scalar(va, st[3], 0.0, None, ALU.is_ge))
                done(dve.scalar_tensor_tensor(vb, st[3], float(P - 1), va, ALU.is_le, ALU.mult))
                done(dve.scalar_tensor_tensor(vc, vb, -64.0, vc, ALU.mult, ALU.add))
                dve.tensor_scalar(st[1], vc, 64.0, None, ALU.add)
                dve.tensor_scalar(invalid_neg[:, g, :], vb, 1.0, BIG, ALU.subtract, ALU.mult)
                done(dve.tensor_tensor(va, dr[:, 1], dr[:, 2], ALU.not_equal))
                dve.tensor_tensor(st[4], va, vb, ALU.mult).then_inc(s("kinds_ready"), 1)
            for f in range(0, N_FILL, 2):
                dve.wait_ge(s("fill_turned"), f + 1)
                dst, src = fill_copy(f)
                dve.tensor_copy(dst, src).then_inc(s("fill_copied_dve"), 1)
            dve.wait_ge(s("fill_copied_act"), N_FILL // 2)
            dve.wait_ge(s("fill_copied_dve"), N_FILL - N_FILL // 2)
            dve.tensor_copy(src_idx[:], EI[:, 0, 0:NV + 1]).then_inc(s("idx_made"), 1)
            done(dve.tensor_copy(RES, H[:]))
            dve.wait_ge(s("ones_made"), 2)

            def one_hot(dst, kind, k):
                return dve.tensor_tensor(dst, view(iota, 0, [[0, VB], [1, P]]), view(EI, kind * VW + VB * k, [[1, VB], [0, P]]), ALU.is_equal)

            for i in range(LAYERS):
                name = passes[i]
                r0 = 12 - CH * i
                dve.memset(PSF, 0.0).then_inc(s("sums_zeroed"), 1)

                def hot(k, p, m):
                    if late(k, DEPTH):
                        dve.wait_ge(s(f"{name}_rows_used"), k - DEPTH + 1)
                    sbh = view(SCR, PR_AT + p * VB * NBLK * 7, [[NBLK, VB], [1, NBLK]])
                    prod = view(SCR, PR_AT + p * VB * NBLK * 7 + VB * NBLK, [[NBLK * CH, VB], [CH, NBLK], [1, CH]])
                    dve.tensor_tensor(sbh, view(iota, 0, [[0, VB], [1, NBLK]]), view(EI, VW + VB * k, [[1, VB], [0, NBLK]]), ALU.is_equal).then_inc(s(f"{name}_src_block"), 1)
                    one_hot(OH[:, p], 3, k)
                    one_hot(OHS(p), 2, k)
                    dve.wait_ge(s(f"{name}_src_block"), k + 1)
                    dve.tensor_tensor(prod, view(SCR, PR_AT + p * VB * NBLK * 7, [[NBLK, VB], [1, NBLK], [0, CH]]),
                                      view(AT, r0 * (NV + 1) + VB * k, [[1, VB], [0, NBLK], [NV + 1, CH]]), ALU.mult).then_inc(s(f"{name}_hot"), 1)
                batches(dve, hot)
                dve.wait_ge(s(f"{name}_rows_used"), NB)
                by_src = view(PS, SRC_SUM, [[CH, NBLK], [1, CH]])
                by_dst = view(PS, DST_SUM, [[CH, NBLK], [1, CH]])
                n = min(CH, 16 - r0)
                if i == 0:
                    for side, sums in enumerate((by_src, by_dst)):
                        done(dve.tensor_scalar(small[:, side, :], sums[:, :, 4], 1.0, None, ALU.max))
                        done(dve.reciprocal(inv_deg[:, side, :], small[:, side, :]))
                    dve.tensor_scalar(no_edges[:], by_dst[:, :, 4], 0.5, None, ALU.is_lt)
                dve.tensor_copy(means[:, :, r0:r0 + n], by_src[:, :, 0:n])
                dve.tensor_copy(means[:, :, 16 + r0:16 + r0 + n], by_dst[:, :, 0:n])
                done(dve.tensor_tensor(XL, view(PS, 0, [[D, NBLK], [1, D]]), view(inv_deg, NBLK, [[1, NBLK], [0, D]]), ALU.mult))
                dve.wait_ge(s("table_written"), 16 * (i + 1))
                add = dve.tensor_tensor(H[:], H[:], XL, ALU.add)
                if i < LAYERS - 1:
                    add.then_inc(s("table_ready"), 1)
                    dve.wait_ge(s("table_ready"), i + 2)
                else:
                    done(add)
                done(dve.scalar_tensor_tensor(RES, H[:], 1.0 / (1.0 + i), RES, ALU.mult, ALU.add))
            done(dve.tensor_tensor(X[:], X[:], RES, ALU.add))

            done(dve.tensor_tensor(means[:, :, 0:16], means[:, :, 0:16], view(inv_deg, 0, [[1, NBLK], [0, 16]]), ALU.mult))
            dve.tensor_tensor(means[:, :, 16:32], means[:, :, 16:32], view(inv_deg, NBLK, [[1, NBLK], [0, 16]]), ALU.mult).then_inc(s("means_ready"), 1)
            norm(1).then_inc(s("h_ready"), 1)
            dve.wait_ge(s("weights_loaded"), W_ALL)
            done(dve.tensor_tensor(X[:], X[:], view(rows_s, 0, [[0, NBLK], [1, D]]), ALU.add))
            for g in range(7):
                w = min(4, NBLK - 4 * g) * P
                dve.wait_ge(s("hidden_biased"), g + 1)
                hg = hid[:, g * 512:g * 512 + w]
                dve.scalar_tensor_tensor(hg, hg, 0.01, hg, ALU.mult, ALU.max).then_inc(s("hidden_ready"), 1)
            for g in range(7):
                w = min(4, NBLK - 4 * g)
                dve.wait_ge(s("mlp_made"), g + 1)
                xg = view(X, g * 512, [[1, w * P]])
                ins = dve.tensor_tensor(xg, xg, PS[:, 4 + g % 2, 0:w * P], ALU.add)
                ins.then_inc(s("mlp_added"), 1)
            dve.wait_ge(s("mlp_added"), 7)

            norm(2).then_inc(s("h_ready"), 1)
            for g in range(13):
                w = min(2, NBLK - 2 * g)
                dve.wait_ge(s("lr_made"), g + 1)
                bank = g % 4
                dve.tensor_tensor(XL[:, 2 * g:2 * g + w, :], view(PS, bank * 512, [[256, w], [1, D]]),
                                  view(rows_s, 3 * D, [[0, w], [1, D]]), ALU.add)
                ins = dve.tensor_tensor(XR[:, 2 * g:2 * g + w, 0:D], view(PS, bank * 512 + D, [[256, w], [1, D]]),
                                        view(rows_s, 4 * D, [[0, w], [1, D]]), ALU.add)
                ins.then_inc(s("lr_copied"), 1)
            dve.wait_ge(s("lr_copied"), 13)
            ins = dve.tensor_tensor(H[:], XL, XR[:, :, 0:D], ALU.add)
            ins.then_inc(s("table_ready"), 1)
            dve.wait_ge(s("table_ready"), 4)
            done(dve.scalar_tensor_tensor(H[:], H[:], 0.2, H[:], ALU.mult, ALU.max))
            done(dve.tensor_tensor(H[:], H[:], view(rows_s, D, [[0, NBLK], [1, D]]), ALU.mult))
            done(dve.tensor_reduce(self_score[:], H[:].rearrange("p b (h c) -> p b h c", h=HEADS), AX, ALU.add))
            dve.tensor_copy(XR[:, :, D:XR_W], self_score[:]).then_inc(s("xr_ready"), 1)

            def score(k, p, m):
                if late(k, DEPTH):
                    dve.wait_ge(s("oh_turned"), k - DEPTH + 1)
                one_hot(OHB(p), 3, k).then_inc(s("score_hot"), 1)
                if late(k, 2):
                    rate(k - 2, *before(*before(p, m)))

            def rate(k, p, m):
                z_at = Z_AT + p * VB * D
                dve.wait_ge(s(f"score_gathered{p}"), 16 * VB * (m + 1))
                dve.wait_ge(s("z_made"), k + 1)
                dve.tensor_scalar(view(HT, MS_AT + VB * HEADS * k, [[HEADS, VB], [1, HEADS]]),
                                  bc(PS, 4 * 512 + D, [[256, VB], [1, HEADS]]), 0.0, None, ALU.add)
                dve.tensor_tensor(bc(SCR, z_at, [[D, VB], [1, D]]), bc(PS, 4 * 512, [[256, VB], [1, D]]), G[:, p], ALU.add).then_inc(s("z_read"), 1)
                dve.wait_ge(s("z_read"), k + 1)
                zz = bc(SCR, z_at, [[1, VB * D]])
                ll = bc(SCR, L_AT, [[1, VB * D]])
                dve.scalar_tensor_tensor(ll, zz, 0.2, zz, ALU.mult, ALU.max).then_inc(s("leaky"), 1)
                dve.wait_ge(s("leaky"), k + 1)
                dve.tensor_tensor(bc(SCR, L_AT, [[D, VB], [1, D]]), bc(SCR, L_AT, [[D, VB], [1, D]]),
                                  view(rows_s, D, [[0, VB], [1, D]]), ALU.mult).then_inc(s("weighed"), 1)
                dve.wait_ge(s("weighed"), k + 1)
                gate(dve)
                dve.tensor_reduce(view(HT, VB * HEADS * k, [[1, VB * HEADS]]), bc(SCR, L_AT, [[C, VB * HEADS], [1, C]]),
                                  AX, ALU.add).then_inc(s("scored"), 1)
            batches(dve, score)
            for k, buf in ((NB - 2, before(*LAST)), (NB - 1, LAST)):
                dve.wait_ge(s("scored"), k)
                rate(k, *buf)
            dve.wait_ge(s("scored"), NB)

            N16 = VG * HEADS * P
            CF_AT, PRE_AT, SUF_AT = 0, N16 + 1, 2 * N16 + 1
            E2 = view(H, 0, [[HEADS * P, VG], [P, HEADS], [1, P]])
            cont = view(SCR, CF_AT, [[HEADS * P, VG], [P, HEADS], [1, P]])
            dve.memset(view(H, 0, [[1, N16]]), -BIG)
            done(dve.memset(view(SCR, CF_AT, [[1, N16 + 1]]), -BIG))
            for g in range(VG):
                first = g * 3 * P + P
                done(dve.tensor_tensor(view(RX, g * P, [[1, P - 1]]), view(dst_rows, first + 1, [[1, P - 1]]), view(dst_rows, first, [[1, P - 1]]), ALU.not_equal))
                done(dve.tensor_scalar(view(SCR, CF_AT + g * HEADS * P + 1, [[P, HEADS], [1, P - 1]]), view(RX, g * P, [[0, HEADS], [1, P - 1]]), -BIG, None, ALU.mult))
            dve.wait_ge(s("scores_turned"), 1)
            for g in range(VG):
                w = WG[g]
                ins = dve.tensor_tensor(view(H, g * HEADS * P, [[P, HEADS], [1, P]], w), view(PS, g * 512, [[P, HEADS], [1, P]], w),
                                        view(invalid_neg, g * P, [[0, HEADS], [1, P]], w), ALU.add)
            done(ins)
            for p in range(DEPTH):
                dve.wait_ge(s(f"hidden_stored{p}"), 16 * uses(p))
            flat = lambda t, at, step=1: view(t, at + (N16 - 1 if step < 0 else 0), [[step, N16]])
            dve.tensor_tensor_scan(flat(SCR, PRE_AT), flat(SCR, CF_AT), flat(H, 0), -BIG, ALU.add, ALU.max)
            done(dve.tensor_tensor_scan(flat(SCR, SUF_AT, -1), flat(SCR, CF_AT + 1, -1), flat(H, 0, -1), -BIG, ALU.add, ALU.max))
            for g in range(VG):
                dve.tensor_copy(view(HT, END_AT + (0 * VG + g) * 4, [[1, 4]]), view(SCR, PRE_AT + g * 512 + P - 1, [[P, 4]]))
                dve.tensor_copy(view(HT, END_AT + (1 * VG + g) * 4, [[1, 4]]), view(SCR, SUF_AT + g * 512, [[P, 4]]))
                dve.tensor_copy(view(HT, END_AT + (2 * VG + g) * 4, [[1, 4]]), view(dst_rows, g * 3 * P + P, [[0, 4]]))
                ins = dve.tensor_copy(view(HT, END_AT + (3 * VG + g) * 4, [[1, 4]]), view(dst_rows, g * 3 * P + 2 * P - 1, [[0, 4]]))
            ins.then_inc(s("ends_made"), 1)
            dve.wait_ge(s("ends_turned"), 1)
            R = lambda i, at=0, n=NV, step=1: view(H, i * VW + at, [[step, n]], 4)
            for i in range(4):
                ins = dve.tensor_copy(R(i), PS[0:4, i, 0:NV])
            done(ins)
            A = lambda i, at=0, n=NV, step=1: view(RX, i * VW + at, [[step, n]], 4)
            done(dve.memset(view(RX, 0, [[1, 6 * VW]], 4), 1.0))
            dve.tensor_tensor(A(0, 1, NV - 1), R(2, 1, NV - 1), R(3, 0, NV - 1), ALU.not_equal)
            done(dve.tensor_tensor(A(1), R(2), R(3), ALU.not_equal))
            dve.tensor_tensor(A(2), A(0), A(1), ALU.max)
            done(dve.tensor_tensor(A(3), A(0, 1), A(1), ALU.max))
            done(dve.tensor_scalar(view(RX, 0, [[VW, 4], [1, NV + 1]], 4), view(RX, 0, [[VW, 4], [1, NV + 1]], 4), -BIG, None, ALU.mult))
            dve.tensor_tensor_scan(A(4), A(2), R(0), -BIG, ALU.add, ALU.max)
            done(dve.tensor_tensor_scan(A(5, NV - 1, NV, -1), A(3, NV - 1, NV, -1), R(1, NV - 1, NV, -1), -BIG, ALU.add, ALU.max))
            done(dve.memset(view(H, 0, [[1, 2 * VW]], 4), -BIG))
            dve.tensor_tensor(R(0, 1, NV - 1), A(4, 0, NV - 1), A(0, 1, NV - 1), ALU.add)
            dve.tensor_tensor(R(1, 0, NV - 1), A(5, 1, NV - 1), A(0, 1, NV - 1), ALU.add).then_inc(s("carries_ready"), 1)
            dve.wait_ge(s("carries_turned"), 1)
            done(dve.tensor_tensor(flat(SCR, PRE_AT), flat(SCR, PRE_AT), flat(SCR, SUF_AT), ALU.max))
            done(dve.tensor_copy(view(HT, END_AT, [[1, 32]]), PS[:, 4, 0:32]))
            for side in range(2):
                edge_of = P if side == 0 else 2 * P - 1
                for g in range(VG):
                    done(dve.tensor_scalar(view(SCR, CF_AT, [[1, P]]), view(dst_rows, g * 3 * P + P, [[1, P]]),
                                           view(dst_rows, g * 3 * P + edge_of, [[1, 1]]), -BIG, ALU.not_equal, ALU.mult))
                    for h in range(HEADS):
                        m_gh = view(SCR, PRE_AT + (g * HEADS + h) * P, [[1, P]])
                        ins = dve.scalar_tensor_tensor(m_gh, view(SCR, CF_AT, [[1, P]]), view(HT, END_AT + side * 16 + g * 4 + h, [[1, 1]]),
                                                       m_gh, ALU.add, ALU.max)
                    done(ins)
            dve.memset(small[:, 6, :], 0.0).then_inc(s("maxima_ready"), 1)
            dve.wait_ge(s("maxima_turned"), 1)
            for g in range(VG):
                w = WG[g]
                ms = view(HT, MS_AT + g * P * HEADS, [[1, HEADS], [HEADS, w]])
                ins = dve.tensor_tensor(ms, ms, view(PS, g * 512, [[P, HEADS], [1, w]]), ALU.max)
            done(ins)
            done(dve.tensor_tensor(ES, ES, MS, ALU.subtract))
            dve.tensor_scalar(ES, ES, 0.0, None, ALU.min).then_inc(s("below_max"), 1)
            dve.tensor_tensor(PM[:, :, HEADS:8], MS, view(EI, 4 * VW, [[1, NV], [0, HEADS]]), ALU.mult)
            dve.memset(PSF, 0.0).then_inc(s("sums_zeroed"), 1)
            dve.wait_ge(s("probs_ready"), 1)

            def weigh(k, p, m):
                if late(k, DEPTH):
                    dve.wait_ge(s("sum_done"), k - DEPTH + 1)
                one_hot(OH[:, p], 3, k)
                dve.wait_ge(s(f"rows_back{p}"), 16 * (m + 1))
                gg = view(G, p * VB * D, [[D, VB], [C, HEADS], [1, C]])
                dve.tensor_tensor(gg, gg, view(RX, 8 * VB * k, [[8, VB], [1, HEADS], [0, C]]), ALU.mult).then_inc(s("sum_hot"), 1)
            batches(dve, weigh)
            dve.wait_ge(s("sum_done"), NB)
            sums8 = view(PS, DST_SUM, [[8, NBLK], [1, 8]])
            done(dve.tensor_tensor(node_max[:], self_score[:], view(no_edges, 0, [[1, NBLK], [0, HEADS]]), ALU.mult))
            done(dve.tensor_tensor(node_max[:], node_max[:], sums8[:, :, 4:8], ALU.add))
            dve.tensor_tensor(self_prob[:], self_score[:], node_max[:], ALU.subtract).then_inc(s("self_below_max"), 1)
            dve.wait_ge(s("self_prob_ready"), 1)
            h4 = H[:].rearrange("p b (h c) -> p b h c", h=HEADS)
            for h in range(HEADS):
                dve.tensor_tensor(H[:, :, h * C:(h + 1) * C], XL[:, :, h * C:(h + 1) * C], view(self_prob, h, [[HEADS, NBLK], [0, C]]), ALU.mult)
            done(dve.tensor_tensor(node_max[:], self_prob[:], sums8[:, :, 0:4], ALU.add))
            done(dve.tensor_tensor(H[:], H[:], view(PS, 0, [[D, NBLK], [1, D]]), ALU.add))
            done(dve.tensor_scalar(node_max[:], node_max[:], 1e-16, None, ALU.add))
            done(dve.reciprocal(node_max[:], node_max[:]))
            for h in range(HEADS):
                ins = dve.tensor_tensor(H[:, :, h * C:(h + 1) * C], H[:, :, h * C:(h + 1) * C], view(node_max, h, [[HEADS, NBLK], [0, C]]), ALU.mult)
            done(ins)
            done(dve.tensor_tensor(H[:], H[:], view(rows_s, 2 * D, [[0, NBLK], [1, D]]), ALU.add))
            done(dve.scalar_tensor_tensor(X[:], H[:], 0.0, X[:], ALU.max, ALU.add))
            dve.tensor_scalar(H[:], H[:], 0.0, None, ALU.min).then_inc(s("elu_arg"), 1)
            dve.wait_ge(s("elu_exp"), 1)
            done(dve.scalar_tensor_tensor(X[:], H[:], -1.0, X[:], ALU.add, ALU.add))

            norm(3).then_inc(s("h_ready"), 1)
            for g in range(7):
                w = min(4, NBLK - 4 * g) * P
                dve.wait_ge(s("up_made"), g + 1)
                dve.tensor_scalar(view(RX, XL_AT + g * 512, [[1, w]]), PS[:, g, 0:w], 32.0 ** -0.5, None, ALU.mult).then_inc(s("up_copied"), 1)
            dve.wait_ge(s("up_copied"), 7)
            dve.tensor_copy(spec_f[:], spec_s[:]).then_inc(s("table_ready"), 1)
            dve.wait_ge(s("table_ready"), 5)
            for sp_ in range(4):
                dve.tensor_scalar(smask[:, :, sp_], spec_f[:], float(sp_), None, ALU.is_equal)
            dve.wait_ge(s("table_written"), 16 * 5)
            done(dve.memset(view(RX, 0, [[1, NBLK * MSG]]), 0.0))

            def message(k, p, m):
                if late(k, DEPTH):
                    dve.wait_ge(s("message_sums"), VB * (k - DEPTH + 1))
                dve.wait_ge(s(f"conv_gathered{p}"), 16 * VB * (m + 1))
                dve.wait_ge(s("conv_weights"), k + 1)
                g0 = p * VB * D
                m0 = M_AT + p * VB * MSG
                w0 = W_AT + p * VB * P
                y = lambda dims: view(AT, (SH + 1) * (NV + 1) + VB * k, dims)
                dve.tensor_tensor(view(SCR, C_AT, [[C, VB], [1, C]]), view(G, g0, [[D, VB], [1, C]]), view(SCR, w0 + 64, [[P, VB], [1, C]]), ALU.mult)
                dve.tensor_tensor(view(SCR, T_AT, [[96, VB], [C, 3], [1, C]]), view(G, g0 + C, [[D, VB], [C, 3], [1, C]]),
                                  y([[1, VB], [NV + 1, 3], [0, C]]), ALU.mult).then_inc(s("conv_parts"), 1)
                dve.tensor_tensor(view(SCR, m0, [[MSG, VB], [1, C]]), view(G, g0, [[D, VB], [1, C]]), view(SCR, w0, [[P, VB], [1, C]]), ALU.mult)
                dve.tensor_tensor(view(SCR, m0 + 64, [[MSG, VB], [64, 3], [1, C]]), view(G, g0 + C, [[D, VB], [C, 3], [1, C]]),
                                  view(SCR, w0 + C, [[P, VB], [0, 3], [1, C]]), ALU.mult)
                dve.wait_ge(s("conv_parts"), k + 1)
                dve.tensor_tensor(view(SCR, m0 + 96, [[MSG, VB], [64, 3], [1, C]]), view(SCR, C_AT, [[C, VB], [0, 3], [1, C]]),
                                  y([[1, VB], [NV + 1, 3], [0, C]]), ALU.mult)
                dve.tensor_reduce(view(SCR, U_AT, [[C, VB], [1, C]]), view(SCR, T_AT, [[96, VB], [1, C], [C, 3]]), AX, ALU.add).then_inc(s("conv_dot"), 1)
                dve.wait_ge(s("conv_dot"), k + 1)
                dve.scalar_tensor_tensor(view(SCR, m0 + C, [[MSG, VB], [1, C]]), view(SCR, U_AT, [[C, VB], [1, C]]), INV_SQRT3,
                                         view(SCR, w0 + 96, [[P, VB], [1, C]]), ALU.mult, ALU.mult).then_inc(s("messages_ready"), 1)
                if late(k, 1):
                    add_up(k - 1)

            def add_up(k):
                word = dve.value_load(block_words[0:1, bass.ds(k, 1)])
                dve.wait_ge(s("message_sums"), VB * (k + 1))
                for q in range(VB):
                    acc = view(RX, ((word >> (5 * q)) & 31) * MSG, [[1, MSG]])
                    if late(k, 1) or q:
                        dve.wait_ge(s("added"), VB * k + q)
                    dve.tensor_tensor(acc, acc, PS[:, q, 0:MSG], ALU.add).then_inc(s("added"), 1)
            batches(dve, message)
            add_up(NB - 1)
            dve.wait_ge(s("added"), NV)
            dve.memset(small[:, 7, :], 0.0).then_inc(s("messages_summed"), 1)

            for b in range(NBLK):
                dve.wait_ge(s("update_made"), b + 1)
                dve.tensor_scalar(view(SCR, b * OUTW, [[1, OUTW]]), PS[:, 4 + b % 2, 0:OUTW], 0.5 * 32.0 ** -0.5, None, ALU.mult).then_inc(s("update_copied"), 1)
            dve.wait_ge(s("update_copied"), NBLK)
            dve.memset(small[:, 7, :], 0.0).then_inc(s("update_ready"), 1)
            dve.wait_ge(s("gates_ready"), 1)
            for i3 in range(3):
                ins = dve.tensor_tensor(view(SCR, 64 + 32 * i3, [[OUTW, NBLK], [1, 32]]), view(SCR, 64 + 32 * i3, [[OUTW, NBLK], [1, 32]]),
                                        view(SCR, 32, [[OUTW, NBLK], [1, 32]]), ALU.mult)
            done(ins)
            dve.tensor_tensor(X[:, :, 0:32], X[:, :, 0:32], view(SCR, 0, [[OUTW, NBLK], [1, 32]]), ALU.add)
            xv = view(X, 32, [[D, NBLK], [3, 32], [1, 3]])
            dve.tensor_tensor(xv, xv, view(SCR, 64, [[OUTW, NBLK], [1, 32], [32, 3]]), ALU.add).then_inc(s("result_ready"), 1)

        @block.tensor
        def _(pe):
            def turn_h(n):
                pe.wait_ge(s("h_ready"), n + 1)
                for b in range(NBLK):
                    ins = pe.transpose(PS[:, b // 4, (b % 4) * P:(b % 4 + 1) * P], H[:, b, :], ident[:])
                    if b % 4 == 3 or b == NBLK - 1:
                        ins.then_inc(s("h_turned"), 1)

            pe.wait_ge(s("ends_ready"), 1)
            pe.wait_ge(s("ones_made"), 2)
            pe.matmul(PS[:, 0, 0:NT], ones_row[:], rowf[:, 0:NT], start=True, stop=True).then_inc(s("ends_spread"), 1)
            pe.wait_ge(s("blocks_ready"), 1)
            pe.wait_ge(s("ident_made"), 1)
            pe.transpose(PS[0:4, 1, 0:P], tv[:, 4, :], ident[:]).then_inc(s("blocks_in_psum"), 1)
            pe.wait_ge(s("blocks_turned"), 1)
            for f in range(N_FILL):
                g, j = divmod(f, 9)
                if j == 0:
                    pe.wait_ge(s("kinds_ready"), g + 1)
                if j == 2:
                    pe.wait_ge(s(f"attrs_in{g}"), 16)
                if f >= 6:
                    o = f - 6
                    pe.wait_ge(s("fill_copied_act" if o % 2 else "fill_copied_dve"), o // 2 + 1)
                n = 4 if j != 1 else 1
                for i in range(n):
                    if j < 2:
                        src = view(RX, (5 * g + 4 * j + i) * P, [[1, P]])
                    else:
                        src = view(SCR, (g % 2) * N_ATTR * P + (4 * (j - 2) + i) * P, [[1, P]])
                    ins = pe.transpose(PS[:, 2 + f % 6, i * P:(i + 1) * P], src, ident[:])
                ins.then_inc(s("fill_turned"), 1)

            for i in range(LAYERS):
                name = passes[i]
                r0 = 12 - CH * i
                pe.wait_ge(s("sums_zeroed"), i + 1)

                def scatter(k, p, m):
                    word = pe.value_load(block_words[0:1, bass.ds(k, 1)])
                    pe.wait_ge(s(f"{name}_hot"), k + 1)
                    pe.wait_ge(s(f"{name}_gathered{p}"), 16 * VB * (m + 1))
                    for q in range(VB):
                        b = (word >> (5 * q)) & 31
                        pe.matmul(PSF[:, bass.ds(b * P, P)], OH[:, p, q, :], G[:, p, q, :], start=False, stop=False, skip_group_check=True)
                        pe.matmul(PSF[:, bass.ds(b * CH + DST_SUM, CH)], OH[:, p, q, :],
                                  view(AT, r0 * (NV + 1) + VB * k + q, [[NV + 1, CH]]), start=False, stop=False, skip_group_check=True)
                        ins = pe.matmul(PSF[:, SRC_SUM:SRC_SUM + CH * NBLK], view(SCR, p * VB * P + q * P, [[1, P]]),
                                        view(SCR, PR_AT + p * VB * NBLK * 7 + VB * NBLK + q * NBLK * CH, [[1, NBLK * CH]]),
                                        start=False, stop=False, skip_group_check=True)
                    ins.then_inc(s(f"{name}_rows_used"), 1)
                batches(pe, scatter)

            turn_h(0)
            pe.wait_ge(s("means_ready"), 1)
            pe.wait_ge(s("ht_ready"), 7)
            for g in range(7):
                w = min(4, NBLK - 4 * g)
                if g >= 2:
                    pe.wait_ge(s("mt_ready"), g - 1)
                for b in range(w):
                    ins = pe.transpose(PS[0:32, g % 2, b * P:(b + 1) * P], means[:, 4 * g + b, :], ident[:])
                ins.then_inc(s("means_turned"), 1)
            pe.wait_ge(s("weights_loaded"), W_ALL)
            for g in range(7):
                w = min(4, NBLK - 4 * g) * P
                pe.wait_ge(s("mt_ready"), g + 1)
                if g >= 2:
                    pe.wait_ge(s("hidden_biased"), g - 1)
                pe.matmul(PS[:, 2 + g % 2, 0:w], w1a_s[:], HTF[:, g * 512:g * 512 + w], start=True, stop=False)
                pe.matmul(PS[:, 2 + g % 2, 0:w], w1b_s[:], view(SCR, g * 512, [[1, w]], 32), start=False, stop=True).then_inc(s("hidden_made"), 1)
            for g in range(7):
                w = min(4, NBLK - 4 * g)
                pe.wait_ge(s("hidden_ready"), g + 1)
                if g >= 2:
                    pe.wait_ge(s("mlp_added"), g - 1)
                for b in range(w):
                    ins = pe.matmul(PS[:, 4 + g % 2, b * P:(b + 1) * P], hid[:, (4 * g + b) * P:(4 * g + b + 1) * P], w2_s[:], start=True, stop=True)
                ins.then_inc(s("mlp_made"), 1)

            turn_h(1)
            pe.wait_ge(s("ht_ready"), 14)
            for g in range(13):
                if g >= 4:
                    pe.wait_ge(s("lr_copied"), g - 3)
                for b in range(min(2, NBLK - 2 * g)):
                    ins = pe.matmul(PS[:, g % 4, b * 256:(b + 1) * 256], HTF[:, (2 * g + b) * P:(2 * g + b + 1) * P], wlr_s[:], start=True, stop=True)
                ins.then_inc(s("lr_made"), 1)
            pe.wait_ge(s("xr_ready"), 1)

            def score(k, p, m):
                pe.wait_ge(s("score_hot"), k + 1)
                if late(k, DEPTH):
                    pe.wait_ge(s("ot_ready"), k - DEPTH + 1)
                for q in range(VB):
                    ins = pe.transpose(ot_ps(p)[:, q * P:(q + 1) * P], OHB(p)[:, q, :], ident_b[:])
                ins.then_inc(s("oh_turned"), 1)
                pe.wait_ge(s("radial_ready"), k + 1)
                if late(k, 1):
                    pe.wait_ge(s("radial_hidden_ready"), k)
                gate(pe)
                pe.transpose(PS[0:8 * VB, 7, 0:P], view(SCR, RS_AT, [[1, 8 * VB]]), ident[:]).then_inc(s("radial_turned"), 1)
                if late(k, 1):
                    add_r(k - 1, *before(p, m))
                pe.wait_ge(s("radial_t_ready"), k + 1)
                gate(pe)
                pe.matmul(PS[0:8 * VB, 7, 256:256 + P], wr1_s[:], view(SCR, RT_AT, [[1, P]], 8 * VB), start=True, stop=True).then_inc(s("hidden_pre_made"), 1)

            def add_r(k, p, m):
                word = pe.value_load(block_words[0:1, bass.ds(k, 1)])
                pe.wait_ge(s("ot_ready"), k + 1)
                if late(k, 1):
                    pe.wait_ge(s("z_read"), k)
                for q in range(VB):
                    b = (word >> (5 * q)) & 31
                    zq = 4 * 512 + 256 * q
                    ins = pe.matmul(view(PS, zq, [[1, XR_W]]), view(SCR, OT_AT + (p * VB + q) * P, [[1, P]]),
                                    view(RX, b * XR_W, [[1, XR_W]]), start=True, stop=True)
                ins.then_inc(s("z_made"), 1)
            batches(pe, score)
            add_r(NB - 1, *LAST)

            pe.wait_ge(s("scored"), NB)
            for g in range(VG):
                for h in range(HEADS):
                    ins = pe.transpose(view(PS, g * 512 + h * P, [[1, P]], WG[g]), view(HT, g * P * HEADS + h, [[HEADS, WG[g]]]), ident[:])
            ins.then_inc(s("scores_turned"), 1)
            pe.wait_ge(s("ends_made"), 1)
            for i in range(4):
                for g in range(VG):
                    ins = pe.transpose(PS[0:4, i, g * P:(g + 1) * P], view(HT, END_AT + (i * VG + g) * 4, [[1, 4]]), ident[:])
            ins.then_inc(s("ends_turned"), 1)
            pe.wait_ge(s("carries_ready"), 1)
            for i in range(2):
                for g in range(VG):
                    ins = pe.transpose(PS[:, 4, i * 16 + g * 4:i * 16 + g * 4 + 4], view(H, i * VW + g * P, [[1, P]], 4), ident[0:4, 0:4])
            ins.then_inc(s("carries_turned"), 1)
            pe.wait_ge(s("maxima_ready"), 1)
            for g in range(VG):
                for h in range(HEADS):
                    ins = pe.transpose(view(PS, g * 512 + h * P, [[1, WG[g]]]), view(SCR, VG * HEADS * P + 1 + (g * HEADS + h) * P, [[1, P]], WG[g]), ident[0:WG[g], 0:WG[g]])
            ins.then_inc(s("maxima_turned"), 1)

            pe.wait_ge(s("sums_zeroed"), LAYERS + 1)
            pe.wait_ge(s("probs_ready"), 1)

            def weighted(k, p, m):
                word = pe.value_load(block_words[0:1, bass.ds(k, 1)])
                pe.wait_ge(s("sum_hot"), k + 1)
                for q in range(VB):
                    b = (word >> (5 * q)) & 31
                    pe.matmul(PSF[:, bass.ds(b * P, P)], OH[:, p, q, :], G[:, p, q, :], start=False, stop=False, skip_group_check=True)
                    ins = pe.matmul(PSF[:, bass.ds(b * 8 + DST_SUM, 8)], OH[:, p, q, :],
                                    view(RX, 8 * (VB * k + q), [[1, 8]]), start=False, stop=False, skip_group_check=True)
                ins.then_inc(s("sum_done"), 1)
            batches(pe, weighted)

            turn_h(2)
            for b in range(NBLK):
                if b % 4 == 0:
                    pe.wait_ge(s("ht_ready"), 14 + b // 4 + 1)
                ins = pe.matmul(PS[:, b // 4, (b % 4) * P:(b % 4 + 1) * P], HTF[:, b * P:(b + 1) * P], wup_s[:], start=True, stop=True)
                if b % 4 == 3 or b == NBLK - 1:
                    ins.then_inc(s("up_made"), 1)
            pe.wait_ge(s("up_copied"), 7)

            def conv(k, p, m):
                pe.wait_ge(s(f"hidden_back{p}"), 16 * (m + 1))
                if late(k, 1):
                    pe.wait_ge(s("conv_weights"), k)
                for q in range(VB):
                    ins = pe.matmul(view(PS, 5 * 512 + q * P, [[1, P]]), view(SCR, CH_AT + p * P, [[1, P]], 8 * VB), wr2_s[:, q, :], start=True, stop=True)
                ins.then_inc(s("conv_weights_made"), 1)
                if late(k, 1):
                    sums(k - 1, before(p, m)[0])

            def sums(k, p):
                pe.wait_ge(s("messages_ready"), k + 1)
                pe.wait_ge(s("conv_hot"), k + 1)
                if late(k, 1):
                    pe.wait_ge(s("added"), VB * k)
                for q in range(VB):
                    ins = pe.matmul(PS[:, q, 0:MSG], OH[:, p, q, :], view(SCR, M_AT + (p * VB + q) * MSG, [[1, MSG]]), start=True, stop=True)
                    ins.then_inc(s("message_sums"), 1)
            batches(pe, conv)
            sums(NB - 1, LAST[0])

            def update(b):
                pe.wait_ge(s("final_copied"), b + 1)
                if b >= 2:
                    pe.wait_ge(s("update_copied"), b - 1)
                ps = PS[:, 4 + b % 2, :]
                sums_t = lambda j: view(SCR, AC_AT + (b % 2) * 256 + j * P, [[1, P]])
                spread_t = lambda j: view(SCR, ST_AT + (b % 2) * 512 + j * P, [[1, P]])
                pe.matmul(ps[:, 0:96], sums_t(0), wdna_s[:], start=True, stop=False, skip_group_check=True)
                pe.matmul(ps[:, 96:160], sums_t(1), wdnb_s[:], start=False, stop=False, skip_group_check=True)
                pe.matmul(ps[:, 0:64], spread_t(0), wsk_s[:, 0:64], start=False, stop=False, skip_group_check=True)
                for i3 in range(3):
                    ins = pe.matmul(ps[:, 64 + 32 * i3:96 + 32 * i3], spread_t(i3 + 1), wsk_s[:, 64:96], start=False,
                                    stop=i3 == 2, skip_group_check=True)
                ins.then_inc(s("update_made"), 1)

            pe.wait_ge(s("messages_summed"), 1)
            for b in range(NBLK):
                if b >= 2:
                    pe.wait_ge(s("final_copied"), b - 1)
                for j in range(2):
                    ins = pe.transpose(PS[:, b % 2, j * P:(j + 1) * P], view(RX, b * MSG + j * P, [[1, P]]), ident[:])
                ins.then_inc(s("acc_turned"), 1)
                pe.wait_ge(s("spread"), b + 1)
                for j in range(4):
                    ins = pe.transpose(PS[:, 2 + b % 2, j * P:(j + 1) * P], view(SCR, SP_AT + (b % 2) * 512 + j * P, [[1, P]]), ident[:])
                ins.then_inc(s("spread_turned"), 1)
                if b >= 1:
                    update(b - 1)
            update(NBLK - 1)


def kernel(x, src, dst, edge_attr_16, edge_attr_4, edge_attr_8, node_type_4, L1_gnn_W1, L1_gnn_b1, L1_gnn_W2, L1_gnn_b2,
           L2_gnn_W_l, L2_gnn_b_l, L2_gnn_W_r, L2_gnn_b_r, L2_gnn_att, L2_gnn_bias, L3_gnn_W_up_s, L3_gnn_W_up_v,
           L3_gnn_W_r1, L3_gnn_W_r2, L3_gnn_W_dn_s, L3_gnn_W_dn_v, L3_gnn_W_sk_s, L3_gnn_W_sk_v):
    import numpy as np
    import concourse.bacc as bacc
    from concourse.bass_utils import run_bass_kernel_spmd

    a = lambda t: np.ascontiguousarray(np.asarray(t))
    f32, i32 = np.float32, np.int32
    ids = np.full((3, NT * P), NPAD - 1, i32)
    ids[0, :EDGES], ids[1, :EDGES] = a(src), a(dst)
    ids[2, 1:], ids[2, 0] = ids[1, :-1], -1
    attrs = np.zeros((NT * P, N_ATTR), f32)
    attrs[:EDGES] = np.concatenate([a(edge_attr_16), a(edge_attr_4), a(edge_attr_8)], 1)
    types = np.zeros((NPAD,), i32)
    types[:NODES] = a(node_type_4)

    up = np.zeros((D, D), f32)
    up[0:32, 0:32] = a(L3_gnn_W_up_s)
    for i in range(3):
        up[32 + i::3, 32 + 32 * i:64 + 32 * i] = a(L3_gnn_W_up_v)
    wr1 = np.zeros((8, VB, VB, 8), f32)
    wr2 = np.zeros((VB, 8, VB, P), f32)
    for q in range(VB):
        wr1[:, q, q, :] = a(L3_gnn_W_r1)
        wr2[q, :, q, :] = a(L3_gnn_W_r2)
    dn_a, dn_b = np.zeros((P, 96), f32), np.zeros((P, 64), f32)
    dn_a[0:64, 0:64] = a(L3_gnn_W_dn_s)
    dn_a[64:128, 64:96] = dn_b[0:64, 0:32] = dn_b[64:128, 32:64] = a(L3_gnn_W_dn_v)
    arrays = {
        "x": a(x),
        "edge_ids": a(ids.reshape(3, NT, P).transpose(1, 0, 2).reshape(NT, 3 * P)),
        "last_dst": a(ids[1, P - 1::P].reshape(1, NT)),
        "edge_attrs": a(attrs.reshape(NT, P, N_ATTR).transpose(0, 2, 1).reshape(NT, N_ATTR * P)),
        "species": a(types.reshape(NBLK, P).T),
        "w1a": a(L1_gnn_W1)[0:D], "w1b": a(a(L1_gnn_W1)[D:D + 32]), "b1": a(L1_gnn_b1).reshape(D, 1), "w2": a(L1_gnn_W2),
        "row_params": np.concatenate([a(L1_gnn_b2), a(L2_gnn_att).reshape(-1), a(L2_gnn_bias), a(L2_gnn_b_l), a(L2_gnn_b_r)]),
        "wlr": a(np.concatenate([a(L2_gnn_W_l).T, a(L2_gnn_W_r).T], 1)),
        "wup": up, "wr1": wr1.reshape(8 * VB, 8 * VB), "wr2": wr2.reshape(8 * VB, VB, P), "wdn_a": dn_a, "wdn_b": dn_b,
        "wsk": a(np.concatenate([a(L3_gnn_W_sk_s).reshape(P, 64), a(L3_gnn_W_sk_v).reshape(P, 32)], 1)),
    }
    nc = bacc.Bacc("TRN2", target_bir_lowering=False, num_devices=1)
    handles = [nc.dram_tensor(f"in_{n}", v.shape, mybir.dt.from_np(v.dtype), kind="ExternalInput").ap() for n, v in arrays.items()]
    handles.append(nc.dram_tensor("out", (NODES, D), F32, kind="ExternalOutput").ap())
    gnn_program(nc, *handles)
    r = run_bass_kernel_spmd(nc, [{f"in_{n}": v for n, v in arrays.items()}], core_ids=[0])
    return r.results[0]["out"]
```

```python
from contextlib import ExitStack

import concourse.bass as bass
from concourse import mybir

F32 = mybir.dt.float32
BF16 = mybir.dt.bfloat16
I32 = mybir.dt.int32
ALU = mybir.AluOpType
ACT = mybir.ActivationFunctionType
AX = mybir.AxisListType.X

P = 128
NODES, D = 3125, 128
EDGES = 50000
NBLK = -(-NODES // P)
NPAD = NBLK * P
NT = -(-EDGES // P)
NV = NT + NBLK - 1
VB = 5
NB = NV // VB
DEPTH = 3
CHUNKS = 5
CB = NBLK // CHUNKS
PEEL = 5
LAST = ((NB - 1) % DEPTH, (NB - 1) // DEPTH)
VG = -(-NV // P)
VW = VG * P
WG = [min(P, NV - g * P) for g in range(VG)]
HEADS, C = 4, 32
N_ATTR = 16 + 4 + 8
LAYERS = 3
SPECIES = 4
CH = 6
ROWS = 18 + 4 + 8
SH, RAD = 18, 22
BIG = 1.0e30
LN_EPS = 1e-5
INV_SQRT3 = 0.5773502691896258
MSG = 256
SUM_SCALE = 16.0 ** -0.5 * 8.0 ** -0.5 * 64.0 ** -0.5 * 32.0 ** 0.5
OUTW = 160
SLOT = 24
PART_SUM = NPAD
SRC_SUM = PART_SUM + SLOT * NBLK
ACT_GROUPS = 3
assert CB * CHUNKS == NBLK
assert NB * VB == NV and (NB - PEEL) % DEPTH == 0 and 3 * CH <= SLOT and SRC_SUM >= 7 * 512 and SRC_SUM + CH * NBLK <= 8 * 512


def gnn_program(nc, x, edge_ids, last_dst, edge_attrs, species, w1a, w1b, b1, w2, row_params, wlr, wup,
                wr1, wr2, wdn_a, wdn_b, wsk, out):
    ctx = ExitStack()
    with ctx:
        def sb(name, shape, dt=F32):
            return ctx.enter_context(nc.sbuf_tensor(name, shape, dt))

        def sem(name):
            return ctx.enter_context(nc.semaphore(name))

        def dram(name, shape, dt=F32):
            return nc.dram_tensor(name, shape, dt).ap()

        tables = [dram(f"table{i}", [NPAD, D]) for i in range(LAYERS + 2)]
        gathered_rows = dram("gathered_rows", [NB, P, VB * D])
        radial_hidden = dram("radial_hidden", [NB, 8 * VB, P])
        block_of_visit = dram("block_of_visit", [VG, P], I32)

        X = sb("X", [P, NBLK, D])
        H = sb("H", [P, NBLK, D])
        HT_AT = NV * 8 + NPAD + 136
        RX = sb("RX", [P, HT_AT + 2 * NV * HEADS + 80])
        HT = (RX, HT_AT)
        SCR = sb("SCR", [P, 7680])
        AT = sb("AT", [P, ROWS, NV + 1])
        EI = sb("EI", [P, 5, VW])
        G = sb("G", [P, DEPTH, VB, D])
        OH = sb("OH", [P, DEPTH, VB, P])
        dst_rows = sb("dst_rows", [P, VG, 3, P])
        invalid_neg = sb("invalid_neg", [P, VG, P])
        begins = sb("begins", [P, 4 * NT + 600])
        src_idx = sb("src_idx", [P, NV + 1], I32)
        gather_idx = sb("gather_idx", [P, DEPTH, VB], I32)
        block_words = sb("block_words", [1, NB], I32)
        ident = sb("ident", [P, P])
        ident_b = sb("ident_b", [P, P], BF16)
        iota_i = sb("iota_i", [P, P], I32)
        iota = sb("iota", [P, P])
        small = sb("small", [P, 8, NBLK])
        inv_deg = sb("inv_deg", [P, 2, NBLK])
        no_edges = sb("no_edges", [P, NBLK])
        self_score = sb("self_score", [P, NBLK, HEADS])
        node_max = sb("node_max", [P, NBLK, HEADS])
        self_prob = sb("self_prob", [P, NBLK, HEADS])
        means = sb("means", [P, NBLK, 32])
        tv = sb("tv", [P, 6, VG])
        tvi = sb("tvi", [P, VG], I32)
        vrow = sb("vrow", [4, P], I32)
        rowi = begins[0:1, 0:2 * NT + 600].bitcast(I32)
        rowf = begins[0:1, 2 * NT + 600:4 * NT + 600]
        ones_row = sb("ones_row", [1, P])
        w1a_s, w2_s, wup_s = (sb(n, [P, D]) for n in ("w1a_s", "w2_s", "wup_s"))
        w1b_s = sb("w1b_s", [32, D])
        b1_s = sb("b1_s", [P, 1])
        rows_s = sb("rows_s", [P, 5 * D])
        wlr_s = sb("wlr_s", [P, 2 * D])
        wr1_s = sb("wr1_s", [8 * VB, 8 * VB])
        wr2_s = sb("wr2_s", [8 * VB, VB, P])
        wdna_s, wdnb_s = sb("wdna_s", [P, 96]), sb("wdnb_s", [P, 64])
        PS = ctx.enter_context(nc.psum_tensor("PS", [P, 8, 512], F32))
        PSF = PS[:, :, :].rearrange("p a b -> p (a b)")

        def view(t, offset, dims, parts=P, dt=None):
            t, at = t if isinstance(t, tuple) else (t, 0)
            width = 1
            for n in t.shape[1:]:
                width *= n
            return bass.AP(t, offset + at, [[width, parts]] + [list(d) for d in dims])

        RES = view(RX, 0, [[D, NBLK], [1, D]])
        XR_W = D + HEADS
        XR = view(RX, 0, [[XR_W, NBLK], [1, XR_W]])
        PM = view(RX, 0, [[8, NV], [1, 8]])
        XL_AT = NV * 8 + 8
        XL = view(RX, XL_AT, [[D, NBLK], [1, D]])
        HTF = view(HT, 0, [[1, NPAD]])
        ES = view(HT, 0, [[HEADS, NV], [1, HEADS]])
        MS_AT = NV * HEADS
        MS = view(HT, MS_AT, [[HEADS, NV], [1, HEADS]])
        hid = view(RX, 0, [[1, NPAD]])

        def id_rows(g):
            return view(HT, g * 3 * P, [[1, 3 * P]]).bitcast(I32)

        FILLS = [(g, j) for g in range(VG) for j in range(2)] + [(g, j) for g in range(VG) for j in range(2, 9)]
        N_FILL = len(FILLS)
        ACT_FILLS = 18

        def on_dve(f):
            return f >= ACT_FILLS and f % 2 == 0

        def copies(f):
            n = sum(on_dve(i) == on_dve(f) for i in range(f + 1))
            return s("fill_copied_dve" if on_dve(f) else "fill_copied_act"), n

        def fill_copy(f):
            g, j = FILLS[f]
            n = 1 if j == 1 else 4
            if j < 2:
                w = P
                dst = view(EI, 4 * j * VW + g * P, [[VW, n], [1, w]])
            else:
                w = min(P, NV + 1 - g * P)
                row = (0, 4, 8, 12, SH, RAD, RAD + 4)[j - 2]
                dst = view(AT, row * (NV + 1) + g * P, [[NV + 1, n], [1, w]])
            return dst, view(PS, (2 + f % 6) * 512, [[P, n], [1, w]])

        def OHS(p):
            return view(SCR, p * VB * P, [[P, VB], [1, P]])

        PR_AT = DEPTH * VB * P
        AP_AT = PR_AT + DEPTH * VB * NBLK * 7
        AO_AT = AP_AT + DEPTH * VB * 3 * CH // 2 + 2
        AR_AT = AO_AT + DEPTH * VB * P // 2

        def attr_parts(p):
            return view((SCR, AP_AT), p * VB * 3 * CH // 2, [[1, VB * 3 * CH // 2]]).bitcast(BF16).rearrange("p (v n) -> p v n", v=VB)

        def OHA(p):
            return view(SCR, AO_AT + p * VB * P // 2, [[1, VB * P // 2]]).bitcast(BF16).rearrange("p (v n) -> p v n", v=VB)


        def OHB(p):
            return OH[:, p].rearrange("p a b -> p (a b)").bitcast(BF16)[:, 0:VB * P].rearrange("p (a b) -> p a b", a=VB)

        def ot_ps(p):
            return PS[:, p, :].bitcast(BF16)[:, 0:VB * P]

        OT_AT = 0
        Z_AT = DEPTH * VB * P
        L_AT = Z_AT + DEPTH * VB * D
        RS_AT = L_AT + VB * D
        RT_AT = RS_AT + 8 * VB
        RH_AT = RT_AT + P
        END_AT = 2 * NV * HEADS
        PARTS = 3 * 8
        PART_AT = 0
        OHW_AT = PART_AT + DEPTH * VB * PARTS // 2
        REST_AT = OHW_AT + DEPTH * VB * P // 2

        def parts(p):
            return view(SCR, PART_AT + p * VB * PARTS // 2, [[1, VB * PARTS // 2]]).bitcast(BF16).rearrange("p (v n) -> p v n", v=VB)

        def OHW(p):
            return view(SCR, OHW_AT + p * VB * P // 2, [[1, VB * P // 2]]).bitcast(BF16).rearrange("p (v n) -> p v n", v=VB)

        M_AT = 0
        C_AT = DEPTH * VB * MSG
        T_AT = C_AT + VB * C
        U_AT = T_AT + 3 * VB * C
        CH_AT = U_AT + VB * C
        W_AT = CH_AT + DEPTH * P
        AC_AT = NBLK * OUTW
        SPECIES_AT = 0
        SKIP_AT = SPECIES_AT + NPAD
        HM_AT = SKIP_AT + SPECIES * OUTW
        assert HM_AT + 2 * SPECIES * 2 * P <= SH * (NV + 1)

        S = {}

        def s(name):
            if name not in S:
                S[name] = sem(name)
            return S[name]

        block = ctx.enter_context(nc.Block())

        def batches(eng, body):
            for k in range(PEEL):
                body(k, k % DEPTH, k // DEPTH)
            with eng.Fori(1, (NB - PEEL) // DEPTH + 1) as j:
                for i in range(DEPTH):
                    k0 = PEEL - DEPTH + i
                    body(DEPTH * j + k0, k0 % DEPTH, j + k0 // DEPTH)

        uses = lambda p: (NB - 1 - p) // DEPTH + 1

        def before(p, m):
            return (p - 1, m) if p else (DEPTH - 1, m - 1)

        def late(k, n):
            return not (isinstance(k, int) and k < n)

        def written(n):
            return 16 * CHUNKS * n

        def gate(eng):
            eng.sem_inc(s("gates_passed"))

        def load_all(eng):
            for t, a in ((w1a_s, w1a), (w1b_s, w1b), (b1_s, b1), (w2_s, w2), (wlr_s, wlr), (wup_s, wup),
                         (wr1_s, wr1), (wr2_s, wr2), (wdna_s, wdn_a), (wdnb_s, wdn_b)):
                eng.dma_start(t[:], a).then_inc(s("weights_loaded"), 16)
            eng.dma_start(rows_s[:], row_params.partition_broadcast(P)).then_inc(s("weights_loaded"), 16)

        W_ALL = 11 * 16
        HALVES = ((0, 13), (13, NBLK))
        N16 = VG * HEADS * P
        MASK_AT, PRE_AT, SUF_AT = 0, N16 + 1, 2 * N16 + 1

        passes = ["sage0", "sage1", "sage2", "score", "conv"]

        @block.sync
        def _(sp):
            sp.dma_start(rowi[:, 0:NT], last_dst).then_inc(s("last_loaded"), 16)
            sp.wait_ge(s("x_tail_zeroed"), 1)
            sp.dma_start(X[:, 0:NBLK - 1, :], x[0:(NBLK - 1) * P, :].rearrange("(b p) d -> p b d", p=P)).then_inc(s("x_loaded"), 16)
            sp.dma_start(X[0:NODES - (NBLK - 1) * P, NBLK - 1, :], x[(NBLK - 1) * P:NODES, :]).then_inc(s("x_loaded"), 16)
            sp.wait_ge(s("blocks_turned"), 1)
            sp.dma_start(block_of_visit, vrow[:, 0:P]).then_inc(s("blocks_out"), 16)
            sp.wait_ge(s("blocks_out"), 16)
            sp.dma_start(rowi[:, 2 * NT:2 * NT + VW], block_of_visit.rearrange("g v -> (g v)").rearrange("(o n) -> o n", o=1)).then_inc(s("blocks_in"), 16)
            for i in range(LAYERS + 2):
                src = [H[:], H[:], H[:], XL, XL][i]
                for c in range(CHUNKS):
                    sp.wait_ge(s("table_ready"), CHUNKS * i + c + 1)
                    sp.dma_start(tables[i][c * CB * P:(c + 1) * CB * P, :].rearrange("(b p) d -> p b d", p=P),
                                 src[:, c * CB:(c + 1) * CB]).then_inc(s("table_written"), 16)
                if i == LAYERS:
                    sp.wait_ge(s("sage2_rows_used"), NB)
                    sp.dma_start(view(AT, SPECIES_AT, [[1, NPAD]]).bitcast(I32), species.partition_broadcast(P)).then_inc(s("species_loaded"), 16)
                    sp.dma_start(view(AT, SKIP_AT, [[1, SPECIES * OUTW]]), wsk).then_inc(s("species_loaded"), 16)

                    def store(k, p, m):
                        sp.wait_ge(s(f"score_gathered{p}"), 16 * VB * (m + 1))
                        sp.dma_start(gathered_rows[bass.ds(k, 1)].rearrange("o p n -> p (o n)"),
                                     G[:, p].rearrange("p a b -> p (a b)")).then_inc(s(f"rows_stored{p}"), 16)
                        sp.wait_ge(s("radial_hidden_ready"), k + 1)
                        sp.dma_start(radial_hidden[bass.ds(k, 1)].rearrange("o p n -> p (o n)"),
                                     view(SCR, RH_AT + p * P, [[1, P]], 8 * VB)).then_inc(s(f"hidden_stored{p}"), 16)
                    batches(sp, store)
                    for p in range(DEPTH):
                        n = uses(p)
                        sp.wait_ge(s(f"rows_stored{p}"), 16 * n)
                        sp.wait_ge(s(f"hidden_stored{p}"), 16 * n)

                    sp.wait_ge(s("probs_ready"), 1)
                    sp.wait_ge(s("maxima_placed"), 1)

                    def load(k, p, m):
                        if late(k, DEPTH):
                            sp.wait_ge(s("sum_hot"), k - DEPTH + 1)
                        sp.dma_start(view(HT, p * VB * D, [[1, VB * D]]),
                                     gathered_rows[bass.ds(k, 1)].rearrange("o p n -> p (o n)")).then_inc(s(f"rows_back{p}"), 16)
                    batches(sp, load)
                if i == LAYERS + 1:
                    def load_hidden(k, p, m):
                        if late(k, DEPTH):
                            sp.wait_ge(s("conv_weights_made"), k - DEPTH + 1)
                        sp.dma_start(view(SCR, CH_AT + p * P, [[1, P]], 8 * VB),
                                     radial_hidden[bass.ds(k, 1)].rearrange("o p n -> p (o n)")).then_inc(s(f"hidden_back{p}"), 16)
                    batches(sp, load_hidden)
            for half, (b0, b1) in enumerate(HALVES):
                b1 = min(b1, NBLK - 1)
                sp.wait_ge(s("result_ready"), half + 1)
                sp.dma_start(out[b0 * P:b1 * P, :].rearrange("(b p) d -> p b d", p=P), X[:, b0:b1, :]).then_inc(s("out_written"), 16)
            sp.dma_start(out[(NBLK - 1) * P:NODES, :], X[0:NODES - (NBLK - 1) * P, NBLK - 1, :]).then_inc(s("out_written"), 16)
            sp.wait_ge(s("out_written"), 48)
            sp.wait_ge(s("table_written"), written(LAYERS + 2))

        @block.gpsimd
        def _(pool):
            pool.memset(X[:, NBLK - 1, :], 0.0).then_inc(s("x_tail_zeroed"), 1)
            pool.iota(iota_i[:], pattern=[[1, P]], base=0, channel_multiplier=0).then_inc(s("iota_made"), 1)
            pool.iota(tvi[:], pattern=[[P, VG]], base=0, channel_multiplier=1).then_inc(s("iota_made"), 1)
            pool.iota(rowi[:, NT:2 * NT], pattern=[[1, NT]], base=0, channel_multiplier=0).then_inc(s("iota_made"), 1)
            pool.memset(ident[:], 0.0).then_inc(s("ident_zeroed"), 1)
            pool.memset(ones_row[:], 1.0).then_inc(s("ones_made"), 1)
            pool.memset(AT[:, 16:18, :], 1.0).then_inc(s("ones_made"), 1)
            pool.wait_ge(s("ident_zeroed"), 1)
            pool.affine_select(out=ident[:], in_=ident[:], compare_op=ALU.not_equal, fill=1.0, base=0,
                               pattern=[[-1, P]], channel_multiplier=1).then_inc(s("ident_made"), 1)
            pool.wait_ge(s("tiles_found"), 1)
            for g in range(VG):
                at = bass.IndirectOffsetOnAxis(ap=tvi[:, g:g + 1], axis=0)
                pool.indirect_dma_start(id_rows(g), None, edge_ids, at).then_inc(s(f"ids_in{g}"), 16)
            for g in range(VG):
                at = bass.IndirectOffsetOnAxis(ap=tvi[:, g:g + 1], axis=0)
                if g >= 2:
                    pool.wait_ge(s("fill_turned"), 2 * VG + 7 * (g - 1))
                pool.indirect_dma_start(view(SCR, (g % 2) * N_ATTR * P, [[1, N_ATTR * P]]), None, edge_attrs, at).then_inc(s(f"attrs_in{g}"), 16)

            def split_all():
                pool.wait_ge(s("probs_ready"), 1)
                pool.wait_ge(s("maxima_placed"), 1)

                def split(k, p, m):
                    step = [pool.snap(4 * k + i + 1) if late(k, PEEL) else 4 * k + i + 1 for i in range(4)]
                    pm = view(RX, 8 * VB * k, [[8, VB], [1, 8]])
                    rest = view(SCR, REST_AT + p * VB * 8, [[8, VB], [1, 8]])
                    if late(k, DEPTH):
                        pool.wait_ge(s("sum_done"), k - DEPTH + 1)
                        gate(pool)
                    pool.tensor_copy(parts(p)[:, :, 0:8], pm).then_inc(s("split_step"), 1)
                    pool.wait_ge(s("split_step"), step[0])
                    gate(pool)
                    gate(pool)
                    pool.tensor_tensor(rest, pm, parts(p)[:, :, 0:8], ALU.subtract).then_inc(s("split_step"), 1)
                    pool.wait_ge(s("split_step"), step[1])
                    gate(pool)
                    pool.tensor_copy(parts(p)[:, :, 8:16], rest).then_inc(s("split_step"), 1)
                    pool.wait_ge(s("split_step"), step[2])
                    gate(pool)
                    pool.tensor_tensor(rest, rest, parts(p)[:, :, 8:16], ALU.subtract).then_inc(s("split_step"), 1)
                    pool.wait_ge(s("split_step"), step[3])
                    gate(pool)
                    pool.tensor_copy(parts(p)[:, :, 16:24], rest).then_inc(s("parts_made"), 1)
                batches(pool, split)

            for i, name in enumerate(passes):
                pool.wait_ge(s("table_written"), written(i + 1))

                def gather(k, p, m):
                    pool.wait_ge(s(f"{name}_idx_ready"), k + 1)
                    gate(pool)
                    if late(k, DEPTH):
                        pool.wait_ge(s({"score": "z_read", "conv": "messages_ready"}.get(name, f"{name}_rows_used")), k - DEPTH + 1)
                        gate(pool)
                        if name == "score":
                            pool.wait_ge(s(f"rows_stored{p}"), 16 * m)
                            gate(pool)
                    for q in range(VB):
                        pool.indirect_dma_start(G[:, p, q, :], None, tables[i],
                                                bass.IndirectOffsetOnAxis(ap=gather_idx[:, p, q:q + 1], axis=0)
                                                ).then_inc(s(f"{name}_gathered{p}"), 16)
                batches(pool, gather)

                if name == "score":
                    pool.wait_ge(s("species_loaded"), 32)
                    pool.tensor_copy(view(AT, SPECIES_AT, [[1, NPAD]]), view(AT, SPECIES_AT, [[1, NPAD]]).bitcast(I32)).then_inc(s("species_ready"), 1)
                    split_all()

        @block.scalar
        def _(act):
            load_all(act)

            def norm_part(n):
                act.wait_ge(s("var_ready"), n + 1)
                act.activation(small[:, 4, :], small[:, 3, :], ACT.Sqrt).then_inc(s("std_ready"), 1)
                act.wait_ge(s("norm_scales"), n + 1)
                for b in range(4 * ACT_GROUPS):
                    ins = act.activation(H[:, b, :], X[:, b, :], ACT.Relu, bias=small[:, 2, b:b + 1], scale=small[:, 5, b:b + 1])
                    if b % 4 == 3:
                        ins.then_inc(s("normed_act"), 1)

            def copy_idx(name, k, p, m):
                if late(k, DEPTH):
                    act.wait_ge(s(f"{name}_gathered{p}"), 16 * VB * m)
                    gate(act)
                act.copy(gather_idx[:, p, :], src_idx[:, bass.ds(VB * k, VB)]).then_inc(s(f"{name}_idx_ready"), 1)

            for f in range(N_FILL):
                if f == ACT_FILLS:
                    norm_part(0)
                if not on_dve(f):
                    act.wait_ge(s("fill_turned"), f + 1)
                    dst, src = fill_copy(f)
                    act.copy(dst, src).then_inc(s("fill_copied_act"), 1)

            act.wait_ge(s("idx_made"), 1)
            for i, name in enumerate(passes[:LAYERS]):
                if i:
                    act.wait_ge(s(f"{passes[i - 1]}_rows_used"), NB)

                def idx(k, p, m):
                    copy_idx(name, k, p, m)
                    act.wait_ge(s(f"{name}_hot"), k + 1)
                    act.copy(OHA(p), OH[:, p]).then_inc(s(f"{name}_hot_bf16"), 1)
                batches(act, idx)
            for g in range(7):
                w = min(4, NBLK - 4 * g) * P
                act.wait_ge(s("means_turned"), g + 1)
                act.copy(view(SCR, g * 512, [[1, w]], 32), PS[0:32, g % 2, 0:w]).then_inc(s("mt_ready"), 1)
            norm_part(1)
            act.wait_ge(s("weights_loaded"), W_ALL)
            for g in range(7):
                w = min(4, NBLK - 4 * g) * P
                act.wait_ge(s("hidden_made"), g + 1)
                act.activation(hid[:, g * 512:g * 512 + w], PS[:, 2 + g % 2, 0:w], ACT.Identity, bias=b1_s[:, 0:1]).then_inc(s("hidden_biased"), 1)
            norm_part(2)
            for g in range(7):
                w = min(4, NBLK - 4 * g)
                act.wait_ge(s("xr_made"), g + 1)
                act.copy(XR[:, 4 * g:4 * g + w, 0:D], PS[:, 2 * (g % 3) + 1, 0:w * P].rearrange("p (b d) -> p b d", b=w)).then_inc(s("xr_copied"), 1)

            def score(k, p, m):
                copy_idx("score", k, p, m)
                if late(k, 1):
                    act.wait_ge(s("radial_turned"), k)
                    gate(act)
                act.copy(view(SCR, RS_AT, [[VB, 8], [1, VB]]), AT[:, RAD:RAD + 8, bass.ds(VB * k, VB)]).then_inc(s("radial_ready"), 1)
                act.wait_ge(s("oh_turned"), k + 1)
                if late(k, DEPTH):
                    act.wait_ge(s("z_made"), k - DEPTH + 1)
                act.copy(view(SCR, OT_AT + p * VB * P, [[1, VB * P]]), ot_ps(p)).then_inc(s("ot_ready"), 1)
                act.wait_ge(s("radial_turned"), k + 1)
                act.copy(view(SCR, RT_AT, [[1, P]], 8 * VB), PS[0:8 * VB, 7, 0:P]).then_inc(s("radial_t_ready"), 1)
                act.wait_ge(s("hidden_pre_made"), k + 1)
                if late(k, DEPTH):
                    act.wait_ge(s(f"hidden_stored{p}"), 16 * m)
                act.activation(view(SCR, RH_AT + p * P, [[1, P]], 8 * VB), PS[0:8 * VB, 7, 256:256 + P], ACT.Silu,
                               scale=8.0 ** -0.5).then_inc(s("radial_hidden_ready"), 1)

            batches(act, score)

            act.wait_ge(s("below_max"), 1)
            act.activation(PM[:, :, 0:HEADS], ES, ACT.Exp).then_inc(s("probs_ready"), 1)
            def hot_in_bf16(k, p, m):
                act.wait_ge(s("parts_made"), k + 1)
                act.wait_ge(s("sum_hot"), k + 1)
                act.copy(OHW(p), OH[:, p]).then_inc(s("sum_hot_bf16"), 1)
            batches(act, hot_in_bf16)
            act.wait_ge(s("self_below_max"), 1)
            act.activation(self_prob[:], self_prob[:], ACT.Exp).then_inc(s("self_prob_ready"), 1)
            for half, (b0, b1) in enumerate(HALVES):
                act.wait_ge(s("elu_arg"), half + 1)
                act.activation(H[:, b0:b1, :], H[:, b0:b1, :], ACT.Exp).then_inc(s("elu_exp"), 1)
            norm_part(3)

            def conv(k, p, m):
                copy_idx("conv", k, p, m)
                if late(k, 1):
                    weights_and_hot(k - 1, before(p, m)[0])

            def weights_and_hot(k, p):
                act.wait_ge(s("conv_weights_made"), k + 1)
                act.copy(view(SCR, W_AT + p * VB * P, [[1, VB * P]]), view(PS, 5 * 512, [[1, VB * P]])).then_inc(s("conv_weights"), 1)
                if late(k, DEPTH):
                    act.wait_ge(s("message_sums"), VB * (k - DEPTH + 1))
                    gate(act)
                for q in range(VB):
                    ins = act.activation(OH[:, p, q, :], iota[:], ACT.Abs, bias=view(EI, 3 * VW + VB * k + q, [[1, 1]]), scale=-1.0)
                ins.then_inc(s("conv_distance"), 1)
                act.wait_ge(s("conv_distance"), k + 1)
                oh = OH[:, p].rearrange("p a b -> p (a b)")
                act.activation(oh, oh, ACT.Relu, bias=1.0, scale=-1.0).then_inc(s("conv_hot"), 1)
            batches(act, conv)
            weights_and_hot(NB - 1, LAST[0])
            def gate_part(half):
                b0, b1 = HALVES[half]
                gates = view(SCR, b0 * OUTW, [[OUTW, b1 - b0], [1, 64]])
                act.wait_ge(s("update_ready"), half + 1)
                act.activation(gates, gates, ACT.Silu).then_inc(s("gates_ready"), 1)

            for b in range(NBLK):
                act.wait_ge(s("acc_turned"), b + 1)
                if b >= 4:
                    act.wait_ge(s("update_made"), b - 3)
                act.activation(view(SCR, AC_AT + (b % 4) * 256, [[1, 256]]), PS[:, b % 4, 0:256], ACT.Copy, scale=SUM_SCALE).then_inc(s("final_copied"), 1)
                if b == HALVES[0][1] + 1:
                    gate_part(0)
            gate_part(1)

        @block.vector
        def _(dve):
            steps = [0]

            def done(ins):
                steps[0] += 1
                ins.then_inc(s("dve_step"), 1)
                dve.wait_ge(s("dve_step"), steps[0])

            def norm(n):
                stats = view(RX, XL_AT, [[6, NBLK], [1, 6]])
                mean_var = view(RX, XL_AT + 6 * NBLK, [[2, NBLK], [1, 2]])
                for b in range(NBLK):
                    ins = dve.bn_stats(stats[:, b], X[:, b, :])
                done(ins)
                for b in range(NBLK):
                    ins = dve.bn_aggr(mean_var[:, b], stats[:, b])
                done(ins)
                dve.tensor_scalar(small[:, 3, :], mean_var[:, :, 1], LN_EPS, None, ALU.add).then_inc(s("var_ready"), 1)
                dve.wait_ge(s("std_ready"), n + 1)
                done(dve.reciprocal(small[:, 5, :], small[:, 4, :]))
                dve.scalar_tensor_tensor(small[:, 2, :], mean_var[:, :, 0], -1.0, small[:, 5, :], ALU.mult, ALU.mult).then_inc(s("norm_scales"), 1)
                for b in range(4 * ACT_GROUPS, NBLK):
                    ins = dve.tensor_scalar(H[:, b, :], X[:, b, :], mean_var[:, b, 0:1], small[:, 5, b:b + 1], ALU.subtract, ALU.mult)
                done(ins)
                rest = H[:, 4 * ACT_GROUPS:NBLK, :]
                dve.tensor_scalar(rest, rest, 0.0, None, ALU.max).then_inc(s("normed_dve"), 1)

            def turned_h(n):
                for g in range(7):
                    w = min(4, NBLK - 4 * g) * P
                    dve.wait_ge(s("h_turned"), 7 * n + g + 1)
                    dve.tensor_copy(HTF[:, g * 512:g * 512 + w], PSF[:, g * 512:g * 512 + w]).then_inc(s("ht_ready"), 1)

            dve.wait_ge(s("iota_made"), 3)
            dve.tensor_copy(iota[:], iota_i[:])
            dve.wait_ge(s("ident_made"), 1)
            dve.tensor_copy(ident_b[:], ident[:])
            dve.tensor_copy(tv[:, 0, :], tvi[:])
            done(dve.tensor_copy(rowf[:, NT:2 * NT], rowi[:, NT:2 * NT]))
            dve.wait_ge(s("last_loaded"), 16)
            done(dve.tensor_scalar(rowi[:, 0:NT], rowi[:, 0:NT], 7, None, ALU.arith_shift_right))
            done(dve.tensor_copy(rowf[:, 0:NT], rowi[:, 0:NT]))
            dve.tensor_tensor(rowf[:, 0:NT], rowf[:, 0:NT], rowf[:, NT:2 * NT], ALU.add).then_inc(s("ends_ready"), 1)
            dve.wait_ge(s("ends_spread"), 1)
            for g in range(VG):
                done(dve.tensor_scalar(H[:, g * 4:g * 4 + 4, :].rearrange("p a b -> p (a b)")[:, 0:NT], PS[:, 0, 0:NT], tv[:, 0, g:g + 1], None, ALU.is_lt))
                done(dve.tensor_reduce(tv[:, 1, g:g + 1], H[:, g * 4:g * 4 + 4, :].rearrange("p a b -> p (a b)")[:, 0:NT], AX, ALU.add))
            done(dve.tensor_scalar(tv[:, 2, :], tv[:, 1, :], float(NT - 1), None, ALU.min))
            dve.tensor_copy(tvi[:], tv[:, 2, :]).then_inc(s("tiles_found"), 1)
            done(dve.tensor_tensor(tv[:, 3, :], tv[:, 0, :], tv[:, 2, :], ALU.subtract))
            done(dve.tensor_scalar(tv[:, 4, :], tv[:, 3, :], float(NBLK - 1), None, ALU.min))
            dve.tensor_scalar(tv[:, 5, :], tv[:, 4, :], -float(P), None, ALU.mult).then_inc(s("blocks_ready"), 1)
            dve.wait_ge(s("blocks_in_psum"), 1)
            dve.tensor_copy(vrow[:, 0:P], PS[0:4, 1, 0:P]).then_inc(s("blocks_turned"), 1)
            dve.wait_ge(s("blocks_in"), 16)
            B0 = 2 * NT
            done(dve.tensor_copy(block_words[:], view(begins, B0, [[VB, NB]], 1).bitcast(I32)))
            for q in range(1, VB):
                done(dve.tensor_scalar(rowi[:, 0:NB], view(begins, B0 + q, [[VB, NB]], 1).bitcast(I32), 5 * q, None, ALU.logical_shift_left))
                done(dve.tensor_tensor(block_words[:], block_words[:], rowi[:, 0:NB], ALU.bitwise_or))
            for g in range(VG):
                dve.wait_ge(s(f"ids_in{g}"), 16)
                dr = dst_rows[:, g]
                idr = id_rows(g)
                done(dve.tensor_copy(dr.rearrange("p a b -> p (a b)"), idr))
                st = [view(RX, (5 * g + i) * P, [[1, P]]) for i in range(5)]
                dve.tensor_copy(st[0], dr[:, 0])
                dve.tensor_scalar(view(HT, 1536, [[1, P]]).bitcast(I32), idr[:, 0:P], 7, None, ALU.arith_shift_right)
                dve.tensor_scalar(view(HT, 1664, [[1, P]]).bitcast(I32), idr[:, 0:P], 127, None, ALU.bitwise_and)
                done(dve.tensor_scalar(st[3], dr[:, 1], tv[:, 5, g:g + 1], None, ALU.add))
                va, vb, vc = (view(HT, 1792 + 128 * i, [[1, P]]) for i in range(3))
                dve.tensor_copy(st[2], view(HT, 1664, [[1, P]]).bitcast(I32))
                dve.tensor_copy(vc, view(HT, 1536, [[1, P]]).bitcast(I32))
                done(dve.tensor_scalar(va, st[3], 0.0, None, ALU.is_ge))
                done(dve.scalar_tensor_tensor(vb, st[3], float(P - 1), va, ALU.is_le, ALU.mult))
                done(dve.scalar_tensor_tensor(vc, vb, -64.0, vc, ALU.mult, ALU.add))
                dve.tensor_scalar(st[1], vc, 64.0, None, ALU.add)
                dve.tensor_scalar(invalid_neg[:, g, :], vb, 1.0, BIG, ALU.subtract, ALU.mult)
                done(dve.tensor_tensor(va, dr[:, 1], dr[:, 2], ALU.not_equal))
                dve.tensor_tensor(st[4], va, vb, ALU.mult).then_inc(s("kinds_ready"), 1)
            dve.wait_ge(s("x_loaded"), 32)
            norm(0)
            dve.wait_ge(s("fill_copied_act"), 2 * VG)
            dve.tensor_copy(src_idx[:], EI[:, 0, 0:NV + 1]).then_inc(s("idx_made"), 1)
            dve.wait_ge(s("normed_dve"), 1)
            dve.wait_ge(s("normed_act"), ACT_GROUPS)
            dve.memset(small[:, 6, :], 0.0).then_inc(s("table_ready"), CHUNKS)
            dve.wait_ge(s("table_ready"), CHUNKS)
            for f in range(N_FILL):
                if on_dve(f):
                    dve.wait_ge(s("fill_turned"), f + 1)
                    dst, src = fill_copy(f)
                    dve.tensor_copy(dst, src).then_inc(s("fill_copied_dve"), 1)
            for f in (N_FILL - 2, N_FILL - 1):
                dve.wait_ge(*copies(f))
            done(dve.tensor_copy(RES, H[:]))
            dve.wait_ge(s("ones_made"), 2)

            def one_hot(dst, kind, k):
                return dve.tensor_tensor(dst, view(iota, 0, [[0, VB], [1, P]]), view(EI, kind * VW + VB * k, [[1, VB], [0, P]]), ALU.is_equal)

            for i in range(LAYERS):
                name = passes[i]
                r0 = 12 - CH * i
                dve.memset(PSF, 0.0).then_inc(s("sums_zeroed"), 1)

                def hot(k, p, m):
                    if late(k, DEPTH):
                        dve.wait_ge(s(f"{name}_rows_used"), k - DEPTH + 1)
                    sbh = view(SCR, PR_AT + p * VB * NBLK * 7, [[NBLK, VB], [1, NBLK]])
                    prod = view(SCR, PR_AT + p * VB * NBLK * 7 + VB * NBLK, [[NBLK * CH, VB], [CH, NBLK], [1, CH]])
                    dve.tensor_tensor(sbh, view(iota, 0, [[0, VB], [1, NBLK]]), view(EI, VW + VB * k, [[1, VB], [0, NBLK]]), ALU.is_equal).then_inc(s(f"{name}_src_block"), 1)
                    attrs = view(AT, r0 * (NV + 1) + VB * k, [[1, VB], [NV + 1, CH]])
                    rest = view(SCR, AR_AT + p * VB * CH, [[CH, VB], [1, CH]])
                    part = lambda j: attr_parts(p)[:, :, j * CH:(j + 1) * CH]
                    dve.tensor_copy(part(0), attrs).then_inc(s("attrs_split"), 1)
                    one_hot(OH[:, p], 3, k)
                    dve.wait_ge(s("attrs_split"), 4 * NB * i + 4 * k + 1)
                    gate(dve)
                    dve.tensor_tensor(rest, attrs, part(0), ALU.subtract).then_inc(s("attrs_split"), 1)
                    one_hot(OHS(p), 2, k)
                    dve.wait_ge(s("attrs_split"), 4 * NB * i + 4 * k + 2)
                    dve.tensor_copy(part(1), rest).then_inc(s("attrs_split"), 1)
                    dve.wait_ge(s(f"{name}_src_block"), k + 1)
                    dve.tensor_tensor(prod, view(SCR, PR_AT + p * VB * NBLK * 7, [[NBLK, VB], [1, NBLK], [0, CH]]),
                                      view(AT, r0 * (NV + 1) + VB * k, [[1, VB], [0, NBLK], [NV + 1, CH]]), ALU.mult)
                    dve.wait_ge(s("attrs_split"), 4 * NB * i + 4 * k + 3)
                    dve.tensor_tensor(rest, rest, part(1), ALU.subtract).then_inc(s("attrs_split"), 1)
                    dve.wait_ge(s("attrs_split"), 4 * NB * i + 4 * k + 4)
                    dve.tensor_copy(part(2), rest).then_inc(s(f"{name}_hot"), 1)
                batches(dve, hot)
                dve.wait_ge(s(f"{name}_rows_used"), NB)
                by_src = view(PS, SRC_SUM, [[CH, NBLK], [1, CH]])
                by_dst = view(PS, PART_SUM, [[SLOT, NBLK], [CH, 3], [1, CH]])
                n = min(CH, 16 - r0)
                if i == 0:
                    for side, counts in enumerate((by_src[:, :, 4], by_dst[:, :, 0, 4])):
                        done(dve.tensor_scalar(small[:, side, :], counts, 1.0, None, ALU.max))
                        done(dve.reciprocal(inv_deg[:, side, :], small[:, side, :]))
                    dve.tensor_scalar(no_edges[:], by_dst[:, :, 0, 4], 0.5, None, ALU.is_lt)
                dve.wait_ge(s("table_written"), written(i + 1))
                for b in range(NBLK):
                    ins = dve.scalar_tensor_tensor(H[:, b, :], PSF[:, b * D:(b + 1) * D], inv_deg[:, 1, b:b + 1], H[:, b, :], ALU.mult, ALU.add)
                    if i < LAYERS - 1 and b % CB == CB - 1:
                        ins.then_inc(s("table_ready"), 1)
                if i < LAYERS - 1:
                    dve.wait_ge(s("table_ready"), CHUNKS * (i + 2))
                else:
                    done(ins)
                dve.tensor_copy(means[:, :, r0:r0 + n], by_src[:, :, 0:n])
                dst_means = means[:, :, 16 + r0:16 + r0 + n]
                done(dve.tensor_copy(dst_means, by_dst[:, :, 0, 0:n]))
                done(dve.tensor_tensor(dst_means, dst_means, by_dst[:, :, 1, 0:n], ALU.add))
                done(dve.tensor_tensor(dst_means, dst_means, by_dst[:, :, 2, 0:n], ALU.add))
                done(dve.scalar_tensor_tensor(RES, H[:], 1.0 / (1.0 + i), RES, ALU.mult, ALU.add))
            done(dve.tensor_tensor(X[:], X[:], RES, ALU.add))

            done(dve.tensor_tensor(means[:, :, 0:16], means[:, :, 0:16], view(inv_deg, 0, [[1, NBLK], [0, 16]]), ALU.mult))
            dve.tensor_tensor(means[:, :, 16:32], means[:, :, 16:32], view(inv_deg, NBLK, [[1, NBLK], [0, 16]]), ALU.mult).then_inc(s("means_ready"), 1)
            norm(1)
            turned_h(0)
            dve.wait_ge(s("weights_loaded"), W_ALL)
            row = lambda i: rows_s[:, i * D:(i + 1) * D]
            dve.tensor_tensor(row(3), row(3), row(4), ALU.add)
            dve.tensor_tensor(row(2), row(2), row(4), ALU.subtract)
            done(dve.tensor_tensor(X[:], X[:], view(rows_s, 0, [[0, NBLK], [1, D]]), ALU.add))
            for g in range(7):
                w = min(4, NBLK - 4 * g) * P
                dve.wait_ge(s("hidden_biased"), g + 1)
                hg = hid[:, g * 512:g * 512 + w]
                dve.scalar_tensor_tensor(hg, hg, 0.01, hg, ALU.mult, ALU.max).then_inc(s("hidden_ready"), 1)
            for g in range(7):
                w = min(4, NBLK - 4 * g)
                dve.wait_ge(s("mlp_made"), g + 1)
                xg = view(X, g * 512, [[1, w * P]])
                ins = dve.tensor_tensor(xg, xg, PS[:, 4 + g % 2, 0:w * P], ALU.add)
                ins.then_inc(s("mlp_added"), 1)
            dve.wait_ge(s("mlp_added"), 7)

            norm(2)
            turned_h(1)
            for g in range(7):
                w = min(4, NBLK - 4 * g)
                dve.wait_ge(s("xl_made"), g + 1)
                dve.tensor_tensor(XL[:, 4 * g:4 * g + w, :], PS[:, 2 * (g % 3), 0:w * P].rearrange("p (b d) -> p b d", b=w),
                                  view(rows_s, 3 * D, [[0, w], [1, D]]), ALU.add).then_inc(s("xl_copied"), 1)
                if (4 * g + w) // CB > 4 * g // CB:
                    dve.wait_ge(s("xl_copied"), g + 1)
                    dve.memset(small[:, 6, :], 0.0).then_inc(s("table_ready"), 1)
            dve.wait_ge(s("xl_copied"), 7)
            dve.wait_ge(s("xr_copied"), 7)
            done(dve.tensor_tensor(H[:], XL, XR[:, :, 0:D], ALU.add))
            done(dve.scalar_tensor_tensor(H[:], H[:], 0.2, H[:], ALU.mult, ALU.max))
            done(dve.tensor_tensor(H[:], H[:], view(rows_s, D, [[0, NBLK], [1, D]]), ALU.mult))
            done(dve.tensor_reduce(self_score[:], H[:].rearrange("p b (h c) -> p b h c", h=HEADS), AX, ALU.add))
            dve.tensor_copy(XR[:, :, D:XR_W], self_score[:]).then_inc(s("xr_ready"), 1)

            def score(k, p, m):
                if late(k, DEPTH):
                    dve.wait_ge(s("oh_turned"), k - DEPTH + 1)
                one_hot(OHB(p), 3, k).then_inc(s("score_hot"), 1)
                if not late(k, VG):
                    begin(k)
                if late(k, 2):
                    rate(k - 2, *before(*before(p, m)))

            def begin(g):
                if g == 0:
                    dve.memset(view(H, (VG - 1) * HEADS * P, [[1, HEADS * P]]), -BIG)
                    done(dve.memset(begins[:, 0:VG * HEADS * P + 1], -BIG))
                inner = view(begins, g * HEADS * P + 1, [[P, HEADS], [1, P - 1]])
                done(dve.tensor_tensor(inner, view(dst_rows, (3 * g + 1) * P + 1, [[0, HEADS], [1, P - 1]]),
                                       view(dst_rows, (3 * g + 1) * P, [[0, HEADS], [1, P - 1]]), ALU.not_equal))
                done(dve.tensor_scalar(inner, inner, -BIG, None, ALU.mult))

            def rate(k, p, m):
                z_at = Z_AT + p * VB * D
                dve.wait_ge(s(f"score_gathered{p}"), 16 * VB * (m + 1))
                dve.wait_ge(s("z_made"), k + 1)
                dve.tensor_scalar(view(HT, MS_AT + VB * HEADS * k, [[HEADS, VB], [1, HEADS]]),
                                  view(PS, 4 * 512 + D, [[256, VB], [1, HEADS]]), 0.0, None, ALU.add)
                dve.tensor_tensor(view(SCR, z_at, [[D, VB], [1, D]]), view(PS, 4 * 512, [[256, VB], [1, D]]), G[:, p], ALU.add).then_inc(s("z_read"), 1)
                dve.wait_ge(s("z_read"), k + 1)
                zz = view(SCR, z_at, [[1, VB * D]])
                ll = view(SCR, L_AT, [[1, VB * D]])
                dve.scalar_tensor_tensor(ll, zz, 0.2, zz, ALU.mult, ALU.max).then_inc(s("leaky"), 1)
                dve.wait_ge(s("leaky"), k + 1)
                dve.tensor_tensor(view(SCR, L_AT, [[D, VB], [1, D]]), view(SCR, L_AT, [[D, VB], [1, D]]),
                                  view(rows_s, D, [[0, VB], [1, D]]), ALU.mult).then_inc(s("weighed"), 1)
                dve.wait_ge(s("weighed"), k + 1)
                gate(dve)
                dve.tensor_reduce(view(HT, VB * HEADS * k, [[1, VB * HEADS]]), view(SCR, L_AT, [[C, VB * HEADS], [1, C]]),
                                  AX, ALU.add).then_inc(s("scored"), 1)
            batches(dve, score)
            for k, buf in ((NB - 2, before(*LAST)), (NB - 1, LAST)):
                dve.wait_ge(s("scored"), k)
                rate(k, *buf)
            dve.wait_ge(s("scored"), NB)

            flat = lambda t, at, step=1: view(t, at + (N16 - 1 if step < 0 else 0), [[step, N16]])
            dve.wait_ge(s("scores_turned"), 1)
            for g in range(VG):
                w = WG[g]
                ins = dve.tensor_tensor(view(H, g * HEADS * P, [[P, HEADS], [1, P]], w), view(PS, g * 512, [[P, HEADS], [1, P]], w),
                                        view(invalid_neg, g * P, [[0, HEADS], [1, P]], w), ALU.add)
            done(ins)
            for p in range(DEPTH):
                dve.wait_ge(s(f"hidden_stored{p}"), 16 * uses(p))
            dve.tensor_tensor_scan(flat(SCR, PRE_AT), flat(begins, 0), flat(H, 0), -BIG, ALU.add, ALU.max)
            done(dve.tensor_tensor_scan(flat(SCR, SUF_AT, -1), flat(begins, 1, -1), flat(H, 0, -1), -BIG, ALU.add, ALU.max))
            for g in range(VG):
                dve.tensor_copy(view(HT, END_AT + (0 * VG + g) * 4, [[1, 4]]), view(SCR, PRE_AT + g * 512 + P - 1, [[P, 4]]))
                dve.tensor_copy(view(HT, END_AT + (1 * VG + g) * 4, [[1, 4]]), view(SCR, SUF_AT + g * 512, [[P, 4]]))
                dve.tensor_copy(view(HT, END_AT + (2 * VG + g) * 4, [[1, 4]]), view(dst_rows, g * 3 * P + P, [[0, 4]]))
                ins = dve.tensor_copy(view(HT, END_AT + (3 * VG + g) * 4, [[1, 4]]), view(dst_rows, g * 3 * P + 2 * P - 1, [[0, 4]]))
            ins.then_inc(s("ends_made"), 1)
            dve.memset(PS[:, 5:8, :], 0.0)
            for side in range(2):
                for g in range(VG):
                    dve.tensor_scalar(view(SCR, MASK_AT + (side * VG + g) * P, [[1, P]]), view(dst_rows, g * 3 * P + P, [[1, P]]),
                                      view(dst_rows, g * 3 * P + (P, 2 * P - 1)[side], [[1, 1]]), -BIG, ALU.not_equal, ALU.mult)
            dve.wait_ge(s("ends_turned"), 1)
            R = lambda i, at=0, n=NV, step=1: view(H, i * VW + at, [[step, n]], 4)
            for i in range(4):
                ins = dve.tensor_copy(R(i), PS[0:4, i, 0:NV])
            done(ins)
            A = lambda i, at=0, n=NV, step=1: view(RX, i * VW + at, [[step, n]], 4)
            dve.memset(A(0, 0, 1), 1.0)
            done(dve.memset(view(RX, NV, [[VW, 4], [1, 1]], 4), 1.0))
            dve.tensor_tensor(A(0, 1, NV - 1), R(2, 1, NV - 1), R(3, 0, NV - 1), ALU.not_equal)
            done(dve.tensor_tensor(A(1), R(2), R(3), ALU.not_equal))
            dve.tensor_tensor(A(2), A(0), A(1), ALU.max)
            done(dve.tensor_tensor(A(3), A(0, 1), A(1), ALU.max))
            done(dve.tensor_scalar(view(RX, 0, [[VW, 4], [1, NV + 1]], 4), view(RX, 0, [[VW, 4], [1, NV + 1]], 4), -BIG, None, ALU.mult))
            dve.tensor_tensor_scan(A(4), A(2), R(0), -BIG, ALU.add, ALU.max)
            done(dve.tensor_tensor_scan(A(5, NV - 1, NV, -1), A(3, NV - 1, NV, -1), R(1, NV - 1, NV, -1), -BIG, ALU.add, ALU.max))
            dve.memset(R(0, 0, 1), -BIG)
            done(dve.memset(view(H, NV - 1, [[VW, 2], [1, VW - NV + 1]], 4), -BIG))
            dve.tensor_tensor(R(0, 1, NV - 1), A(4, 0, NV - 1), A(0, 1, NV - 1), ALU.add)
            dve.tensor_tensor(R(1, 0, NV - 1), A(5, 1, NV - 1), A(0, 1, NV - 1), ALU.add).then_inc(s("carries_ready"), 1)
            dve.wait_ge(s("carries_turned"), 1)
            done(dve.tensor_tensor(flat(SCR, PRE_AT), flat(SCR, PRE_AT), flat(SCR, SUF_AT), ALU.max))
            dve.tensor_copy(view(HT, END_AT, [[1, 32]]), PS[:, 4, 0:32]).then_inc(s("carries_placed"), 1)
            dve.wait_ge(s("carries_placed"), 1)
            for side in range(2):
                for g in range(VG):
                    for h in range(HEADS):
                        maxima = view(SCR, PRE_AT + (g * HEADS + h) * P, [[1, P]])
                        ins = dve.scalar_tensor_tensor(maxima, view(SCR, MASK_AT + (side * VG + g) * P, [[1, P]]),
                                                       view(HT, END_AT + side * 16 + g * 4 + h, [[1, 1]]), maxima, ALU.add, ALU.max)
                done(ins)
            dve.memset(small[:, 6, :], 0.0).then_inc(s("maxima_ready"), 1)
            dve.wait_ge(s("maxima_turned"), 1)
            for g in range(VG):
                w = WG[g]
                ms = view(HT, MS_AT + g * P * HEADS, [[1, HEADS], [HEADS, w]])
                ins = dve.tensor_tensor(ms, ms, view(PS, g * 512, [[P, HEADS], [1, w]]), ALU.max)
            done(ins)
            done(dve.tensor_tensor(ES, ES, MS, ALU.subtract))
            dve.tensor_scalar(ES, ES, 0.0, None, ALU.min).then_inc(s("below_max"), 1)
            dve.tensor_tensor(PM[:, :, HEADS:8], MS, view(EI, 4 * VW, [[1, NV], [0, HEADS]]), ALU.mult).then_inc(s("maxima_placed"), 1)
            dve.memset(PS[:, 0:5, :], 0.0).then_inc(s("sums_zeroed"), 1)
            dve.wait_ge(s("probs_ready"), 1)

            def weigh(k, p, m):
                if late(k, DEPTH):
                    dve.wait_ge(s("sum_done"), k - DEPTH + 1)
                one_hot(OH[:, p], 3, k)
                dve.wait_ge(s(f"rows_back{p}"), 16 * (m + 1))
                gg = view(G, p * VB * D, [[D, VB], [C, HEADS], [1, C]])
                dve.tensor_tensor(gg, view(HT, p * VB * D, [[D, VB], [C, HEADS], [1, C]]), view(RX, 8 * VB * k, [[8, VB], [1, HEADS], [0, C]]), ALU.mult).then_inc(s("sum_hot"), 1)
            batches(dve, weigh)
            dve.wait_ge(s("sum_done"), NB)
            part_sums = view(PS, PART_SUM, [[SLOT, NBLK], [8, 3], [1, 8]])
            sums8 = view(SCR, REST_AT + DEPTH * VB * 8, [[8, NBLK], [1, 8]])
            done(dve.tensor_copy(sums8, part_sums[:, :, 0]))
            done(dve.tensor_tensor(sums8, sums8, part_sums[:, :, 1], ALU.add))
            done(dve.tensor_tensor(sums8, sums8, part_sums[:, :, 2], ALU.add))
            done(dve.tensor_tensor(node_max[:], self_score[:], view(no_edges, 0, [[1, NBLK], [0, HEADS]]), ALU.mult))
            done(dve.tensor_tensor(node_max[:], node_max[:], sums8[:, :, 4:8], ALU.add))
            dve.tensor_tensor(self_prob[:], self_score[:], node_max[:], ALU.subtract).then_inc(s("self_below_max"), 1)
            dve.wait_ge(s("self_prob_ready"), 1)
            done(dve.tensor_tensor(node_max[:], self_prob[:], sums8[:, :, 0:4], ALU.add))
            done(dve.tensor_scalar(node_max[:], node_max[:], 1e-16, None, ALU.add))
            done(dve.reciprocal(node_max[:], node_max[:]))
            for b0, b1 in HALVES:
                n = b1 - b0
                heads = lambda t: t[:, b0:b1, :].rearrange("p b (h c) -> p b h c", h=HEADS)
                factor = lambda t: view(t, b0 * HEADS, [[HEADS, n], [1, HEADS], [0, C]])
                h_half, x_half = H[:, b0:b1, :], X[:, b0:b1, :]
                done(dve.tensor_tensor(heads(H), heads(XL), factor(self_prob), ALU.mult))
                done(dve.tensor_tensor(h_half, h_half, view(PS, b0 * D, [[D, n], [1, D]]), ALU.add))
                done(dve.tensor_tensor(heads(H), heads(H), factor(node_max), ALU.mult))
                done(dve.tensor_tensor(h_half, h_half, view(rows_s, 2 * D, [[0, n], [1, D]]), ALU.add))
                done(dve.scalar_tensor_tensor(x_half, h_half, 0.0, x_half, ALU.max, ALU.add))
                dve.tensor_scalar(h_half, h_half, 0.0, None, ALU.min).then_inc(s("elu_arg"), 1)
            for half, (b0, b1) in enumerate(HALVES):
                dve.wait_ge(s("elu_exp"), half + 1)
                ins = dve.scalar_tensor_tensor(X[:, b0:b1, :], H[:, b0:b1, :], -1.0, X[:, b0:b1, :], ALU.add, ALU.add)
            done(ins)

            norm(3)
            turned_h(2)
            for g in range(7):
                w = min(4, NBLK - 4 * g) * P
                dve.wait_ge(s("up_made"), g + 1)
                dve.tensor_scalar(view(RX, XL_AT + g * 512, [[1, w]]), PS[:, g, 0:w], 32.0 ** -0.5, None, ALU.mult).then_inc(s("up_copied"), 1)
                if (4 * g + w // P) // CB > 4 * g // CB:
                    dve.wait_ge(s("up_copied"), g + 1)
                    dve.memset(small[:, 6, :], 0.0).then_inc(s("table_ready"), 1)

            def by_species(g):
                w = min(2, NBLK - 2 * g) * P
                for kind in range(SPECIES):
                    ins = dve.scalar_tensor_tensor(view(AT, HM_AT + (g % 2 * SPECIES + kind) * 2 * P, [[1, w]]),
                                                   view(AT, SPECIES_AT + g * 2 * P, [[1, w]]), float(kind),
                                                   view(HT, g * 2 * P, [[1, w]]), ALU.is_equal, ALU.mult)
                ins.then_inc(s("by_species"), 1)

            dve.wait_ge(s("species_ready"), 1)
            by_species(0)
            by_species(1)
            dve.wait_ge(s("table_written"), written(LAYERS + 2))
            done(dve.memset(view(RX, 0, [[1, NBLK * MSG]]), 0.0))

            def where_to_add(k):
                word = dve.value_load(block_words[0:1, bass.ds(k, 1)])
                at = [dve.snap(((word >> (5 * q)) & 31) * MSG, min_val=0, max_val=(NBLK - 1) * MSG) for q in range(VB)]
                return at, [dve.snap(VB * k + q) if late(k, 1) or q else None for q in range(VB)]

            def add_up(k, q, at, adds):
                if not late(k, 1):
                    return
                acc = view(RX, at[q], [[1, MSG]])
                dve.wait_ge(s("message_sums"), adds[q] + 1 if adds[q] is not None else 1)
                if adds[q] is not None:
                    dve.wait_ge(s("added"), adds[q])
                dve.tensor_tensor(acc, acc, PS[:, q, 0:MSG], ALU.add).then_inc(s("added"), 1)

            ahead = []

            def message(k, p, m):
                g0 = p * VB * D
                m0 = M_AT + p * VB * MSG
                w0 = W_AT + p * VB * P
                y = lambda dims: view(AT, (SH + 1) * (NV + 1) + VB * k, dims)
                at, adds = (ahead.pop() if ahead else where_to_add(k - 1)) if late(k, 1) else (None, None)
                if late(k, DEPTH):
                    dve.wait_ge(s("message_sums"), VB * (k - DEPTH + 1))
                dve.wait_ge(s(f"conv_gathered{p}"), 16 * VB * (m + 1))
                dve.wait_ge(s("conv_weights"), k + 1)
                dve.tensor_tensor(view(SCR, T_AT, [[96, VB], [C, 3], [1, C]]), view(G, g0 + C, [[D, VB], [C, 3], [1, C]]),
                                  y([[1, VB], [NV + 1, 3], [0, C]]), ALU.mult)
                dve.tensor_tensor(view(SCR, C_AT, [[C, VB], [1, C]]), view(G, g0, [[D, VB], [1, C]]), view(SCR, w0 + 64, [[P, VB], [1, C]]), ALU.mult).then_inc(s("conv_parts"), 1)
                dve.tensor_tensor(view(SCR, m0, [[MSG, VB], [1, C]]), view(G, g0, [[D, VB], [1, C]]), view(SCR, w0, [[P, VB], [1, C]]), ALU.mult)
                add_up(k, 0, at, adds)
                dve.wait_ge(s("conv_parts"), k + 1)
                dve.tensor_tensor(view(SCR, m0 + 96, [[MSG, VB], [64, 3], [1, C]]), view(SCR, C_AT, [[C, VB], [0, 3], [1, C]]),
                                  y([[1, VB], [NV + 1, 3], [0, C]]), ALU.mult)
                add_up(k, 1, at, adds)
                dve.tensor_reduce(view(SCR, U_AT, [[C, VB], [1, C]]), view(SCR, T_AT, [[96, VB], [1, C], [C, 3]]), AX, ALU.add).then_inc(s("conv_dot"), 1)
                add_up(k, 2, at, adds)
                dve.tensor_tensor(view(SCR, m0 + 64, [[MSG, VB], [64, 3], [1, C]]), view(G, g0 + C, [[D, VB], [C, 3], [1, C]]),
                                  view(SCR, w0 + C, [[P, VB], [0, 3], [1, C]]), ALU.mult)
                add_up(k, 3, at, adds)
                dve.wait_ge(s("conv_dot"), k + 1)
                dve.scalar_tensor_tensor(view(SCR, m0 + C, [[MSG, VB], [1, C]]), view(SCR, U_AT, [[C, VB], [1, C]]), INV_SQRT3,
                                         view(SCR, w0 + 96, [[P, VB], [1, C]]), ALU.mult, ALU.mult).then_inc(s("messages_ready"), 1)
                if (p + 1) % DEPTH != (PEEL - DEPTH) % DEPTH:
                    ahead.append(where_to_add(k))
                add_up(k, 4, at, adds)

            batches(dve, message)
            for q, at_adds in enumerate([where_to_add(NB - 1)] * VB):
                add_up(NB, q, *at_adds)
            dve.wait_ge(s("added"), NV)
            dve.memset(small[:, 7, :], 0.0).then_inc(s("messages_summed"), 1)

            for b in range(NBLK):
                dve.wait_ge(s("update_made"), b + 1)
                dve.tensor_scalar(view(SCR, b * OUTW, [[1, OUTW]]), PS[:, 4 + b % 4, 0:OUTW], 0.5 * 32.0 ** -0.5, None, ALU.mult).then_inc(s("update_copied"), 1)
                if b % 2 and b // 2 + 2 < 13:
                    by_species(b // 2 + 2)
                if b + 1 in (HALVES[0][1], NBLK):
                    dve.wait_ge(s("update_copied"), b + 1)
                    dve.memset(small[:, 7, :], 0.0).then_inc(s("update_ready"), 1)
                if b in (HALVES[0][1] + 2, NBLK - 1):
                    half = int(b == NBLK - 1)
                    b0, b1 = HALVES[half]
                    at = lambda c, dims: view(SCR, b0 * OUTW + c, [[OUTW, b1 - b0]] + dims)
                    dve.wait_ge(s("gates_ready"), half + 1)
                    for i3 in range(3):
                        ins = dve.tensor_tensor(at(64 + 32 * i3, [[1, 32]]), at(64 + 32 * i3, [[1, 32]]), at(32, [[1, 32]]), ALU.mult)
                    done(ins)
                    dve.tensor_tensor(X[:, b0:b1, 0:32], X[:, b0:b1, 0:32], at(0, [[1, 32]]), ALU.add)
                    xv = view(X, b0 * D + 32, [[D, b1 - b0], [3, 32], [1, 3]])
                    dve.tensor_tensor(xv, xv, at(64, [[1, 32], [32, 3]]), ALU.add).then_inc(s("result_ready"), 1)

        @block.tensor
        def _(pe):
            def turn_h(n):
                for b in range(NBLK):
                    if b % 4 == 0:
                        if b < 4 * ACT_GROUPS:
                            pe.wait_ge(s("normed_act"), ACT_GROUPS * (n + 1) + b // 4 + 1)
                        elif b == 4 * ACT_GROUPS:
                            pe.wait_ge(s("normed_dve"), n + 2)
                    ins = pe.transpose(PS[:, b // 4, (b % 4) * P:(b % 4 + 1) * P], H[:, b, :], ident[:])
                    if b % 4 == 3 or b == NBLK - 1:
                        ins.then_inc(s("h_turned"), 1)

            pe.wait_ge(s("ends_ready"), 1)
            pe.wait_ge(s("ones_made"), 2)
            pe.matmul(PS[:, 0, 0:NT], ones_row[:], rowf[:, 0:NT], start=True, stop=True).then_inc(s("ends_spread"), 1)
            pe.wait_ge(s("blocks_ready"), 1)
            pe.wait_ge(s("ident_made"), 1)
            pe.transpose(PS[0:4, 1, 0:P], tv[:, 4, :], ident[:]).then_inc(s("blocks_in_psum"), 1)
            pe.wait_ge(s("blocks_turned"), 1)
            for f in range(N_FILL):
                g, j = FILLS[f]
                if j == 0:
                    pe.wait_ge(s("kinds_ready"), g + 1)
                if j == 2:
                    pe.wait_ge(s(f"attrs_in{g}"), 16)
                if f >= 6:
                    pe.wait_ge(*copies(f - 6))
                n = 4 if j != 1 else 1
                for i in range(n):
                    if j < 2:
                        src = view(RX, (5 * g + 4 * j + i) * P, [[1, P]])
                    else:
                        src = view(SCR, (g % 2) * N_ATTR * P + (4 * (j - 2) + i) * P, [[1, P]])
                    ins = pe.transpose(PS[:, 2 + f % 6, i * P:(i + 1) * P], src, ident[:])
                ins.then_inc(s("fill_turned"), 1)

            for i in range(LAYERS):
                name = passes[i]
                r0 = 12 - CH * i
                pe.wait_ge(s("sums_zeroed"), i + 1)

                def scatter(k, p, m):
                    word = pe.value_load(block_words[0:1, bass.ds(k, 1)])
                    pe.wait_ge(s(f"{name}_hot_bf16"), k + 1)
                    pe.wait_ge(s(f"{name}_gathered{p}"), 16 * VB * (m + 1))
                    blocks = [(word >> (5 * q)) & 31 for q in range(VB)]
                    for q, b in enumerate(blocks):
                        pe.matmul(PSF[:, bass.ds(b * P, P)], OH[:, p, q, :], G[:, p, q, :], start=False, stop=False, skip_group_check=True)
                        pe.matmul(PSF[:, SRC_SUM:SRC_SUM + CH * NBLK], view(SCR, p * VB * P + q * P, [[1, P]]),
                                  view(SCR, PR_AT + p * VB * NBLK * 7 + VB * NBLK + q * NBLK * CH, [[1, NBLK * CH]]),
                                  start=False, stop=False, skip_group_check=True)
                    for q, b in enumerate(blocks):
                        ins = pe.matmul(PSF[:, bass.ds(b * SLOT + PART_SUM, 3 * CH)], OHA(p)[:, q], attr_parts(p)[:, q],
                                        start=False, stop=False, skip_group_check=True)
                    ins.then_inc(s(f"{name}_rows_used"), 1)
                batches(pe, scatter)

            pe.wait_ge(s("means_ready"), 1)
            for g in range(7):
                w = min(4, NBLK - 4 * g)
                if g >= 2:
                    pe.wait_ge(s("mt_ready"), g - 1)
                for b in range(w):
                    ins = pe.transpose(PS[0:32, g % 2, b * P:(b + 1) * P], means[:, 4 * g + b, :], ident[:])
                ins.then_inc(s("means_turned"), 1)
            pe.wait_ge(s("mt_ready"), 7)
            turn_h(0)
            pe.wait_ge(s("weights_loaded"), W_ALL)
            for g in range(7):
                w = min(4, NBLK - 4 * g) * P
                pe.wait_ge(s("ht_ready"), max(g, 2 + g % 2) + 1)
                if g >= 2:
                    pe.wait_ge(s("hidden_biased"), g - 1)
                pe.matmul(PS[:, 2 + g % 2, 0:w], w1a_s[:], HTF[:, g * 512:g * 512 + w], start=True, stop=False)
                pe.matmul(PS[:, 2 + g % 2, 0:w], w1b_s[:], view(SCR, g * 512, [[1, w]], 32), start=False, stop=True).then_inc(s("hidden_made"), 1)
            for g in range(7):
                w = min(4, NBLK - 4 * g)
                pe.wait_ge(s("hidden_ready"), g + 1)
                if g >= 2:
                    pe.wait_ge(s("mlp_added"), g - 1)
                for b in range(w):
                    ins = pe.matmul(PS[:, 4 + g % 2, b * P:(b + 1) * P], hid[:, (4 * g + b) * P:(4 * g + b + 1) * P], w2_s[:], start=True, stop=True)
                ins.then_inc(s("mlp_made"), 1)

            turn_h(1)
            for g in range(7):
                pe.wait_ge(s("ht_ready"), 7 + max(g, 2 * g + 1 if g < 3 else 0) + 1)
                if g >= 3:
                    pe.wait_ge(s("xl_copied"), g - 2)
                    pe.wait_ge(s("xr_copied"), g - 2)
                for side in range(2):
                    for b in range(min(4, NBLK - 4 * g)):
                        ins = pe.matmul(PS[:, 2 * (g % 3) + side, b * P:(b + 1) * P], HTF[:, (4 * g + b) * P:(4 * g + b + 1) * P],
                                        wlr_s[:, side * P:(side + 1) * P], start=True, stop=True)
                    ins.then_inc(s("xr_made" if side else "xl_made"), 1)
            pe.wait_ge(s("xr_ready"), 1)

            def score(k, p, m):
                pe.wait_ge(s("score_hot"), k + 1)
                if late(k, DEPTH):
                    pe.wait_ge(s("ot_ready"), k - DEPTH + 1)
                for q in range(VB):
                    ins = pe.transpose(ot_ps(p)[:, q * P:(q + 1) * P], OHB(p)[:, q, :], ident_b[:])
                ins.then_inc(s("oh_turned"), 1)
                pe.wait_ge(s("radial_ready"), k + 1)
                if late(k, 1):
                    pe.wait_ge(s("radial_hidden_ready"), k)
                gate(pe)
                pe.transpose(PS[0:8 * VB, 7, 0:P], view(SCR, RS_AT, [[1, 8 * VB]]), ident[:]).then_inc(s("radial_turned"), 1)
                if late(k, 1):
                    add_r(k - 1, *before(p, m))
                pe.wait_ge(s("radial_t_ready"), k + 1)
                gate(pe)
                pe.matmul(PS[0:8 * VB, 7, 256:256 + P], wr1_s[:], view(SCR, RT_AT, [[1, P]], 8 * VB), start=True, stop=True).then_inc(s("hidden_pre_made"), 1)

            def add_r(k, p, m):
                word = pe.value_load(block_words[0:1, bass.ds(k, 1)])
                pe.wait_ge(s("ot_ready"), k + 1)
                if late(k, 1):
                    pe.wait_ge(s("z_read"), k)
                for q in range(VB):
                    b = (word >> (5 * q)) & 31
                    zq = 4 * 512 + 256 * q
                    ins = pe.matmul(view(PS, zq, [[1, XR_W]]), view(SCR, OT_AT + (p * VB + q) * P, [[1, P]]),
                                    view(RX, b * XR_W, [[1, XR_W]]), start=True, stop=True)
                ins.then_inc(s("z_made"), 1)
            batches(pe, score)
            add_r(NB - 1, *LAST)

            pe.wait_ge(s("scored"), NB)
            for g in range(VG):
                for h in range(HEADS):
                    ins = pe.transpose(view(PS, g * 512 + h * P, [[1, P]], WG[g]), view(HT, g * P * HEADS + h, [[HEADS, WG[g]]]), ident[:])
            ins.then_inc(s("scores_turned"), 1)
            pe.wait_ge(s("ends_made"), 1)
            for i in range(4):
                for g in range(VG):
                    ins = pe.transpose(PS[0:4, i, g * P:(g + 1) * P], view(HT, END_AT + (i * VG + g) * 4, [[1, 4]]), ident[:])
            ins.then_inc(s("ends_turned"), 1)
            pe.wait_ge(s("carries_ready"), 1)
            for i in range(2):
                for g in range(VG):
                    ins = pe.transpose(PS[:, 4, i * 16 + g * 4:i * 16 + g * 4 + 4], view(H, i * VW + g * P, [[1, P]], 4), ident[0:4, 0:4])
            ins.then_inc(s("carries_turned"), 1)
            pe.wait_ge(s("maxima_ready"), 1)
            for g in range(VG):
                for h in range(HEADS):
                    ins = pe.transpose(view(PS, g * 512 + h * P, [[1, WG[g]]]), view(SCR, PRE_AT + (g * HEADS + h) * P, [[1, P]], WG[g]), ident[0:WG[g], 0:WG[g]])
            ins.then_inc(s("maxima_turned"), 1)

            pe.wait_ge(s("sums_zeroed"), LAYERS + 1)
            pe.wait_ge(s("probs_ready"), 1)

            def weighted(k, p, m):
                word = pe.value_load(block_words[0:1, bass.ds(k, 1)])
                pe.wait_ge(s("sum_hot_bf16"), k + 1)
                blocks = [(word >> (5 * q)) & 31 for q in range(VB)]
                for q, b in enumerate(blocks):
                    pe.matmul(PSF[:, bass.ds(b * P, P)], OH[:, p, q, :], G[:, p, q, :], start=False, stop=False, skip_group_check=True)
                for q, b in enumerate(blocks):
                    ins = pe.matmul(PSF[:, bass.ds(b * SLOT + PART_SUM, PARTS)], OHW(p)[:, q], parts(p)[:, q],
                                    start=False, stop=False, skip_group_check=True)
                ins.then_inc(s("sum_done"), 1)
            batches(pe, weighted)

            turn_h(2)
            for b in range(NBLK):
                if b % 4 == 0:
                    pe.wait_ge(s("ht_ready"), 14 + b // 4 + 1)
                ins = pe.matmul(PS[:, b // 4, (b % 4) * P:(b % 4 + 1) * P], HTF[:, b * P:(b + 1) * P], wup_s[:], start=True, stop=True)
                if b % 4 == 3 or b == NBLK - 1:
                    ins.then_inc(s("up_made"), 1)
            pe.wait_ge(s("up_copied"), 7)

            def conv(k, p, m):
                pe.wait_ge(s(f"hidden_back{p}"), 16 * (m + 1))
                if late(k, 1):
                    pe.wait_ge(s("conv_weights"), k)
                for q in range(VB):
                    ins = pe.matmul(view(PS, 5 * 512 + q * P, [[1, P]]), view(SCR, CH_AT + p * P, [[1, P]], 8 * VB), wr2_s[:, q, :], start=True, stop=True)
                ins.then_inc(s("conv_weights_made"), 1)
                if late(k, 2):
                    sums(k - 2, before(*before(p, m))[0])

            def sums(k, p):
                pe.wait_ge(s("messages_ready"), k + 1)
                pe.wait_ge(s("conv_hot"), k + 1)
                for q in range(VB):
                    if late(k, 1):
                        pe.wait_ge(s("added"), VB * (k - 1) + q + 1)
                    ins = pe.matmul(PS[:, q, 0:MSG], OH[:, p, q, :], view(SCR, M_AT + (p * VB + q) * MSG, [[1, MSG]]), start=True, stop=True)
                    ins.then_inc(s("message_sums"), 1)
            batches(pe, conv)
            sums(NB - 2, before(*LAST)[0])
            sums(NB - 1, LAST[0])

            def update(b):
                if b >= 4:
                    pe.wait_ge(s("update_copied"), b - 3)
                pe.wait_ge(s("by_species"), b // 2 + 1)
                ps = PS[:, 4 + b % 4, :]
                for kind in range(SPECIES):
                    pe.matmul(ps[:, 0:OUTW], view(AT, HM_AT + (b // 2 % 2 * SPECIES + kind) * 2 * P + b % 2 * P, [[1, P]]),
                              view(AT, SKIP_AT + kind * OUTW, [[1, OUTW]]), start=kind == 0, stop=False, skip_group_check=True)
                pe.wait_ge(s("final_copied"), b + 1)
                sums_t = lambda j: view(SCR, AC_AT + (b % 4) * 256 + j * P, [[1, P]])
                pe.matmul(ps[:, 0:96], sums_t(0), wdna_s[:], start=False, stop=False, skip_group_check=True)
                ins = pe.matmul(ps[:, 96:160], sums_t(1), wdnb_s[:], start=False, stop=True, skip_group_check=True)
                ins.then_inc(s("update_made"), 1)

            pe.wait_ge(s("messages_summed"), 1)
            for b in range(NBLK):
                if b >= 4:
                    pe.wait_ge(s("final_copied"), b - 3)
                for j in range(2):
                    ins = pe.transpose(PS[:, b % 4, j * P:(j + 1) * P], view(RX, b * MSG + j * P, [[1, P]]), ident[:])
                ins.then_inc(s("acc_turned"), 1)
                if b >= 1:
                    update(b - 1)
            update(NBLK - 1)


def kernel(x, src, dst, edge_attr_16, edge_attr_4, edge_attr_8, node_type_4, L1_gnn_W1, L1_gnn_b1, L1_gnn_W2, L1_gnn_b2,
           L2_gnn_W_l, L2_gnn_b_l, L2_gnn_W_r, L2_gnn_b_r, L2_gnn_att, L2_gnn_bias, L3_gnn_W_up_s, L3_gnn_W_up_v,
           L3_gnn_W_r1, L3_gnn_W_r2, L3_gnn_W_dn_s, L3_gnn_W_dn_v, L3_gnn_W_sk_s, L3_gnn_W_sk_v):
    import numpy as np
    import concourse.bacc as bacc
    from concourse.bass_utils import run_bass_kernel_spmd

    a = lambda t: np.ascontiguousarray(np.asarray(t))
    f32, i32 = np.float32, np.int32
    ids = np.full((3, NT * P), NPAD - 1, i32)
    ids[0, :EDGES], ids[1, :EDGES] = a(src), a(dst)
    ids[2, 1:], ids[2, 0] = ids[1, :-1], -1
    attrs = np.zeros((NT * P, N_ATTR), f32)
    attrs[:EDGES] = np.concatenate([a(edge_attr_16), a(edge_attr_4), a(edge_attr_8)], 1)
    types = np.zeros((NPAD,), i32)
    types[:NODES] = a(node_type_4)

    up = np.zeros((D, D), f32)
    up[0:32, 0:32] = a(L3_gnn_W_up_s)
    for i in range(3):
        up[32 + i::3, 32 + 32 * i:64 + 32 * i] = a(L3_gnn_W_up_v)
    skip = np.zeros((D, SPECIES, OUTW), f32)
    skip[0:32, :, 0:64] = a(L3_gnn_W_sk_s).transpose(1, 0, 2)
    for i in range(3):
        skip[32 + i::3, :, 64 + 32 * i:96 + 32 * i] = a(L3_gnn_W_sk_v).transpose(1, 0, 2)
    wr1 = np.zeros((8, VB, VB, 8), f32)
    wr2 = np.zeros((VB, 8, VB, P), f32)
    for q in range(VB):
        wr1[:, q, q, :] = a(L3_gnn_W_r1)
        wr2[q, :, q, :] = a(L3_gnn_W_r2)
    dn_a, dn_b = np.zeros((P, 96), f32), np.zeros((P, 64), f32)
    dn_a[0:64, 0:64] = a(L3_gnn_W_dn_s)
    dn_a[64:128, 64:96] = dn_b[0:64, 0:32] = dn_b[64:128, 32:64] = a(L3_gnn_W_dn_v)
    arrays = {
        "x": a(x),
        "edge_ids": a(ids.reshape(3, NT, P).transpose(1, 0, 2).reshape(NT, 3 * P)),
        "last_dst": a(ids[1, P - 1::P].reshape(1, NT)),
        "edge_attrs": a(attrs.reshape(NT, P, N_ATTR).transpose(0, 2, 1).reshape(NT, N_ATTR * P)),
        "species": types,
        "w1a": a(L1_gnn_W1)[0:D], "w1b": a(a(L1_gnn_W1)[D:D + 32]), "b1": a(L1_gnn_b1).reshape(D, 1), "w2": a(L1_gnn_W2),
        "row_params": np.concatenate([a(L1_gnn_b2), a(L2_gnn_att).reshape(-1), a(L2_gnn_bias), a(L2_gnn_b_l), a(L2_gnn_b_r)]),
        "wlr": a(np.concatenate([a(L2_gnn_W_l).T, a(L2_gnn_W_r).T], 1)),
        "wup": up, "wr1": wr1.reshape(8 * VB, 8 * VB), "wr2": wr2.reshape(8 * VB, VB, P), "wdn_a": dn_a, "wdn_b": dn_b,
        "wsk": skip.reshape(D, SPECIES * OUTW),
    }
    nc = bacc.Bacc("TRN2", target_bir_lowering=False, num_devices=1)
    handles = [nc.dram_tensor(f"in_{n}", v.shape, mybir.dt.from_np(v.dtype), kind="ExternalInput").ap() for n, v in arrays.items()]
    handles.append(nc.dram_tensor("out", (NODES, D), F32, kind="ExternalOutput").ap())
    gnn_program(nc, *handles)
    r = run_bass_kernel_spmd(nc, [{f"in_{n}": v for n, v in arrays.items()}], core_ids=[0])
    return r.results[0]["out"]
```
